# Optimizing a Trainium2 kernel written in Bass

```python
import numpy as np
import jax
import jax.numpy as jnp

def _softmax(x, axis=-1):
    return jax.nn.softmax(x, axis=axis)

def _gelu(x):
    return jax.nn.gelu(x, approximate=True)

def _silu(x):
    return jax.nn.silu(x)

def _sigmoid(x):
    return jax.nn.sigmoid(x)

def _layernorm(x, axis=-1, eps=1e-05):
    m = jnp.mean(x, axis=axis, keepdims=True)
    v = jnp.var(x, axis=axis, keepdims=True)
    return (x - m) / jnp.sqrt(v + eps)

def _scatter_add(tgt, idx, src, axis=0):
    return tgt.at[idx].add(src)

def _segment_sum(src, seg, n):
    return jax.ops.segment_sum(src, seg, n)
kernel_name = 'mk_gnn_preln_d2_gnn_r8_5d20ee'

def setup_inputs(seed: int=0):
    np.random.seed(seed)
    _w = jnp.asarray

    def _rec_inputs():
        import jax
        import jax.numpy as jnp
        _gk = jax.random.key(seed)
        x = -0.0007083 + 1.001 * jax.random.normal(jax.random.fold_in(_gk, 1), (6250, 48), jnp.float32)
        src = jax.random.randint(jax.random.fold_in(_gk, 2), (200000,), 0, 6250, jnp.int32)
        dst = jax.random.randint(jax.random.fold_in(_gk, 3), (200000,), 0, 6250, jnp.int32)
        _o = jnp.argsort(dst, stable=True)
        src = src[_o]
        dst = dst[_o]
        edge_attr_40 = jax.random.uniform(jax.random.fold_in(_gk, 12), (200000, 40), jnp.float32, 0.0, 1)
        edge_weight = jax.random.uniform(jax.random.fold_in(_gk, 14), (200000,), jnp.float32, 0.0, 7.99999)
        node_type_119 = jax.random.randint(jax.random.fold_in(_gk, 15), (6250,), 0, 119, jnp.int32)
        node_vec = jax.random.uniform(jax.random.fold_in(_gk, 16), (6250,), jnp.float32, 0.0, 3.99996)
        return (x, src, dst, edge_attr_40, edge_weight, node_type_119, node_vec)
    x, src, dst, edge_attr_40, edge_weight, node_type_119, node_vec = _rec_inputs()

    def _L0_gnn_setup():
        import jax, jax.numpy as jnp
        import numpy as np
        N = 6250
        E = 150000
        H = 48
        RBF = 40
        L = 4
        NELEM = 119
        G = 32
        CUT = 6.0

        def _ln(x, g, b):
            m = x.mean(-1, keepdims=True)
            v = ((x - m) ** 2).mean(-1, keepdims=True)
            return (x - m) * jax.lax.rsqrt(v + 1e-05) * g + b
        key = jax.random.key(seed)
        k = jax.random.split(key, 16)
        s = 0.1
        return {'h': jax.random.normal(k[0], (N, H), jnp.float32), 'edge_index': jax.random.randint(k[1], (2, E), 0, N), 'edge_attr': jax.random.uniform(k[2], (E, RBF), dtype=jnp.float32), 'distances': jax.random.uniform(k[3], (E,), dtype=jnp.float32) * 8.0, 'atom_z': jax.random.randint(k[4], (N,), 0, NELEM), 'node_mult': jax.random.uniform(k[5], (N,), dtype=jnp.float32) * 3.0 + 1.0, 'batch': jnp.sort(jax.random.randint(k[6], (N,), 0, 64)), 'Wq': jax.random.normal(k[7], (L, H, H), jnp.float32) * s, 'gq': jnp.ones((L, H), jnp.float32), 'bq': jnp.zeros((L, H), jnp.float32), 'Wk': jax.random.normal(k[8], (L, H, H), jnp.float32) * s, 'gk': jnp.ones((L, H), jnp.float32), 'bk': jnp.zeros((L, H), jnp.float32), 'Wm': jax.random.normal(k[9], (L, H, H), jnp.float32) * s, 'Wu': jax.random.normal(k[10], (L, 2 * H, H), jnp.float32) * s, 'go': jnp.ones((L, H), jnp.float32), 'bo': jnp.zeros((L, H), jnp.float32), 'F1W': jax.random.normal(k[11], (RBF, H), jnp.float32) * s, 'F1b': jnp.zeros((H,), jnp.float32), 'F2W': jax.random.normal(k[12], (H, H), jnp.float32) * s, 'F2b': jnp.zeros((H,), jnp.float32), 'gn': jnp.ones((H,), jnp.float32), 'bn': jnp.zeros((H,), jnp.float32), 'emb': jax.random.normal(k[13], (NELEM, G), jnp.float32) * 0.01, 'adapt': jax.random.normal(k[14], (G, G), jnp.float32) * 0.01}
    _L0_gnn_all = _L0_gnn_setup()
    _L0_gnn_in = {k: v for k, v in _L0_gnn_all.items() if k in ('Wq', 'gq', 'bq', 'Wk', 'gk', 'bk', 'Wm', 'Wu', 'go', 'bo', 'F1W', 'F1b', 'F2W', 'F2b', 'gn', 'bn', 'emb', 'adapt')}
    del _L0_gnn_all

    def _L1_gnn_setup():
        import jax, jax.numpy as jnp
        import numpy as np
        N = 12500
        E = 200000
        D = 48
        K = 5
        ALPHA = 0.8
        key = jax.random.key(seed)
        k1, k2 = jax.random.split(key)
        x = jax.random.normal(k1, (N, D), dtype=jnp.float32)
        edge_index = jax.random.randint(k2, (2, E), 0, N, dtype=jnp.int32)
        return {'x': x, 'edge_index': edge_index}
    _L1_gnn_all = _L1_gnn_setup()
    _L1_gnn_in = {k: v for k, v in _L1_gnn_all.items() if k in ()}
    del _L1_gnn_all
    return {'x': x, 'src': src, 'dst': dst, 'edge_attr_40': edge_attr_40, 'edge_weight': edge_weight, 'node_type_119': node_type_119, 'node_vec': node_vec, 'L0_gnn_Wq': _L0_gnn_in['Wq'], 'L0_gnn_gq': _L0_gnn_in['gq'], 'L0_gnn_bq': _L0_gnn_in['bq'], 'L0_gnn_Wk': _L0_gnn_in['Wk'], 'L0_gnn_gk': _L0_gnn_in['gk'], 'L0_gnn_bk': _L0_gnn_in['bk'], 'L0_gnn_Wm': _L0_gnn_in['Wm'], 'L0_gnn_Wu': _L0_gnn_in['Wu'], 'L0_gnn_go': _L0_gnn_in['go'], 'L0_gnn_bo': _L0_gnn_in['bo'], 'L0_gnn_F1W': _L0_gnn_in['F1W'], 'L0_gnn_F1b': _L0_gnn_in['F1b'], 'L0_gnn_F2W': _L0_gnn_in['F2W'], 'L0_gnn_F2b': _L0_gnn_in['F2b'], 'L0_gnn_gn': _L0_gnn_in['gn'], 'L0_gnn_bn': _L0_gnn_in['bn'], 'L0_gnn_emb': _L0_gnn_in['emb'], 'L0_gnn_adapt': _L0_gnn_in['adapt']}

def reference(x, src, dst, edge_attr_40, edge_weight, node_type_119, node_vec, L0_gnn_Wq, L0_gnn_gq, L0_gnn_bq, L0_gnn_Wk, L0_gnn_gk, L0_gnn_bk, L0_gnn_Wm, L0_gnn_Wu, L0_gnn_go, L0_gnn_bo, L0_gnn_F1W, L0_gnn_F1b, L0_gnn_F2W, L0_gnn_F2b, L0_gnn_gn, L0_gnn_bn, L0_gnn_emb, L0_gnn_adapt):
    import jax
    import jax.numpy as jnp

    def _L0_gnn_ref(h, edge_index, edge_attr, distances, atom_z, node_mult, batch, Wq, gq, bq, Wk, gk, bk, Wm, Wu, go, bo, F1W, F1b, F2W, F2b, gn, bn, emb, adapt):
        import jax, jax.numpy as jnp
        import numpy as np
        N = 6250
        E = 150000
        H = 48
        RBF = 40
        L = 4
        NELEM = 119
        G = 32
        CUT = 6.0

        def _ln(x, g, b):
            m = x.mean(-1, keepdims=True)
            v = ((x - m) ** 2).mean(-1, keepdims=True)
            return (x - m) * jax.lax.rsqrt(v + 1e-05) * g + b
        src, dst = (edge_index[0], edge_index[1])
        gate = jax.nn.silu(edge_attr @ F1W + F1b) @ F2W + F2b
        ei = emb[atom_z[src]]
        ej = emb[atom_z[dst]]
        gate = gate + (ei * (ej @ adapt)).sum(-1, keepdims=True)
        cw = jnp.where(distances < CUT, 0.5 * (jnp.cos(jnp.pi * distances / CUT) + 1.0), 0.0)
        mj = node_mult[dst]
        msg = gate * h[dst] * (cw * mj)[:, None]
        agg = jax.ops.segment_sum(msg, src, num_segments=N)
        tot = jnp.clip(jax.ops.segment_sum(mj, src, num_segments=N), 1e-08, None)
        h = _ln(h + agg / tot[:, None], gn, bn)
        logm = jnp.log(jnp.clip(node_mult, 1.0, None))
        for i in range(L):
            Q = _ln(h @ Wq[i], gq[i], bq[i])
            K = _ln(h @ Wk[i], gk[i], bk[i])
            qi = Q[src]
            kj = K[dst]
            score = (qi * kj).sum(-1) + 0.1 * (edge_attr * qi[:, :RBF]).sum(-1) + logm[dst]
            smax = jax.ops.segment_max(score, src, num_segments=N)
            es = jnp.exp(jnp.minimum(score - smax[src], 20.0))
            denom = jax.ops.segment_sum(es, src, num_segments=N)
            alpha = es / (denom[src] + 1e-10)
            m = h[dst] @ Wm[i]
            aggi = jax.ops.segment_sum(alpha[:, None] * m, src, num_segments=N)
            z = jnp.concatenate([h, aggi], axis=-1) @ Wu[i]
            z = jnp.where(z > 0, z, 0.01 * z)
            h = _ln(h + z, go[i], bo[i])
        return h

    def _L1_gnn_ref(x, edge_index):
        import jax, jax.numpy as jnp
        import numpy as np
        N = 12500
        E = 200000
        D = 48
        K = 5
        ALPHA = 0.8
        n = x.shape[0]
        loops = jnp.arange(n, dtype=edge_index.dtype)
        row = jnp.concatenate([edge_index[0], loops])
        col = jnp.concatenate([edge_index[1], loops])
        deg = jax.ops.segment_sum(jnp.ones(row.shape, x.dtype), col, num_segments=n)
        dinv = jnp.where(deg > 0, jax.lax.rsqrt(deg), jnp.zeros((), x.dtype))
        w = dinv[row] * dinv[col]

        def step(h, _):
            m = jax.ops.segment_sum(w[:, None] * h[row], col, num_segments=n)
            h = (1.0 - ALPHA) * m + ALPHA * x
            return (h, None)
        h, _ = jax.lax.scan(step, x, None, length=K)
        return h
    edge_index = jnp.stack([src, dst])
    batch0 = jnp.zeros((6250,), jnp.int32)
    h = jnp.maximum(_layernorm(x, axis=-1), 0.0)
    x = x + _L0_gnn_ref(h, edge_index, edge_attr_40, edge_weight, node_type_119, node_vec, batch0, L0_gnn_Wq, L0_gnn_gq, L0_gnn_bq, L0_gnn_Wk, L0_gnn_gk, L0_gnn_bk, L0_gnn_Wm, L0_gnn_Wu, L0_gnn_go, L0_gnn_bo, L0_gnn_F1W, L0_gnn_F1b, L0_gnn_F2W, L0_gnn_F2b, L0_gnn_gn, L0_gnn_bn, L0_gnn_emb, L0_gnn_adapt)
    h = jnp.maximum(_layernorm(x, axis=-1), 0.0)
    x = x + _L1_gnn_ref(h, edge_index)
    return x

_drawn_inputs = setup_inputs


def setup_inputs(seed=0):
    import zlib

    import numpy as np

    out = dict(_drawn_inputs(seed))
    spreads = {'L0_gnn_gq': (1.0, 0.2),
     'L0_gnn_bq': (0.0, 0.1),
     'L0_gnn_gk': (1.0, 0.2),
     'L0_gnn_bk': (0.0, 2.0),
     'L0_gnn_go': (1.0, 0.2),
     'L0_gnn_bo': (0.0, 0.1),
     'L0_gnn_F1b': (0.0, 0.716),
     'L0_gnn_F2b': (0.0, 0.1),
     'L0_gnn_gn': (1.0, 0.2),
     'L0_gnn_bn': (0.0, 0.1)}
    factors = {'L0_gnn_emb': 64.0, 'L0_gnn_adapt': 64.0}
    for name, (base, spread) in spreads.items():
        noise = np.random.default_rng([zlib.crc32(name.encode()), seed]).standard_normal(out[name].shape)
        drawn = base * np.exp(spread * noise) if base else spread * noise
        out[name] = jnp.asarray(drawn.astype(out[name].dtype))
    for name, factor in factors.items():
        out[name] = (out[name] * factor).astype(out[name].dtype)
    return out
```

```python
from contextlib import ExitStack

import concourse.bass as bass
from concourse import mybir

F32, BF16, FP8, I32 = mybir.dt.float32, mybir.dt.bfloat16, mybir.dt.float8e4, mybir.dt.int32
ALU, ACT, AX = mybir.AluOpType, mybir.ActivationFunctionType, mybir.AxisListType
ds = bass.ds

N, E, H, RBF, L, G, NELEM = 6250, 200000, 48, 40, 4, 32, 119
CUT, KSTEP, ALPHA = 6.0, 5, 0.8
P = 128
NB = -(-N // P)
TAIL = N - (NB - 1) * P
NPAD = NB * P
CAP = P
EP = 125
ET = E // EP
NS = 8
SC = ET // NS
JB = 10
CELLS = NB * NB
GRID = CELLS * P
NOV = E // P
F_SRC, F_DST, F_W, F_BS, F_BD, RW = 40, 41, 42, 43, 44, 45
GC = 7
NG = NB // GC
KW = H + 1
DW = 2 * H + 1
GW = H + 1 + G
BIG = 1e30
HALF_PI = 1.5707963267948966
ENGINES = ("sync", "tensor", "vector", "scalar", "gpsimd")


def build(nc, x, src, dst, edge_attr_40, edge_weight, node_type_119, node_vec, Wq, gq, bq, Wk, gk, bk, Wm, Wu, go,
          bo, F1W, F1b, F2W, F2b, gn, bn, emb, adapt, out, debug=None):
    REC = nc.dram_tensor("edge_records", (GRID + NOV * P, RW), F32)
    OHD = nc.dram_tensor("one_hots", (NB, NG, P, 3 * GC * P // 4), F32)
    ADJ = nc.dram_tensor("adjacency", (NB, P, NB * P), BF16)
    rec_rows = REC[0:GRID, :].rearrange("(b p c) w -> b p (c w)", p=P, c=NB)
    rec_extra = REC[GRID:GRID + NOV * P, :].rearrange("(j p) w -> j p w", p=P)
    adj_groups = ADJ[:, :, :].rearrange("b s e -> s b e")

    ctx = ExitStack()
    with ctx:
        def sem(name):
            return ctx.enter_context(nc.semaphore(name))

        order, turn, absorb = sem("order"), sem("turn"), sem("absorb")
        s_load, s_edges, s_pe, s_dve, s_rank, s_idx = (sem(n) for n in
            ("prep_load", "edge_loads", "prep_pe", "prep_dve", "rank_done", "slots_done"))
        s_asm = sem("records_assembled")
        s_scat = [sem(f"records_scattered_{k}") for k in range(10)]
        s_hpe, s_hdve = sem("hist_pe"), sem("hist_dve")
        s_aload = [sem(f"adj_loaded_{k}") for k in range(2)]
        s_apes, s_afold = sem("adj_multiplied"), sem("adj_folded")

        def scope():
            return ExitStack()

        def sb(stack, name, shape, dt=F32):
            return stack.enter_context(nc.sbuf_tensor(name, shape, dt))

        X = sb(ctx, "X", [P, NB, H])
        HN = sb(ctx, "HN", [P, NB, H])
        ACC = sb(ctx, "ACC", [P, NB, KW])
        SMAX = sb(ctx, "SMAX", [P, NB])
        DEG = sb(ctx, "DEG", [P, NB])
        MULT = sb(ctx, "MULT", [P, NB])
        LOGM = sb(ctx, "LOGM", [P, NB])
        STAT = sb(ctx, "STAT", [P, 4, NB])
        iota_f = sb(ctx, "iota_f", [P, P])
        iota_i = sb(ctx, "iota_i", [P, P], I32)
        part_f = sb(ctx, "part_f", [P, 1])
        part_i = sb(ctx, "part_i", [P, 1], I32)
        ident = sb(ctx, "ident", [P, P])
        ident8 = sb(ctx, "ident8", [P, P], FP8)
        ones8 = sb(ctx, "ones8", [P, 1], FP8)
        ones_row = sb(ctx, "ones_row", [1, P])
        half_pi = sb(ctx, "half_pi", [P, 1])
        zero1 = sb(ctx, "zero1", [P, 1])
        LP = sb(ctx, "LP", [P, 6, L, H])
        GN = sb(ctx, "GN", [P, 2, H])
        WQK = sb(ctx, "WQK", [H, L, 2 * H])
        WM = sb(ctx, "WM", [H, L, H])
        WU = sb(ctx, "WU", [H, L, 2, H])
        F1 = sb(ctx, "F1", [RBF, H])
        F1B = sb(ctx, "F1B", [H, 1])
        F2 = sb(ctx, "F2", [H, H])
        F2B = sb(ctx, "F2B", [1, H])
        n_extra = sb(ctx, "n_extra", [1, 1], I32)

        psum = ctx.enter_context(nc.psum_tensor("psum", [P, 8 * 512], F32))

        def bank(b, n=1):
            return psum[:, b * 512:(b + n) * 512]

        with scope() as st:
            src_i, dst_i = sb(st, "src_i", [EP, ET], I32), sb(st, "dst_i", [EP, ET], I32)
            tmp_i = sb(st, "tmp_i", [EP, ET], I32)
            fields = sb(st, "fields", [EP, ET, RW - RBF])
            bs_f, bd_f, key_f = (sb(st, n, [EP, ET]) for n in ("bs_f", "bd_f", "key_f"))
            home = sb(st, "home", [EP, ET])
            hist = sb(st, "hist", [NB, NS, NB])
            base = sb(st, "base", [NB, NS, 2, NB])
            cell = sb(st, "cell", [NB, 6, NB])
            cell_i = sb(st, "cell_i", [NB, 2, NB], I32)
            one_bs, one_bd = sb(st, "one_bs", [EP, 2, NS, NB], BF16), sb(st, "one_bd", [EP, 2, NS, NB], BF16)
            one_bd32 = sb(st, "one_bd32", [EP, NS, NB])
            one_bsT = sb(st, "one_bsT", [NB, NS, EP])
            lower = sb(st, "lower", [EP, EP])
            upper = sb(st, "upper", [NB, NB])
            ones49 = sb(st, "ones49", [NB, NB])
            junk = sb(st, "junk", [EP, NS, EP])
            look = sb(st, "look", [EP, NS, 2, NB])
            found = sb(st, "found", [EP, NS, 2])
            rank = sb(st, "rank", [EP, NS])
            slot_a, slot_b, slot_m = (sb(st, n, [EP, NS]) for n in ("slot_a", "slot_b", "slot_m"))
            slot_i = sb(st, "slot_i", [EP, 4, NS], I32)
            attr_in = sb(st, "attr_in", [EP, NS, JB, RBF])
            rec_out = sb(st, "rec_out", [EP, 2, NS, 5, RW])
            zeros = sb(st, "zeros", [P, NB * RW])
        ze_tab = sb(ctx, "ze_tab", [P, NB, 2 * G])
        with scope() as st:
            z_row = sb(st, "z_row", [NELEM, NPAD], I32)
            z_hot = sb(st, "z_hot", [NELEM, NPAD])
            EMB = sb(st, "EMB", [NELEM, 2 * G])
            embT = sb(st, "embT", [G, NELEM])
            adapt_sb = sb(st, "adapt_sb", [G, G])
        with scope() as st:
            TD = sb(st, "TD", [P, 3, NB, DW], BF16)
            TS = sb(st, "TS", [P, 3, NB, KW], BF16)
            with scope() as s2:
                HT = sb(s2, "HT", [H, NPAD])
                AT = sb(s2, "AT", [H, NPAD])
                W1 = sb(s2, "W1", [P, NB, DW])
                W2 = sb(s2, "W2", [P, NB, DW])
            with scope() as s2:
                rec = sb(s2, "rec", [P, GC, RW])
                td_row = sb(s2, "td_row", [P, 3, DW], BF16)
                ts_row = sb(s2, "ts_row", [P, 3, KW], BF16)
                oh = sb(s2, "oh", [P, NG, 3, GC, P], FP8)
                oh_d = sb(s2, "oh_d", [P, GC, P], FP8)
                os32 = sb(s2, "os32", [P, GC, P])
                adj_out = sb(s2, "adj_out", [P, GC, P], BF16)
                attrT = sb(s2, "attrT", [RBF, GC * P])
                act1 = sb(s2, "act1", [H, GC * P])
                src_e = sb(s2, "src_e", [P, GC, G])
                gate = sb(s2, "gate", [P, GC, H])
                cw = sb(s2, "cw", [P, 3, GC])
                val = sb(s2, "val", [P, GC, KW])
                xk = sb(s2, "xk", [P, GC, KW])
                runmax = sb(s2, "runmax", [P, P])
                rowmax = sb(s2, "rowmax", [P, 4])
                smax3 = sb(s2, "smax3", [P, 3], BF16)
                S = sb(s2, "S", [P, NB])
                ES = sb(s2, "ES", [P, 2, NB])
                HE = sb(s2, "HE", [P, NB, H])
                VAL = sb(s2, "VAL", [P, NB, KW])
        with scope() as st:
            AJ = sb(st, "AJ", [P, 2, NB, 4 * P], BF16)
            dinv = sb(st, "dinv", [P, NB])
            g_f = sb(st, "g_f", [P, NB, H])
            g_r = sb(st, "g_r", [P, NB, H])
            g3 = sb(st, "g3", [P, NB, 3, H], BF16)
            mm = sb(st, "mm", [P, NB, H])
            rec_l = sb(st, "rec_l", [P, RW])
            ohs_l, ohd_l, ohsT_l = (sb(st, n, [P, P]) for n in ("ohs_l", "ohd_l", "ohsT_l"))
            val_l = sb(st, "val_l", [P, H])

        block = ctx.enter_context(nc.Block())

        def program(name, e):
            count = [0]

            def serial(steps, wait_last=False):
                for who, fn, inc in steps:
                    if who == name:
                        e.wait_ge(order, count[0])
                        fn(e).then_inc(order, inc)
                    count[0] += inc

            def barrier():
                for who in ENGINES:
                    if who == name:
                        e.wait_ge(order, count[0])
                        e.drain().then_inc(order, 1)
                    count[0] += 1
                e.wait_ge(order, count[0])

            turns = e.alloc_register("turns_" + name)
            e.reg_mov(turns, 1)
            if name == "sync":
                e.sem_inc(turn, 1)

            def in_turn(steps):
                off = 0
                for who, fn, inc in steps:
                    if who == name:
                        e.wait_ge(turn, e.snap(turns, min_val=1, max_val=1 << 29) + off)
                        e.sem_inc(absorb, 1)
                        fn(e).then_inc(turn, inc)
                    off += inc
                e.reg_add(turns, turns, off)

            def in_turn_end():
                e.wait_ge(turn, e.snap(turns, min_val=1, max_val=1 << 29))
                e.sem_inc(absorb, 1)

            def sy(fn): return ("sync", fn, 16)
            def po(fn): return ("gpsimd", fn, 1)
            def v(fn): return ("vector", fn, 1)
            def a(fn): return ("scalar", fn, 1)
            def t(fn): return ("tensor", fn, 1)

            def many(fns):
                def run(e):
                    for f in fns:
                        last = f(e)
                    return last
                return run

            def bc(ap, shape):
                return ap.broadcast_to(shape)

            def load_all():
                flat = lambda w: w.rearrange("l h -> (l h)").partition_broadcast(P)
                vec = lambda w: w.partition_broadcast(P)
                col = lambda w: w.rearrange("(h o) -> h o", o=1)
                x_main = x[0:(NB - 1) * P, :].rearrange("(b p) h -> p b h", p=P)
                steps = [
                    v(lambda e: e.memset(X[:, :, :], 0.0)),
                    v(lambda e: e.memset(MULT[:, :], 1.0)),
                    sy(lambda e: e.dma_start(X[:, 0:NB - 1, :], x_main)),
                    sy(lambda e: e.dma_start(X[0:TAIL, NB - 1, :], x[(NB - 1) * P:N, :])),
                    sy(lambda e: e.dma_start(MULT[0:TAIL, NB - 1:NB], node_vec[(NB - 1) * P:N].rearrange("(p o) -> p o", o=1))),
                ]
                def mult_main(e):
                    with nc.allow_non_contiguous_dma(reason="one column of node values per block"):
                        return e.dma_start(MULT[:, 0:NB - 1], node_vec[0:(NB - 1) * P].rearrange("(b p) -> p b", p=P))
                steps.append(sy(mult_main))
                for n, w in enumerate((gq, bq, gk, bk, go, bo)):
                    steps.append(sy(lambda e, n=n, w=w: e.dma_start(LP[:, n, :, :].rearrange("p l h -> p (l h)"), flat(w))))
                steps += [
                    sy(lambda e: e.dma_start(GN[:, 0, :], vec(gn))), sy(lambda e: e.dma_start(GN[:, 1, :], vec(bn))),
                    sy(lambda e: e.dma_start(WQK[:, :, 0:H], Wq.rearrange("l i o -> i l o"))),
                    sy(lambda e: e.dma_start(WQK[:, :, H:2 * H], Wk.rearrange("l i o -> i l o"))),
                    sy(lambda e: e.dma_start(WM[:, :, :], Wm.rearrange("l i o -> i l o"))),
                    sy(lambda e: e.dma_start(WU[:, :, 0, :], Wu[:, 0:H, :].rearrange("l i o -> i l o"))),
                    sy(lambda e: e.dma_start(WU[:, :, 1, :], Wu[:, H:2 * H, :].rearrange("l i o -> i l o"))),
                    sy(lambda e: e.dma_start(F1[:, :], F1W)), sy(lambda e: e.dma_start(F2[:, :], F2W)),
                    sy(lambda e: e.dma_start(F1B[:, :], col(F1b))),
                    sy(lambda e: e.dma_start(F2B[:, :], F2b.rearrange("(o h) -> o h", o=1))),
                    po(lambda e: e.iota(iota_i[:, :], pattern=[[1, P]], base=1, channel_multiplier=0)),
                    po(lambda e: e.iota(part_i[:, :], pattern=[[0, 1]], base=0, channel_multiplier=1)),
                    v(lambda e: e.tensor_copy(iota_f[:, :], iota_i[:, :])),
                    v(lambda e: e.tensor_copy(part_f[:, :], part_i[:, :])),
                    v(lambda e: e.tensor_scalar(ident[:, :], iota_f[:, :], 1.0, part_f[:, 0:1], ALU.subtract, ALU.is_equal)),
                    v(lambda e: e.tensor_copy(ident8[:, :], ident[:, :], saturate=False)),
                    v(lambda e: e.tensor_copy(ones8[:, :], iota_f[:, 0:1], saturate=False)),
                    v(lambda e: e.memset(ones_row[:, :], 1.0)),
                    v(lambda e: e.memset(half_pi[:, :], HALF_PI)),
                    v(lambda e: e.memset(zero1[:, :], 0.0)),
                    v(lambda e: e.memset(DEG[:, :], 1.0)),
                ]
                serial(steps)

            def count_cells():
                serial([
                    v(lambda e: e.memset(zeros[:, :], 0.0)),
                    sy(lambda e: e.dma_start(src_i[:, :], src.rearrange("(p t) -> p t", t=ET))),
                    sy(lambda e: e.dma_start(dst_i[:, :], dst.rearrange("(p t) -> p t", t=ET))),
                    sy(lambda e: e.dma_start(home[:, :], edge_weight.rearrange("(p t) -> p t", t=ET))),
                    v(lambda e: e.tensor_copy(fields[:, :, 2], home[:, :])),
                ])
                for raw, local, block_f, fb in ((src_i, 0, bs_f, 3), (dst_i, 1, bd_f, 4)):
                    serial([
                        v(lambda e, raw=raw: e.tensor_scalar(tmp_i[:, :], raw[:, :], P - 1, None, ALU.bitwise_and)),
                        v(lambda e, local=local: e.tensor_scalar(fields[:, :, local], tmp_i[:, :], 1.0, None, ALU.add)),
                        v(lambda e, raw=raw: e.tensor_scalar(tmp_i[:, :], raw[:, :], 7, None, ALU.logical_shift_right)),
                        v(lambda e, block_f=block_f: e.tensor_copy(block_f[:, :], tmp_i[:, :])),
                        v(lambda e, fb=fb: e.tensor_copy(fields[:, :, fb].bitcast(I32), tmp_i[:, :])),
                    ])
                serial([
                    v(lambda e: e.scalar_tensor_tensor(key_f[:, :], bs_f[:, :], float(NB), bd_f[:, :], ALU.mult, ALU.add)),
                    v(lambda e: e.scalar_tensor_tensor(home[:, :], bs_f[:, :], float(NB * P), bd_f[:, :], ALU.mult, ALU.add)),
                    v(lambda e: e.tensor_scalar(lower[:, :], iota_f[0:EP, 0:EP], 1.0, part_f[0:EP, 0:1], ALU.subtract, ALU.is_lt)),
                    v(lambda e: e.tensor_scalar(upper[:, :], iota_f[0:NB, 0:NB], 1.0, part_f[0:NB, 0:1], ALU.subtract, ALU.is_gt)),
                    v(lambda e: e.memset(ones49[:, :], 1.0)),
                ])
                HG = NS
                groups = ET // HG
                iota49 = lambda n: iota_f[0:EP, 0:NB].unsqueeze(1).broadcast_to([EP, n, NB])
                if name == "vector":
                    e.tensor_scalar(iota_f[:, :], iota_f[:, :], 1.0, None, ALU.subtract).then_inc(s_hdve, 1)
                    e.wait_ge(s_hdve, 1)
                    for g in range(groups):
                        if g >= 2:
                            e.wait_ge(s_hpe, g - 1)
                        c0 = g * HG
                        e.tensor_tensor(one_bs[:, g % 2], iota49(HG), bs_f[:, c0:c0 + HG].unsqueeze(2).broadcast_to([EP, HG, NB]), ALU.is_equal)
                        e.tensor_tensor(one_bd[:, g % 2], iota49(HG), bd_f[:, c0:c0 + HG].unsqueeze(2).broadcast_to([EP, HG, NB]), ALU.is_equal).then_inc(s_hdve, 1)
                    e.wait_ge(s_hpe, groups)
                if name == "tensor":
                    for g in range(groups):
                        e.wait_ge(s_hdve, g + 2)
                        for k in range(HG):
                            c = g * HG + k
                            s, i = c // SC, c % SC
                            last = e.matmul(bank(0)[0:NB, s * NB:(s + 1) * NB], one_bs[:, g % 2, k, :], one_bd[:, g % 2, k, :],
                                            start=i == 0, stop=i == SC - 1)
                        last.then_inc(s_hpe, 1)
                tot, over, chunks, before = cell[:, 0], cell[:, 1], cell[:, 2], cell[:, 3]
                steps = [
                    v(lambda e: e.tensor_copy(hist[:, :, :], bank(0)[0:NB, 0:NS * NB].rearrange("p (s b) -> p s b", s=NS))),
                    v(lambda e: e.tensor_reduce(tot, hist[:, :, :].rearrange("p s b -> p b s"), AX.X, ALU.add)),
                    v(lambda e: e.tensor_scalar(over, tot, float(CAP), 0.0, ALU.subtract, ALU.max)),
                    v(lambda e: e.tensor_scalar(cell_i[:, 0], over, float(P - 1), None, ALU.add)),
                    v(lambda e: e.tensor_scalar(cell_i[:, 1], cell_i[:, 0], 7, None, ALU.logical_shift_right)),
                    v(lambda e: e.tensor_copy(chunks, cell_i[:, 1])),
                    v(lambda e: e.tensor_tensor_scan(before, chunks, chunks, 0.0, ALU.add, ALU.bypass)),
                    t(lambda e: e.matmul(bank(1)[0:NB, 0:1], upper[:, :], before[:, NB - 1:NB], start=True, stop=True)),
                    t(lambda e: e.matmul(bank(2)[0:NB, 0:1], ones49[:, :], before[:, NB - 1:NB], start=True, stop=True)),
                    v(lambda e: e.tensor_copy(n_extra[0:1, 0:1], bank(2)[0:1, 0:1])),
                    v(lambda e: e.tensor_tensor(before, before, chunks, ALU.subtract)),
                    v(lambda e: e.tensor_scalar(before, before, bank(1)[0:NB, 0:1], float(P), ALU.add, ALU.mult)),
                    v(lambda e: e.tensor_scalar(before, before, float(GRID - CAP), None, ALU.add)),
                    v(lambda e: e.memset(base[:, 0, 0, :], 0.0)),
                ]
                for s in range(NS):
                    steps.append(v(lambda e, s=s: e.tensor_copy(base[:, s, 1, :], before)))
                    if s:
                        steps.append(v(lambda e, s=s: e.tensor_tensor(base[:, s, 0, :], base[:, s - 1, 0, :], hist[:, s - 1, :], ALU.add)))
                for b in range(NB):
                    steps.append(sy(lambda e, b=b: e.dma_start(rec_rows[b], zeros[:, :])))
                serial(steps)

            def extra_count():
                e.wait_ge(order, count[0])
                e.sem_inc(absorb, 1)
                return e.value_load(n_extra[0:1, 0:1], min_val=0, max_val=NOV)

            def fill_extra():
                barrier()
                n = extra_count()
                with e.If(n > 0):
                    with e.Fori(0, n) as j:
                        in_turn([sy(lambda e: e.dma_start(rec_extra[ds(j, 1), :, :].rearrange("o p w -> (o p) w"), zeros[:, 0:RW]))])
                    in_turn_end()
                barrier()

            def place_edges():
                ITER = SC
                ident_e = ident[0:EP, 0:EP]
                attr = edge_attr_40.rearrange("(p s i) r -> p s (i r)", s=NS, i=SC)
                fields_s = fields[:, :, :].rearrange("p (s i) f -> p s i f", s=NS)
                by_stream = lambda arr: arr[:, :].rearrange("p (s i) -> p s i", s=NS)
                keyT, bsT, found_ps, hist_ps = bank(0, 2), bank(2, 2), bank(4, 2), bank(6)

                def scattered(i):
                    e.wait_ge(s_scat[i % 10], 16 * NS * (i // 10 + 1))

                at4 = lambda ps, s, w, tot=4: (s // 4) * 512 + (s % 4) * w
                if name == "sync":
                    for b in range(ITER // JB):
                        if b:
                            e.wait_ge(s_asm, 2 * b)
                        e.dma_start(attr_in[:, :, :, :].rearrange("p s i r -> p s (i r)"),
                                    attr[:, :, b * JB * RBF:(b + 1) * JB * RBF]).then_inc(s_edges, 16)
                if name == "scalar":
                    for b in range(ITER // JB):
                        e.wait_ge(s_edges, 16 * (b + 1))
                        for h in range(2):
                            n = 2 * b + h
                            if n >= 2:
                                for i in range(5 * (n - 2), 5 * (n - 1)):
                                    scattered(i)
                            for k in range(5):
                                j = 5 * h + k
                                e.copy(rec_out[:, n % 2, :, k, 0:RBF], attr_in[:, :, j, :])
                                last = e.copy(rec_out[:, n % 2, :, k, RBF:RW], fields_s[:, :, b * JB + j, :])
                            last.then_inc(s_asm, 1)
                if name == "tensor":
                    for i in range(ITER):
                        if i:
                            e.wait_ge(s_rank, i)
                        for s in range(NS):
                            o = at4(None, s, EP)
                            col = s * SC + i
                            e.transpose(keyT[0:EP, o:o + EP], key_f[:, col:col + 1].broadcast_to([EP, EP]), ident_e)
                            last = e.transpose(bsT[0:NB, o:o + EP], bs_f[:, col:col + 1].broadcast_to([EP, NB]), ident_e)
                        last.then_inc(s_pe, 1)
                        e.wait_ge(s_dve, 2 * i + 1)
                        for s in range(NS):
                            e.matmul(hist_ps[0:NB, s * NB:(s + 1) * NB], one_bs[:, i % 2, s, :], one_bd[:, i % 2, s, :], start=True, stop=True)
                        for s in range(NS):
                            o = at4(None, s, 2 * NB)
                            last = e.matmul(found_ps[0:EP, o:o + 2 * NB], one_bsT[:, s, :], base[:, s, :, :].rearrange("p a b -> p (a b)"), start=True, stop=True)
                        last.then_inc(s_pe, 1)
                if name == "vector":
                    iota49 = iota_f[0:EP, 0:NB].unsqueeze(1).broadcast_to([EP, NS, NB])
                    for i in range(ITER):
                        bsv = by_stream(bs_f)[:, :, i:i + 1].broadcast_to([EP, NS, NB])
                        bdv = by_stream(bd_f)[:, :, i:i + 1].broadcast_to([EP, NS, NB])
                        e.tensor_tensor(one_bs[:, i % 2], iota49, bsv, ALU.is_equal)
                        e.tensor_tensor(one_bd[:, i % 2], iota49, bdv, ALU.is_equal)
                        e.tensor_tensor(one_bd32[:, :, :], iota49, bdv, ALU.is_equal)
                        e.wait_ge(s_pe, 2 * i + 1)
                        for h in range(2):
                            last = e.tensor_scalar(one_bsT[:, 4 * h:4 * h + 4, :].rearrange("p s e -> p (s e)"), bsT[0:NB, h * 512:h * 512 + 4 * EP],
                                                   part_f[0:NB, 0:1], None, ALU.is_equal)
                        last.then_inc(s_dve, 1)
                        for s in range(NS):
                            o = at4(None, s, EP)
                            last = e.scalar_tensor_tensor(junk[:, s, :], keyT[0:EP, o:o + EP], key_f[:, s * SC + i:s * SC + i + 1], lower[:, :],
                                                          ALU.is_equal, ALU.mult, accum_out=rank[:, s:s + 1])
                        last.then_inc(s_rank, 1)
                        e.wait_ge(s_pe, 2 * i + 2)
                        for h in range(2):
                            e.tensor_tensor(look[:, 4 * h:4 * h + 4, :, :], found_ps[0:EP, h * 512:h * 512 + 8 * NB].rearrange("p (s a b) -> p s a b", s=4, a=2),
                                            one_bd32[:, 4 * h:4 * h + 4, :].unsqueeze(2).broadcast_to([EP, 4, 2, NB]), ALU.mult)
                        e.tensor_tensor(base[:, :, 0, :], base[:, :, 0, :], hist_ps[0:NB, 0:NS * NB].rearrange("p (s b) -> p s b", s=NS), ALU.add).then_inc(s_dve, 1)
                        e.wait_ge(s_dve, 2 * i + 2)
                        c = [0]
                        def link(ins):
                            c[0] += 1
                            ins.then_inc(s_load, 1)
                            e.wait_ge(s_load, 6 * i + c[0])
                        link(e.tensor_reduce(found[:, :, :], look[:, :, :, :], AX.X, ALU.add))
                        link(e.tensor_tensor(slot_m[:, :], rank[:, :], found[:, :, 0], ALU.add))
                        link(e.scalar_tensor_tensor(slot_a[:, :], slot_m[:, :], float(NB), by_stream(home)[:, :, i], ALU.mult, ALU.add))
                        link(e.tensor_tensor(slot_b[:, :], slot_m[:, :], found[:, :, 1], ALU.add))
                        link(e.tensor_tensor(slot_b[:, :], slot_b[:, :], slot_a[:, :], ALU.subtract))
                        link(e.scalar_tensor_tensor(slot_b[:, :], slot_m[:, :], float(CAP), slot_b[:, :], ALU.is_ge, ALU.mult))
                        if i >= 4:
                            scattered(i - 4)
                        e.tensor_tensor(slot_i[:, i % 4, :], slot_a[:, :], slot_b[:, :], ALU.add).then_inc(s_idx, 1)
                if name == "gpsimd":
                    for i in range(ITER):
                        e.wait_ge(s_idx, i + 1)
                        e.wait_ge(s_asm, i // 5 + 1)
                        for s in range(NS):
                            e.indirect_dma_start(REC[:, :], bass.IndirectOffsetOnAxis(ap=slot_i[:, i % 4, s:s + 1], axis=0),
                                                 rec_out[:, (i // 5) % 2, s, i % 5, :], None).then_inc(s_scat[i % 10], 16)
                    for i in range(ITER - 10, ITER):
                        scattered(i)
                barrier()
                serial([v(lambda e: e.tensor_scalar(iota_f[:, :], iota_f[:, :], 1.0, None, ALU.add))])

            def wide(ap, w=H):
                return ap.unsqueeze(2).broadcast_to([P, NB, w])

            def every(ap, w=H):
                return ap.unsqueeze(1).broadcast_to([P, NB, w])

            def normalise(to, of, tmp, g=None, b=None):
                mean, var = STAT[:, 0, :], STAT[:, 1, :]
                steps = [
                    v(lambda e: e.tensor_reduce(mean, of, AX.X, ALU.add)),
                    v(lambda e: e.tensor_scalar(mean, mean, 1.0 / H, None, ALU.mult)),
                    v(lambda e: e.tensor_tensor(to, of, wide(mean), ALU.subtract)),
                    v(lambda e: e.tensor_tensor(tmp, to, to, ALU.mult)),
                    v(lambda e: e.tensor_reduce(var, tmp, AX.X, ALU.add)),
                    v(lambda e: e.tensor_scalar(var, var, 1.0 / H, 1e-5, ALU.mult, ALU.add)),
                    a(lambda e: e.activation(mean, var, ACT.Sqrt)),
                    v(lambda e: e.reciprocal(var, mean)),
                    v(lambda e: e.tensor_tensor(to, to, wide(var), ALU.mult)),
                ]
                if g is not None:
                    steps += [v(lambda e: e.tensor_tensor(to, to, every(g), ALU.mult)),
                              v(lambda e: e.tensor_tensor(to, to, every(b), ALU.add))]
                return steps

            def split(parts, of, rest):
                return [
                    a(lambda e: e.copy(parts[0], of)),
                    v(lambda e: e.tensor_tensor(rest, of, parts[0], ALU.subtract)),
                    a(lambda e: e.copy(parts[1], rest)),
                    v(lambda e: e.tensor_tensor(parts[2], rest, parts[1], ALU.subtract)),
                ]

            def transposed(to, of):
                steps = []
                for b0 in range(0, NB, 16):
                    n = min(16, NB - b0)
                    steps += [
                        t(many([lambda e, b0=b0, k=k: e.transpose(bank(0, 4)[0:H, k * P:(k + 1) * P], of[:, b0 + k, 0:H], ident[:, :])
                                for k in range(n)])),
                        a(lambda e, b0=b0, n=n: e.copy(to[:, b0 * P:(b0 + n) * P], bank(0, 4)[0:H, 0:n * P])),
                    ]
                return steps

            def per_block(to, width, products):
                fit = 512 // width
                steps = []
                for b0 in range(0, NB, 8 * fit):
                    n = min(8 * fit, NB - b0)
                    spot = lambda k: bank(k // fit)[:, (k % fit) * width:(k % fit + 1) * width]
                    steps.append(t(many([
                        lambda e, b=b0 + k, k=k, m=m: e.matmul(spot(k), products[m][0](b), products[m][1], start=m == 0, stop=m == len(products) - 1)
                        for k in range(n) for m in range(len(products))])))
                    steps.append(a(many([
                        lambda e, b=b0 + j * fit, j=j, c=min(fit, n - j * fit):
                            e.copy(to[:, b:b + c, 0:width], bank(j)[:, 0:c * width].rearrange("p (b w) -> p b w", w=width))
                        for j in range(-(-n // fit))])))
                return steps

            def embed():
                cols = lambda b: z_hot[:, b * P:(b + 1) * P]
                serial([
                    v(lambda e: e.memset(z_row[:, :], 0)),
                    sy(lambda e: e.dma_start(z_row[:, 0:N], node_type_119.partition_broadcast(NELEM))),
                    sy(lambda e: e.dma_start(EMB[:, 0:G], emb)),
                    sy(lambda e: e.dma_start(adapt_sb[:, :], adapt)),
                    v(lambda e: e.tensor_scalar(z_hot[:, :], z_row[:, :], part_f[0:NELEM, 0:1], None, ALU.is_equal)),
                    t(lambda e: e.transpose(bank(0)[0:G, 0:NELEM], EMB[:, 0:G], ident[0:NELEM, 0:NELEM])),
                    a(lambda e: e.copy(embT[:, :], bank(0)[0:G, 0:NELEM])),
                    t(lambda e: e.matmul(bank(0)[0:NELEM, 0:G], embT[:, :], adapt_sb[:, :], start=True, stop=True)),
                    a(lambda e: e.copy(EMB[:, G:2 * G], bank(0)[0:NELEM, 0:G])),
                    *per_block(ze_tab, 2 * G, [(cols, EMB[:, :])]),
                ])

            def first_tables():
                serial([
                    *normalise(HN[:, :, :], X[:, :, :], W1[:, :, 0:H]),
                    v(lambda e: e.tensor_scalar(HN[:, :, :], HN[:, :, :], 0.0, None, ALU.max)),
                    v(lambda e: e.tensor_scalar(LOGM[:, :], MULT[:, :], 1.0, None, ALU.max)),
                    a(lambda e: e.activation(LOGM[:, :], LOGM[:, :], ACT.Ln)),
                    v(lambda e: e.tensor_tensor(W1[:, :, 0:H], HN[:, :, :], wide(MULT[:, :]), ALU.mult)),
                    v(lambda e: e.tensor_copy(W1[:, :, H:KW], MULT[:, :].unsqueeze(2))),
                    v(lambda e: e.tensor_copy(W1[:, :, KW:GW], ze_tab[:, :, G:2 * G])),
                    *split([TD[:, k, :, 0:GW] for k in range(3)], W1[:, :, 0:GW], W2[:, :, 0:GW]),
                    *split([TS[:, k, :, 0:G] for k in range(3)], ze_tab[:, :, 0:G], W2[:, :, 0:G]),
                    v(lambda e: e.memset(ACC[:, :, :], 0.0)),
                ])

            def after_gate():
                tot = STAT[:, 2, :]
                serial([
                    v(lambda e: e.tensor_scalar(tot, ACC[:, :, H], 1e-8, None, ALU.max)),
                    v(lambda e: e.reciprocal(STAT[:, 3, :], tot)),
                    v(lambda e: e.tensor_tensor(W1[:, :, 0:H], ACC[:, :, 0:H], wide(STAT[:, 3, :]), ALU.mult)),
                    v(lambda e: e.tensor_tensor(W1[:, :, 0:H], W1[:, :, 0:H], HN[:, :, :], ALU.add)),
                    *normalise(HN[:, :, :], W1[:, :, 0:H], W2[:, :, 0:H], GN[:, 0, :], GN[:, 1, :]),
                ])

            def layer_tables(l):
                serial([
                    *transposed(HT[:, :], HN[:, :, :]),
                    *per_block(W1[:, :, :], 2 * H, [(lambda b: HT[:, b * P:(b + 1) * P], WQK[:, l, :])]),
                    *normalise(W2[:, :, 0:H], W1[:, :, 0:H], W2[:, :, H:2 * H], LP[:, 0, l, :], LP[:, 1, l, :]),
                    v(lambda e: e.memset(W2[:, :, H:KW], 1.0)),
                ])
                serial([
                    a(lambda e: e.copy(TS[:, 0, :, :], W2[:, :, 0:KW])),
                    v(lambda e: e.tensor_tensor(W2[:, :, 0:KW], W2[:, :, 0:KW], TS[:, 0, :, :], ALU.subtract)),
                    a(lambda e: e.copy(TS[:, 1, :, :], W2[:, :, 0:KW])),
                    v(lambda e: e.tensor_tensor(TS[:, 2, :, :], W2[:, :, 0:KW], TS[:, 1, :, :], ALU.subtract)),
                    *normalise(W2[:, :, 0:H], W1[:, :, H:2 * H], W2[:, :, H:2 * H], LP[:, 2, l, :], LP[:, 3, l, :]),
                    v(lambda e: e.tensor_copy(W2[:, :, H:KW], LOGM[:, :].unsqueeze(2))),
                    v(lambda e: e.tensor_copy(W2[:, :, KW:DW], HN[:, :, :])),
                    *split([TD[:, k, :, :] for k in range(3)], W2[:, :, :], W1[:, :, :]),
                    v(lambda e: e.memset(ACC[:, :, :], 0.0)),
                    v(lambda e: e.memset(SMAX[:, :], -BIG)),
                ])

            def layer_update(l):
                den = STAT[:, 2, :]
                steps = [
                    v(lambda e: e.tensor_scalar(den, ACC[:, :, H], 1e-10, None, ALU.add)),
                    v(lambda e: e.reciprocal(STAT[:, 3, :], den)),
                    v(lambda e: e.tensor_tensor(W1[:, :, 0:H], ACC[:, :, 0:H], wide(STAT[:, 3, :]), ALU.mult)),
                    *transposed(HT[:, :], W1[:, :, 0:H]),
                ]
                for c in range(0, NPAD, 4 * 512):
                    n = min(4 * 512, NPAD - c)
                    steps += [
                        t(many([lambda e, c=c, k=k, w=min(512, n - k): e.matmul(bank(0, 4)[0:H, k:k + w], WM[:, l, :], HT[:, c + k:c + k + w], start=True, stop=True)
                                for k in range(0, n, 512)])),
                        a(lambda e, c=c, n=n: e.copy(AT[:, c:c + n], bank(0, 4)[0:H, 0:n])),
                    ]
                steps += [
                    *transposed(HT[:, :], HN[:, :, :]),
                    *per_block(W1[:, :, :], H, [(lambda b: HT[:, b * P:(b + 1) * P], WU[:, l, 0, :]),
                                                (lambda b: AT[:, b * P:(b + 1) * P], WU[:, l, 1, :])]),
                    v(lambda e: e.scalar_tensor_tensor(W2[:, :, 0:H], W1[:, :, 0:H], 0.01, W1[:, :, 0:H], ALU.mult, ALU.max)),
                    v(lambda e: e.tensor_tensor(W1[:, :, 0:H], W2[:, :, 0:H], HN[:, :, :], ALU.add)),
                    *normalise(HN[:, :, :], W1[:, :, 0:H], W2[:, :, 0:H], LP[:, 4, l, :], LP[:, 5, l, :]),
                ]
                serial(steps)

            def one(ap):
                return ap

            def bd_of(bd, k, n=1):
                return slice(bd + k, bd + k + n) if isinstance(bd, int) else ds(bd, n)

            def build_one_hots(n, ohg):
                spots = bank(0, 2)
                where = lambda f: rec[:, 0:n, f:f + 1].broadcast_to([P, n, P])
                iotas = iota_f[:, :].unsqueeze(1).broadcast_to([P, n, P])
                flip = lambda of: t(many([lambda e, c=c: e.matmul(spots[:, c * P:(c + 1) * P], of[:, c, :], ident8[:, :], start=True, stop=True) for c in range(n)]))
                take = lambda k: a(lambda e: e.activation(ohg[:, k, 0:n, :], spots[:, 0:n * P].rearrange("p (c e) -> p c e", c=n), ACT.Copy, saturate=False))
                return [
                    v(lambda e: e.tensor_tensor(ohg[:, 2, 0:n, :], iotas, where(F_SRC), ALU.is_equal, saturate=False)),
                    v(lambda e: e.tensor_tensor(oh_d[:, 0:n, :], iotas, where(F_DST), ALU.is_equal, saturate=False)),
                    flip(ohg[:, 2, :, :]), take(0), flip(oh_d[:, :, :]), take(1),
                ]

            def gather(n, spot, hot, rows, width):
                return t(many([lambda e, c=c, k=k: e.matmul(spot(c), hot[:, c, :], rows(c, k)[:, 0:width], start=k == 0, stop=k == 2)
                               for c in range(n) for k in range(3)]))

            def stage_src(bs, w=KW):
                return v(lambda e: e.tensor_copy(ts_row[:, :, 0:w], TS[:, :, ds(bs, 1), 0:w].rearrange("p k o w -> p k (o w)")))

            def stage_dst(bd, w=DW):
                return v(lambda e: e.tensor_copy(td_row[:, :, 0:w], TD[:, :, ds(bd, 1), 0:w].rearrange("p k o w -> p k (o w)")))

            def dst_rows(bd):
                return (lambda c, k: TD[:, k, bd + c, :]) if isinstance(bd, int) else (lambda c, k: td_row[:, k, :])

            src_rows = lambda c, k: ts_row[:, k, :]

            def scatter(n, hots, vals, spot):
                return t(many([lambda e, c=c: e.matmul(spot, hots[:, c, :], vals[:, c, :], start=c == 0, stop=c == n - 1) for c in range(n)]))

            d_spot = lambda c: bank(2, 2)[:, c * P:c * P + DW]
            d_all = lambda n: bank(2, 2)[:, 0:GC * P].rearrange("p (c w) -> p c w", w=P)[:, 0:n, :]
            q_spot = lambda c: bank(4)[:, c * KW:(c + 1) * KW]
            q_all = lambda n, w=KW: bank(4)[:, 0:n * KW].rearrange("p (c w) -> p c w", w=KW)[:, :, 0:w]

            def gate_values(n, ohg, bs, bd):
                both = range(0, n * P, 512)
                return [
                    t(many([lambda e, c=c: e.transpose(bank(0, 2)[0:RBF, c * P:(c + 1) * P], rec[:, c, 0:RBF], ident[:, :]) for c in range(n)])),
                    v(lambda e: e.tensor_copy(attrT[:, 0:n * P], bank(0, 2)[0:RBF, 0:n * P])),
                    t(many([lambda e, k=k: e.matmul(bank(0, 2)[0:H, k:min(k + 512, n * P)], F1[:, :], attrT[:, k:min(k + 512, n * P)], start=True, stop=True)
                            for k in both])),
                    a(lambda e: e.activation(act1[:, 0:n * P], bank(0, 2)[0:H, 0:n * P], ACT.Silu, bias=F1B[:, 0:1])),
                    t(many([f for c in range(n) for f in (
                        lambda e, c=c: e.matmul(bank(5)[:, c * H:(c + 1) * H], act1[:, c * P:(c + 1) * P], F2[:, :], start=True, stop=False),
                        lambda e, c=c: e.matmul(bank(5)[:, c * H:(c + 1) * H], ones_row[:, :], F2B[:, :], start=False, stop=True))])),
                    gather(n, lambda c: d_spot(c)[:, 0:GW], ohg[:, 1], dst_rows(bd), GW),
                    gather(n, lambda c: q_spot(c)[:, 0:G], ohg[:, 0], src_rows, G),
                    a(lambda e: e.copy(src_e[:, 0:n, :], q_all(n, G))),
                    v(lambda e: e.tensor_tensor(src_e[:, 0:n, :], src_e[:, 0:n, :], d_all(n)[:, :, KW:GW], ALU.mult)),
                    v(lambda e: e.tensor_reduce(cw[:, 2, 0:n], src_e[:, 0:n, :], AX.X, ALU.add)),
                    v(lambda e: e.tensor_tensor(gate[:, 0:n, :], bank(5)[:, 0:n * H].rearrange("p (c h) -> p c h", h=H),
                                                cw[:, 2, 0:n].unsqueeze(2).broadcast_to([P, n, H]), ALU.add)),
                    v(lambda e: e.tensor_tensor(gate[:, 0:n, :], gate[:, 0:n, :], d_all(n)[:, :, 0:H], ALU.mult)),
                    v(lambda e: e.scalar_tensor_tensor(cw[:, 0, 0:n], rec[:, 0:n, F_W], -1.0, rec[:, 0:n, F_W], ALU.mult, ALU.max)),
                    v(lambda e: e.tensor_scalar(cw[:, 0, 0:n], cw[:, 0, 0:n], CUT, None, ALU.min)),
                    a(lambda e: e.activation(cw[:, 1, 0:n], cw[:, 0, 0:n], ACT.Sin, bias=half_pi[:, 0:1], scale=-2 * HALF_PI / CUT)),
                    v(lambda e: e.tensor_scalar(cw[:, 1, 0:n], cw[:, 1, 0:n], 0.5, 0.5, ALU.mult, ALU.add)),
                    v(lambda e: e.scalar_tensor_tensor(cw[:, 0, 0:n], rec[:, 0:n, F_W], CUT, cw[:, 1, 0:n], ALU.is_lt, ALU.mult)),
                    v(lambda e: e.tensor_tensor(val[:, 0:n, 0:H], gate[:, 0:n, :], cw[:, 0, 0:n].unsqueeze(2).broadcast_to([P, n, H]), ALU.mult)),
                    v(lambda e: e.tensor_copy(val[:, 0:n, H:KW], d_all(n)[:, :, H:KW])),
                    a(lambda e: e.copy(os32[:, 0:n, :], ohg[:, 2, 0:n, :])),
                    scatter(n, os32, val, bank(6)[:, 0:KW]),
                    v(lambda e: e.tensor_tensor(ACC[:, ds(bs, 1), :], ACC[:, ds(bs, 1), :], bank(6)[:, 0:KW].unsqueeze(1), ALU.add)),
                ]

            def degrees(n, bd):
                return [
                    t(many([lambda e, c=c: e.matmul(bank(7)[:, c:c + 1], oh_d[:, c, :], ones8[:, :], start=True, stop=True) for c in range(n)])),
                    v(lambda e: e.tensor_tensor(DEG[:, bd_of(bd, 0, n)], DEG[:, bd_of(bd, 0, n)], bank(7)[:, 0:n], ALU.add)),
                ]

            def adjacency(ohg, bs, g):
                return [
                    t(many([lambda e, c=c: e.matmul(bank(0, 2)[:, c * P:(c + 1) * P], ohg[:, 2, c, :], oh_d[:, c, :], start=True, stop=True) for c in range(GC)])),
                    a(lambda e: e.copy(adj_out[:, :, :], bank(0, 2)[:, 0:GC * P].rearrange("p (c e) -> p c e", c=GC))),
                    sy(lambda e: e.dma_start(ADJ[ds(bs, 1), :, g * GC * P:(g + 1) * GC * P].rearrange("o p w -> (o p) w"),
                                             adj_out[:, :, :].rearrange("p c e -> p (c e)"))),
                    sy(lambda e: e.dma_start(OHD[ds(bs, 1), g, :, :].rearrange("o p w -> (o p) w"), ohg.rearrange("p k c e -> p (k c e)").bitcast(F32))),
                ]

            def load_rec(bs, g):
                return sy(lambda e: e.dma_start(rec[:, :, :].rearrange("p c w -> p (c w)"),
                                                rec_rows[ds(bs, 1), :, g * GC * RW:(g + 1) * GC * RW].rearrange("o p w -> (o p) w")))

            def extra_chunks(body):
                barrier()
                n = extra_count()
                with e.If(n > 0):
                    with e.Fori(0, n) as j:
                        in_turn([sy(lambda e: e.dma_start(rec[:, 0, :], rec_extra[ds(j, 1), :, :].rearrange("o p w -> (o p) w")))])
                        in_turn_end()
                        bs = e.value_load(rec[0:1, 0, F_BS:F_BS + 1].bitcast(I32), min_val=0, max_val=NB - 1)
                        bd = e.value_load(rec[0:1, 0, F_BD:F_BD + 1].bitcast(I32), min_val=0, max_val=NB - 1)
                        in_turn([(who, lambda e: e.drain(), 1) for who in ENGINES])
                        in_turn(body(bs, bd))
                    in_turn_end()
                barrier()

            def gate_pass():
                barrier()
                with e.Fori(0, NB) as bs:
                    in_turn([stage_src(bs, G)])
                    for g in range(NG):
                        ohg = oh[:, g]
                        in_turn([load_rec(bs, g), *build_one_hots(GC, ohg), *adjacency(ohg, bs, g), *degrees(GC, g * GC), *gate_values(GC, ohg, bs, g * GC)])
                in_turn_end()
                extra_chunks(lambda bs, bd: [stage_src(bs, G), stage_dst(bd, GW), *build_one_hots(1, oh[:, 0]), *degrees(1, bd), *gate_values(1, oh[:, 0], bs, bd)])

            def scores(n, ohg, bs, bd, to):
                return [
                    gather(n, d_spot, ohg[:, 1], dst_rows(bd), DW),
                    gather(n, q_spot, ohg[:, 0], src_rows, KW),
                    v(lambda e: e.scalar_tensor_tensor(xk[:, 0:n, 0:RBF], rec[:, 0:n, 0:RBF], 0.1, d_all(n)[:, :, 0:RBF], ALU.mult, ALU.add)),
                    v(lambda e: e.tensor_copy(xk[:, 0:n, RBF:KW], d_all(n)[:, :, RBF:KW])),
                    v(lambda e: e.tensor_tensor(xk[:, 0:n, :], xk[:, 0:n, :], q_all(n), ALU.mult)),
                    v(lambda e: e.tensor_reduce(to, xk[:, 0:n, :], AX.X, ALU.add)),
                ]

            def running_max(n, hots, score):
                return [a(lambda e: e.activation(os32[:, 0:n, :], hots[:, 0:n, :], ACT.Copy, bias=-BIG, scale=BIG))] + [
                    v(lambda e, c=c: e.scalar_tensor_tensor(runmax[:, :], os32[:, c, :], score(c), runmax[:, :], ALU.add, ALU.max)) for c in range(n)]

            def row_max(bs):
                return [
                    t(lambda e: e.transpose(bank(6)[:, 0:P], runmax[:, :], ident[:, :])),
                    v(lambda e: e.tensor_reduce(rowmax[:, 0:1], bank(6)[:, 0:P], AX.X, ALU.max)),
                    v(lambda e: e.tensor_tensor(SMAX[:, ds(bs, 1)], SMAX[:, ds(bs, 1)], rowmax[:, 0:1], ALU.max)),
                ]

            def weights(n, hot, bs, score, es):
                r = rowmax
                return [
                    v(lambda e: e.tensor_copy(r[:, 0:1], SMAX[:, ds(bs, 1)])),
                    v(lambda e: e.tensor_copy(smax3[:, 0:1], r[:, 0:1])),
                    v(lambda e: e.tensor_tensor(r[:, 1:2], r[:, 0:1], smax3[:, 0:1], ALU.subtract)),
                    v(lambda e: e.tensor_copy(smax3[:, 1:2], r[:, 1:2])),
                    v(lambda e: e.tensor_tensor(smax3[:, 2:3], r[:, 1:2], smax3[:, 1:2], ALU.subtract)),
                    t(many([lambda e, c=c: e.matmul(bank(6)[:, 3 * c:3 * c + 3], hot(c), smax3[:, :], start=True, stop=True) for c in range(n)])),
                    v(lambda e: e.tensor_reduce(es[:, 0, 0:n], bank(6)[:, 0:3 * n].rearrange("p (c k) -> p c k", k=3), AX.X, ALU.add)),
                    v(lambda e: e.tensor_tensor(es[:, 0, 0:n], score, es[:, 0, 0:n], ALU.subtract)),
                    v(lambda e: e.tensor_scalar(es[:, 0, 0:n], es[:, 0, 0:n], 20.0, None, ALU.min)),
                    a(lambda e: e.activation(es[:, 1, 0:n], es[:, 0, 0:n], ACT.Exp)),
                ]

            def extra_max(bs, bd):
                return [stage_src(bs), stage_dst(bd), *build_one_hots(1, oh[:, 0]), *scores(1, oh[:, 0], bs, bd, S[:, 0:1]),
                        v(lambda e: e.memset(runmax[:, :], -BIG)),
                        *running_max(1, oh[:, 0, 2], lambda c: S[:, 0:1]), *row_max(bs)]

            def extra_sum(bs, bd):
                return [stage_src(bs), stage_dst(bd), *build_one_hots(1, oh[:, 0]), *scores(1, oh[:, 0], bs, bd, S[:, 0:1]),
                        *weights(1, lambda c: oh[:, 0, 0, 0, :], bs, S[:, 0:1], ES[:, :, :]),
                        v(lambda e: e.tensor_scalar(VAL[:, 0, 0:H], d_spot(0)[:, KW:DW], ES[:, 1, 0:1], None, ALU.mult)),
                        v(lambda e: e.tensor_copy(VAL[:, 0, H:KW], ES[:, 1, 0:1])),
                        a(lambda e: e.copy(os32[:, 0, :], oh[:, 0, 2, 0, :])),
                        scatter(1, os32, VAL, bank(7)[:, 0:KW]),
                        v(lambda e: e.tensor_tensor(ACC[:, ds(bs, 1), :], ACC[:, ds(bs, 1), :], bank(7)[:, 0:KW].unsqueeze(1), ALU.add))]

            def attention_pass():
                extra_chunks(extra_max)
                with e.Fori(0, NB) as bs:
                    in_turn([v(lambda e: e.memset(runmax[:, :], -BIG)), stage_src(bs)])
                    for g in range(NG):
                        ohg = oh[:, g]
                        c0 = g * GC
                        in_turn([
                            load_rec(bs, g),
                            sy(lambda e, ohg=ohg, g=g: e.dma_start(ohg.rearrange("p k c e -> p (k c e)").bitcast(F32), OHD[ds(bs, 1), g, :, :].rearrange("o p w -> (o p) w"))),
                            *scores(GC, ohg, bs, c0, S[:, c0:c0 + GC]),
                            a(lambda e, c0=c0: e.copy(HE[:, c0:c0 + GC, :], d_all(GC)[:, :, KW:DW])),
                            *running_max(GC, ohg[:, 2], lambda c, c0=c0: S[:, c0 + c:c0 + c + 1]),
                        ])
                    in_turn([
                        *row_max(bs),
                        *weights(NB, lambda c: oh[:, c // GC, 0, c % GC, :], bs, S[:, :], ES[:, :, :]),
                        v(lambda e: e.tensor_tensor(VAL[:, :, 0:H], HE[:, :, :], ES[:, 1, :].unsqueeze(2).broadcast_to([P, NB, H]), ALU.mult)),
                        v(lambda e: e.tensor_copy(VAL[:, :, H:KW], ES[:, 1, :].unsqueeze(2))),
                    ])
                    for g in range(NG):
                        in_turn([
                            a(lambda e, g=g: e.copy(os32[:, :, :], oh[:, g, 2, :, :])),
                            t(many([lambda e, g=g, c=c: e.matmul(bank(7)[:, 0:KW], os32[:, c, :], VAL[:, g * GC + c, :],
                                                                 start=g + c == 0, stop=g * GC + c == NB - 1) for c in range(GC)])),
                        ])
                    in_turn([v(lambda e: e.tensor_tensor(ACC[:, ds(bs, 1), :], ACC[:, ds(bs, 1), :], bank(7)[:, 0:KW].unsqueeze(1), ALU.add))])
                in_turn_end()
                extra_chunks(extra_sum)

            def spread_setup():
                serial([
                    v(lambda e: e.tensor_tensor(X[:, :, :], X[:, :, :], HN[:, :, :], ALU.add)),
                    *normalise(HN[:, :, :], X[:, :, :], mm[:, :, :]),
                    v(lambda e: e.tensor_scalar(HN[:, :, :], HN[:, :, :], 0.0, None, ALU.max)),
                    a(lambda e: e.activation(STAT[:, 0, :], DEG[:, :], ACT.Sqrt)),
                    v(lambda e: e.reciprocal(dinv[:, :], STAT[:, 0, :])),
                    v(lambda e: e.tensor_tensor(g_f[:, :, :], HN[:, :, :], wide(dinv[:, :]), ALU.mult)),
                ])

            tiles = [(b, min(4, NB - b)) for b in range(0, NB, 4)]

            def spread_extra(bs, bd):
                hot = lambda to, f: v(lambda e: e.tensor_tensor(to[:, :], iota_f[:, :], rec_l[:, f:f + 1].broadcast_to([P, P]), ALU.is_equal))
                return [
                    hot(ohs_l, F_SRC), hot(ohd_l, F_DST),
                    t(lambda e: e.transpose(bank(4)[:, 0:P], ohs_l[:, :], ident[:, :])),
                    a(lambda e: e.copy(ohsT_l[:, :], bank(4)[:, 0:P])),
                    v(lambda e: e.tensor_copy(val_l[:, :], g_f[:, ds(bs, 1), :].rearrange("p o h -> p (o h)"))),
                    t(lambda e: e.matmul(bank(5)[:, 0:H], ohsT_l[:, :], val_l[:, :], start=True, stop=True)),
                    a(lambda e: e.copy(val_l[:, :], bank(5)[:, 0:H])),
                    t(lambda e: e.matmul(bank(6)[:, 0:H], ohd_l[:, :], val_l[:, :], start=True, stop=True)),
                    v(lambda e: e.tensor_tensor(mm[:, ds(bd, 1), :], mm[:, ds(bd, 1), :], bank(6)[:, 0:H].unsqueeze(1), ALU.add)),
                ]

            def spread_extra_chunks():
                barrier()
                n = extra_count()
                with e.If(n > 0):
                    with e.Fori(0, n) as j:
                        in_turn([sy(lambda e: e.dma_start(rec_l[:, :], rec_extra[ds(j, 1), :, :].rearrange("o p w -> (o p) w")))])
                        in_turn_end()
                        bs = e.value_load(rec_l[0:1, F_BS:F_BS + 1].bitcast(I32), min_val=0, max_val=NB - 1)
                        bd = e.value_load(rec_l[0:1, F_BD:F_BD + 1].bitcast(I32), min_val=0, max_val=NB - 1)
                        in_turn([(who, lambda e: e.drain(), 1) for who in ENGINES])
                        in_turn(spread_extra(bs, bd))
                    in_turn_end()
                barrier()

            def spread_step(k):
                serial(split([g3[:, :, j, :] for j in range(3)], g_f[:, :, :], g_r[:, :, :]))
                barrier()
                for i, (b0, nb) in enumerate(tiles):
                    n = k * len(tiles) + i
                    if name == "sync":
                        if n >= 2:
                            e.wait_ge(s_apes, n - 1)
                        e.dma_start(AJ[:, n % 2, :, 0:nb * P], adj_groups[:, :, b0 * P:(b0 + nb) * P]).then_inc(s_aload[n % 2], 16)
                    if name == "tensor":
                        e.wait_ge(s_aload[n % 2], 16 * (n // 2 + 1))
                        if n >= 2:
                            e.wait_ge(s_afold, n - 1)
                        for c in range(nb):
                            spot = bank(2 * (n % 2), 2)[:, c * 256:c * 256 + 3 * H]
                            for bs in range(NB):
                                last = e.matmul(spot, AJ[:, n % 2, bs, c * P:(c + 1) * P], g3[:, bs, :, :].rearrange("p k h -> p (k h)"),
                                                start=bs == 0, stop=bs == NB - 1)
                        last.then_inc(s_apes, 1)
                    if name == "vector":
                        e.wait_ge(s_apes, n + 1)
                        spots = bank(2 * (n % 2), 2).rearrange("p (c w) -> p c w", w=256)[:, 0:nb, 0:3 * H]
                        e.tensor_reduce(mm[:, b0:b0 + nb, :], spots.rearrange("p c (k h) -> p c h k", k=3), AX.X, ALU.add).then_inc(s_afold, 1)
                spread_extra_chunks()
                serial([
                    v(lambda e: e.tensor_tensor(mm[:, :, :], mm[:, :, :], g_f[:, :, :], ALU.add)),
                    v(lambda e: e.tensor_tensor(mm[:, :, :], mm[:, :, :], wide(dinv[:, :]), ALU.mult)),
                    v(lambda e: e.tensor_scalar(mm[:, :, :], mm[:, :, :], 1.0 - ALPHA, None, ALU.mult)),
                    v(lambda e: e.scalar_tensor_tensor(mm[:, :, :], HN[:, :, :], ALPHA, mm[:, :, :], ALU.mult, ALU.add)),
                    v(lambda e: e.tensor_tensor(g_f[:, :, :], mm[:, :, :], wide(dinv[:, :]), ALU.mult)),
                ])

            def store():
                serial([
                    v(lambda e: e.tensor_tensor(X[:, :, :], X[:, :, :], mm[:, :, :], ALU.add)),
                    sy(lambda e: e.dma_start(out[0:(NB - 1) * P, :].rearrange("(b p) h -> p b h", p=P), X[:, 0:NB - 1, :])),
                    sy(lambda e: e.dma_start(out[(NB - 1) * P:N, :], X[0:TAIL, NB - 1, :])),
                ])

            load_all()
            count_cells()
            fill_extra()
            place_edges()
            if debug == "rec":
                serial([sy(lambda e: e.dma_start(out, REC[0:out.shape[0], :]))])
                e.wait_ge(order, count[0])
                return
            embed()
            first_tables()
            gate_pass()
            after_gate()
            if debug != "gate":
                for l in range(L):
                    layer_tables(l)
                    attention_pass()
                    layer_update(l)
                    if debug == "layer0":
                        break
            if debug in ("gate", "layer0"):
                serial([v(lambda e: e.tensor_copy(X[:, :, :], HN[:, :, :])), v(lambda e: e.memset(W1[:, :, :], 0.0))])
                serial([
                    sy(lambda e: e.dma_start(out[0:(NB - 1) * P, :].rearrange("(b p) h -> p b h", p=P), X[:, 0:NB - 1, :])),
                    sy(lambda e: e.dma_start(out[(NB - 1) * P:N, :], X[0:TAIL, NB - 1, :])),
                ])
                e.wait_ge(order, count[0])
                return
            spread_setup()
            for k in range(KSTEP):
                spread_step(k)
            store()
            e.wait_ge(order, count[0])

        block.sync(lambda e: program("sync", e))
        block.tensor(lambda e: program("tensor", e))
        block.vector(lambda e: program("vector", e))
        block.scalar(lambda e: program("scalar", e))
        block.gpsimd(lambda e: program("gpsimd", e))


def kernel(x, src, dst, edge_attr_40, edge_weight, node_type_119, node_vec, L0_gnn_Wq, L0_gnn_gq, L0_gnn_bq, L0_gnn_Wk,
           L0_gnn_gk, L0_gnn_bk, L0_gnn_Wm, L0_gnn_Wu, L0_gnn_go, L0_gnn_bo, L0_gnn_F1W, L0_gnn_F1b, L0_gnn_F2W,
           L0_gnn_F2b, L0_gnn_gn, L0_gnn_bn, L0_gnn_emb, L0_gnn_adapt):
    import numpy as np
    from concourse import bacc
    from concourse.bass_utils import run_bass_kernel_spmd

    arrays = {
        "x": x, "src": src, "dst": dst, "edge_attr_40": edge_attr_40, "edge_weight": edge_weight,
        "node_type_119": node_type_119, "node_vec": node_vec, "Wq": L0_gnn_Wq, "gq": L0_gnn_gq, "bq": L0_gnn_bq,
        "Wk": L0_gnn_Wk, "gk": L0_gnn_gk, "bk": L0_gnn_bk, "Wm": L0_gnn_Wm, "Wu": L0_gnn_Wu, "go": L0_gnn_go,
        "bo": L0_gnn_bo, "F1W": L0_gnn_F1W, "F1b": L0_gnn_F1b, "F2W": L0_gnn_F2W, "F2b": L0_gnn_F2b, "gn": L0_gnn_gn,
        "bn": L0_gnn_bn, "emb": L0_gnn_emb, "adapt": L0_gnn_adapt,
    }
    arrays = {name: np.ascontiguousarray(a) for name, a in arrays.items()}
    nc = bacc.Bacc("TRN2", target_bir_lowering=False, num_devices=1)
    args = {name: nc.dram_tensor(f"in_{name}", a.shape, mybir.dt.from_np(a.dtype), kind="ExternalInput").ap()
            for name, a in arrays.items()}
    out = nc.dram_tensor("out", (N, H), F32, kind="ExternalOutput").ap()
    build(nc, out=out, **args)
    result = run_bass_kernel_spmd(nc, [{f"in_{name}": a for name, a in arrays.items()}], core_ids=[0])
    return result.results[0]["out"]
```

```python
from contextlib import ExitStack

import concourse.bass as bass
from concourse import mybir

F32, BF16, FP8, I32 = mybir.dt.float32, mybir.dt.bfloat16, mybir.dt.float8e4, mybir.dt.int32
ALU, ACT, AX = mybir.AluOpType, mybir.ActivationFunctionType, mybir.AxisListType
ds = bass.ds

N, E, H, RBF, L, G, NELEM = 6250, 200000, 48, 40, 4, 32, 119
CUT, KSTEP, ALPHA = 6.0, 5, 0.8
P = 128
NB = -(-N // P)
TAIL = N - (NB - 1) * P
NPAD = NB * P
CAP = P
EP = 125
ET = E // EP
NS = 8
SC = ET // NS
JB = 10
CELLS = NB * NB
GRID = CELLS * P
NOV = E // P
F_SRC, F_DST, F_W, F_BS, F_BD, RW = 40, 41, 42, 43, 44, 45
GC = 7
NG = NB // GC
KW = H + 1
DW = 2 * H + 1
GW = H + 1 + G
BIG = 1e30
HALF_PI = 1.5707963267948966
ENGINES = ("sync", "tensor", "vector", "scalar", "gpsimd")


def build(nc, x, src, dst, edge_attr_40, edge_weight, node_type_119, node_vec, Wq, gq, bq, Wk, gk, bk, Wm, Wu, go,
          bo, F1W, F1b, F2W, F2b, gn, bn, emb, adapt, out, debug=None):
    REC = nc.dram_tensor("edge_records", (GRID + NOV * P, RW), F32)
    OHD = nc.dram_tensor("one_hots", (NB, NG, P, 3 * GC * P // 4), F32)
    ADJ = nc.dram_tensor("adjacency", (NB, P, NB * P), BF16)
    rec_rows = REC[0:GRID, :].rearrange("(b p c) w -> b p (c w)", p=P, c=NB)
    rec_extra = REC[GRID:GRID + NOV * P, :].rearrange("(j p) w -> j p w", p=P)
    adj_groups = ADJ[:, :, :].rearrange("b s e -> s b e")

    ctx = ExitStack()
    with ctx:
        def sem(name):
            return ctx.enter_context(nc.semaphore(name))

        order, turn, absorb = sem("order"), sem("turn"), sem("absorb")
        s_load, s_edges, s_pe, s_dve, s_rank, s_idx = (sem(n) for n in
            ("prep_load", "edge_loads", "prep_pe", "prep_dve", "rank_done", "slots_done"))
        s_asm = sem("records_assembled")
        s_scat = [sem(f"records_scattered_{k}") for k in range(10)]
        s_hpe, s_hdve = sem("hist_pe"), sem("hist_dve")
        s_aload = [sem(f"adj_loaded_{k}") for k in range(2)]
        s_apes, s_afold = sem("adj_multiplied"), sem("adj_folded")

        class Rows:

            def __init__(self, name, each, owner):
                self.sem, self.each, self.owner = sem(name), each, owner

        gathered = Rows("cells_gathered", NG, "tensor")
        flipped = Rows("maxima_flipped", 1, "tensor")
        max_gathered = Rows("maxima_gathered", 1, "tensor")
        summed = Rows("cells_summed", NG, "tensor")
        dve_link = Rows("dve_link", 2 * NG, "vector")
        multiplied = Rows("scores_multiplied", NG, "vector")
        maxed = Rows("cells_maxed", NG, "vector")
        combined = Rows("maxima_combined", 1, "vector")
        row_maxed = Rows("row_maximum", 2, "vector")
        folded = Rows("maxima_folded", 1, "vector")
        added = Rows("row_added", 1, "vector")
        carried = Rows("features_carried", NG, "scalar")
        masked = Rows("masks_ready", NG, "scalar")
        raised = Rows("weights_raised", 1, "scalar")
        staged = Rows("source_rows_staged", 1, "gpsimd")
        parted = Rows("maxima_parted", 4, "gpsimd")
        bounded = Rows("scores_bounded", 2, "gpsimd")
        scaled = Rows("values_scaled", NG, "gpsimd")
        less_high = Rows("values_less_high", NG, "gpsimd")
        high_part = Rows("high_parts", NG, "scalar")
        middle_part = Rows("middle_parts", NG, "scalar")
        weighted = Rows("values_weighted", NG, "gpsimd")
        all_rows = [gathered, flipped, max_gathered, summed, dve_link, multiplied, maxed, combined, row_maxed, folded,
                    added, carried, masked, raised, staged, parted, bounded, scaled, less_high, high_part, middle_part, weighted]
        s_cells = [[sem(f"cells_loaded_{p}_{g}") for g in range(NG)] for p in range(2)]

        def scope():
            return ExitStack()

        def sb(stack, name, shape, dt=F32):
            return stack.enter_context(nc.sbuf_tensor(name, shape, dt))

        X = sb(ctx, "X", [P, NB, H])
        HN = sb(ctx, "HN", [P, NB, H])
        ACC = sb(ctx, "ACC", [P, NB, KW])
        SMAX = sb(ctx, "SMAX", [P, NB])
        DEG = sb(ctx, "DEG", [P, NB])
        MULT = sb(ctx, "MULT", [P, NB])
        LOGM = sb(ctx, "LOGM", [P, NB])
        STAT = sb(ctx, "STAT", [P, 4, NB])
        iota_f = sb(ctx, "iota_f", [P, P])
        iota_i = sb(ctx, "iota_i", [P, P], I32)
        part_f = sb(ctx, "part_f", [P, 1])
        part_i = sb(ctx, "part_i", [P, 1], I32)
        ident = sb(ctx, "ident", [P, P])
        ident8 = sb(ctx, "ident8", [P, P], FP8)
        ones8 = sb(ctx, "ones8", [P, 1], FP8)
        ones_row = sb(ctx, "ones_row", [1, P])
        half_pi = sb(ctx, "half_pi", [P, 1])
        zero1 = sb(ctx, "zero1", [P, 1])
        LP = sb(ctx, "LP", [P, 6, L, H])
        GN = sb(ctx, "GN", [P, 2, H])
        WQK = sb(ctx, "WQK", [H, L, 2 * H])
        WM = sb(ctx, "WM", [H, L, H])
        WU = sb(ctx, "WU", [H, L, 2, H])
        F1 = sb(ctx, "F1", [RBF, H])
        F1B = sb(ctx, "F1B", [H, 1])
        F2 = sb(ctx, "F2", [H, H])
        F2B = sb(ctx, "F2B", [1, H])
        n_extra = sb(ctx, "n_extra", [1, 1], I32)

        psum = ctx.enter_context(nc.psum_tensor("psum", [P, 8 * 512], F32))

        def bank(b, n=1):
            return psum[:, b * 512:(b + n) * 512]

        with scope() as st:
            src_i, dst_i = sb(st, "src_i", [EP, ET], I32), sb(st, "dst_i", [EP, ET], I32)
            tmp_i = sb(st, "tmp_i", [EP, ET], I32)
            fields = sb(st, "fields", [EP, ET, RW - RBF])
            bs_f, bd_f, key_f = (sb(st, n, [EP, ET]) for n in ("bs_f", "bd_f", "key_f"))
            home = sb(st, "home", [EP, ET])
            hist = sb(st, "hist", [NB, NS, NB])
            base = sb(st, "base", [NB, NS, 2, NB])
            cell = sb(st, "cell", [NB, 6, NB])
            cell_i = sb(st, "cell_i", [NB, 2, NB], I32)
            one_bs, one_bd = sb(st, "one_bs", [EP, 2, NS, NB], BF16), sb(st, "one_bd", [EP, 2, NS, NB], BF16)
            one_bd32 = sb(st, "one_bd32", [EP, NS, NB])
            one_bsT = sb(st, "one_bsT", [NB, NS, EP])
            lower = sb(st, "lower", [EP, EP])
            upper = sb(st, "upper", [NB, NB])
            ones49 = sb(st, "ones49", [NB, NB])
            junk = sb(st, "junk", [EP, NS, EP])
            look = sb(st, "look", [EP, NS, 2, NB])
            found = sb(st, "found", [EP, NS, 2])
            rank = sb(st, "rank", [EP, NS])
            slot_a, slot_b, slot_m = (sb(st, n, [EP, NS]) for n in ("slot_a", "slot_b", "slot_m"))
            slot_i = sb(st, "slot_i", [EP, 4, NS], I32)
            attr_in = sb(st, "attr_in", [EP, NS, JB, RBF])
            rec_out = sb(st, "rec_out", [EP, 2, NS, 5, RW])
            zeros = sb(st, "zeros", [P, NB * RW])
        ze_tab = sb(ctx, "ze_tab", [P, NB, 2 * G])
        with scope() as st:
            z_row = sb(st, "z_row", [NELEM, NPAD], I32)
            z_hot = sb(st, "z_hot", [NELEM, NPAD])
            EMB = sb(st, "EMB", [NELEM, 2 * G])
            embT = sb(st, "embT", [G, NELEM])
            adapt_sb = sb(st, "adapt_sb", [G, G])
        with scope() as st:
            TD = sb(st, "TD", [P, 3, NB, DW], BF16)
            TS = sb(st, "TS", [P, 3, NB, KW], BF16)
            with scope() as s2:
                HT = sb(s2, "HT", [H, NPAD])
                AT = sb(s2, "AT", [H, NPAD])
                W1 = sb(s2, "W1", [P, NB, DW])
                W2 = sb(s2, "W2", [P, NB, DW])
            with scope() as s2:
                rec = sb(s2, "rec", [P, GC, RW])
                td_row = sb(s2, "td_row", [P, 3, DW], BF16)
                ts_row = sb(s2, "ts_row", [P, 3, KW], BF16)
                oh = sb(s2, "oh", [P, NG, 3, GC, P], FP8)
                oh_d = sb(s2, "oh_d", [P, GC, P], FP8)
                os32 = sb(s2, "os32", [P, GC, P])
                adj_out = sb(s2, "adj_out", [P, GC, P], BF16)
                attrT = sb(s2, "attrT", [RBF, GC * P])
                act1 = sb(s2, "act1", [H, GC * P])
                src_e = sb(s2, "src_e", [P, GC, G])
                gate = sb(s2, "gate", [P, GC, H])
                cw = sb(s2, "cw", [P, 3, GC])
                val = sb(s2, "val", [P, GC, KW])
                xk = sb(s2, "xk", [P, GC, KW])
                runmax = sb(s2, "runmax", [P, P])
                rowmax = sb(s2, "rowmax", [P, 4])
                smax3 = sb(s2, "smax3", [P, 3], BF16)
                S1 = sb(s2, "S1", [P, 1])
                ES = sb(s2, "ES", [P, 2, 1])
                V1 = sb(s2, "V1", [P, 1, KW])
            with scope() as s2:
                cells = sb(s2, "cells", [P, 2, NG, 3, GC, P], FP8)
                recs = sb(s2, "recs", [P, 2, NG, GC, RW])
                values = sb(s2, "values", [P, 2, NB, KW])
                mask = sb(s2, "mask", [P, 2, GC, P])
                values3 = sb(s2, "values3", [P, NB, 3, KW], BF16)
                xks = sb(s2, "xks", [P, 2, GC, KW])
                score = sb(s2, "score", [P, 2, NB])
                slot_max = sb(s2, "slot_max", [P, GC, P])
                slot_top = sb(s2, "slot_top", [P, P])
                row_sum = sb(s2, "row_sum", [P, KW])
                top = sb(s2, "top", [P, 4])
                top3 = sb(s2, "top3", [P, 3], BF16)
                edge_top = sb(s2, "edge_top", [P, 3, NB])
                ts2 = sb(s2, "ts2", [P, 2, 3, KW], BF16)
        with scope() as st:
            AJ = sb(st, "AJ", [P, 2, NB, 4 * P], BF16)
            dinv = sb(st, "dinv", [P, NB])
            g_f = sb(st, "g_f", [P, NB, H])
            g_r = sb(st, "g_r", [P, NB, H])
            g3 = sb(st, "g3", [P, NB, 3, H], BF16)
            mm = sb(st, "mm", [P, NB, H])
            rec_l = sb(st, "rec_l", [P, RW])
            ohs_l, ohd_l, ohsT_l = (sb(st, n, [P, P]) for n in ("ohs_l", "ohd_l", "ohsT_l"))
            val_l = sb(st, "val_l", [P, H])

        block = ctx.enter_context(nc.Block())

        def program(name, e):
            count = [0]

            def serial(steps, wait_last=False):
                for who, fn, inc in steps:
                    if who == name:
                        e.wait_ge(order, count[0])
                        fn(e).then_inc(order, inc)
                    count[0] += inc

            def barrier():
                for who in ENGINES:
                    if who == name:
                        e.wait_ge(order, count[0])
                        e.drain().then_inc(order, 1)
                    count[0] += 1
                e.wait_ge(order, count[0])

            turns = e.alloc_register("turns_" + name)
            e.reg_mov(turns, 1)
            if name == "sync":
                e.sem_inc(turn, 1)

            row = e.alloc_register("row_" + name)
            e.reg_mov(row, 2)
            loads = [e.alloc_register(f"loads_{k}_{name}") for k in range(2)]
            for k in range(2):
                e.reg_mov(loads[k], 0)
            for r in all_rows:
                if r.owner == name:
                    e.sem_inc(r.sem, 2 * r.each)

            def of_row(what, c, back=0, plain=True):
                e.wait_ge(what.sem, e.snap(row, min_val=2, max_val=1 << 20) * what.each + (c - back * what.each))
                if plain:
                    e.sem_inc(absorb, 1)

            def in_turn(steps):
                off = 0
                for who, fn, inc in steps:
                    if who == name:
                        e.wait_ge(turn, e.snap(turns, min_val=1, max_val=1 << 29) + off)
                        e.sem_inc(absorb, 1)
                        fn(e).then_inc(turn, inc)
                    off += inc
                e.reg_add(turns, turns, off)

            def in_turn_end():
                e.wait_ge(turn, e.snap(turns, min_val=1, max_val=1 << 29))
                e.sem_inc(absorb, 1)

            def sy(fn): return ("sync", fn, 16)
            def po(fn): return ("gpsimd", fn, 1)
            def v(fn): return ("vector", fn, 1)
            def a(fn): return ("scalar", fn, 1)
            def t(fn): return ("tensor", fn, 1)

            def many(fns):
                def run(e):
                    for f in fns:
                        last = f(e)
                    return last
                return run

            def bc(ap, shape):
                return ap.broadcast_to(shape)

            def load_all():
                flat = lambda w: w.rearrange("l h -> (l h)").partition_broadcast(P)
                vec = lambda w: w.partition_broadcast(P)
                col = lambda w: w.rearrange("(h o) -> h o", o=1)
                x_main = x[0:(NB - 1) * P, :].rearrange("(b p) h -> p b h", p=P)
                steps = [
                    v(lambda e: e.memset(X[:, :, :], 0.0)),
                    v(lambda e: e.memset(MULT[:, :], 1.0)),
                    sy(lambda e: e.dma_start(X[:, 0:NB - 1, :], x_main)),
                    sy(lambda e: e.dma_start(X[0:TAIL, NB - 1, :], x[(NB - 1) * P:N, :])),
                    sy(lambda e: e.dma_start(MULT[0:TAIL, NB - 1:NB], node_vec[(NB - 1) * P:N].rearrange("(p o) -> p o", o=1))),
                ]
                def mult_main(e):
                    with nc.allow_non_contiguous_dma(reason="one column of node values per block"):
                        return e.dma_start(MULT[:, 0:NB - 1], node_vec[0:(NB - 1) * P].rearrange("(b p) -> p b", p=P))
                steps.append(sy(mult_main))
                for n, w in enumerate((gq, bq, gk, bk, go, bo)):
                    steps.append(sy(lambda e, n=n, w=w: e.dma_start(LP[:, n, :, :].rearrange("p l h -> p (l h)"), flat(w))))
                steps += [
                    sy(lambda e: e.dma_start(GN[:, 0, :], vec(gn))), sy(lambda e: e.dma_start(GN[:, 1, :], vec(bn))),
                    sy(lambda e: e.dma_start(WQK[:, :, 0:H], Wq.rearrange("l i o -> i l o"))),
                    sy(lambda e: e.dma_start(WQK[:, :, H:2 * H], Wk.rearrange("l i o -> i l o"))),
                    sy(lambda e: e.dma_start(WM[:, :, :], Wm.rearrange("l i o -> i l o"))),
                    sy(lambda e: e.dma_start(WU[:, :, 0, :], Wu[:, 0:H, :].rearrange("l i o -> i l o"))),
                    sy(lambda e: e.dma_start(WU[:, :, 1, :], Wu[:, H:2 * H, :].rearrange("l i o -> i l o"))),
                    sy(lambda e: e.dma_start(F1[:, :], F1W)), sy(lambda e: e.dma_start(F2[:, :], F2W)),
                    sy(lambda e: e.dma_start(F1B[:, :], col(F1b))),
                    sy(lambda e: e.dma_start(F2B[:, :], F2b.rearrange("(o h) -> o h", o=1))),
                    po(lambda e: e.iota(iota_i[:, :], pattern=[[1, P]], base=1, channel_multiplier=0)),
                    po(lambda e: e.iota(part_i[:, :], pattern=[[0, 1]], base=0, channel_multiplier=1)),
                    v(lambda e: e.tensor_copy(iota_f[:, :], iota_i[:, :])),
                    v(lambda e: e.tensor_copy(part_f[:, :], part_i[:, :])),
                    v(lambda e: e.tensor_scalar(ident[:, :], iota_f[:, :], 1.0, part_f[:, 0:1], ALU.subtract, ALU.is_equal)),
                    v(lambda e: e.tensor_copy(ident8[:, :], ident[:, :], saturate=False)),
                    v(lambda e: e.tensor_copy(ones8[:, :], iota_f[:, 0:1], saturate=False)),
                    v(lambda e: e.memset(ones_row[:, :], 1.0)),
                    v(lambda e: e.memset(half_pi[:, :], HALF_PI)),
                    v(lambda e: e.memset(zero1[:, :], 0.0)),
                    v(lambda e: e.memset(DEG[:, :], 1.0)),
                ]
                serial(steps)

            def count_cells():
                serial([
                    v(lambda e: e.memset(zeros[:, :], 0.0)),
                    sy(lambda e: e.dma_start(src_i[:, :], src.rearrange("(p t) -> p t", t=ET))),
                    sy(lambda e: e.dma_start(dst_i[:, :], dst.rearrange("(p t) -> p t", t=ET))),
                    sy(lambda e: e.dma_start(home[:, :], edge_weight.rearrange("(p t) -> p t", t=ET))),
                    v(lambda e: e.tensor_copy(fields[:, :, 2], home[:, :])),
                ])
                for raw, local, block_f, fb in ((src_i, 0, bs_f, 3), (dst_i, 1, bd_f, 4)):
                    serial([
                        v(lambda e, raw=raw: e.tensor_scalar(tmp_i[:, :], raw[:, :], P - 1, None, ALU.bitwise_and)),
                        v(lambda e, local=local: e.tensor_scalar(fields[:, :, local], tmp_i[:, :], 1.0, None, ALU.add)),
                        v(lambda e, raw=raw: e.tensor_scalar(tmp_i[:, :], raw[:, :], 7, None, ALU.logical_shift_right)),
                        v(lambda e, block_f=block_f: e.tensor_copy(block_f[:, :], tmp_i[:, :])),
                        v(lambda e, fb=fb: e.tensor_copy(fields[:, :, fb].bitcast(I32), tmp_i[:, :])),
                    ])
                serial([
                    v(lambda e: e.scalar_tensor_tensor(key_f[:, :], bs_f[:, :], float(NB), bd_f[:, :], ALU.mult, ALU.add)),
                    v(lambda e: e.scalar_tensor_tensor(home[:, :], bs_f[:, :], float(NB * P), bd_f[:, :], ALU.mult, ALU.add)),
                    v(lambda e: e.tensor_scalar(lower[:, :], iota_f[0:EP, 0:EP], 1.0, part_f[0:EP, 0:1], ALU.subtract, ALU.is_lt)),
                    v(lambda e: e.tensor_scalar(upper[:, :], iota_f[0:NB, 0:NB], 1.0, part_f[0:NB, 0:1], ALU.subtract, ALU.is_gt)),
                    v(lambda e: e.memset(ones49[:, :], 1.0)),
                ])
                HG = NS
                groups = ET // HG
                iota49 = lambda n: iota_f[0:EP, 0:NB].unsqueeze(1).broadcast_to([EP, n, NB])
                if name == "vector":
                    e.tensor_scalar(iota_f[:, :], iota_f[:, :], 1.0, None, ALU.subtract).then_inc(s_hdve, 1)
                    e.wait_ge(s_hdve, 1)
                    for g in range(groups):
                        if g >= 2:
                            e.wait_ge(s_hpe, g - 1)
                        c0 = g * HG
                        e.tensor_tensor(one_bs[:, g % 2], iota49(HG), bs_f[:, c0:c0 + HG].unsqueeze(2).broadcast_to([EP, HG, NB]), ALU.is_equal)
                        e.tensor_tensor(one_bd[:, g % 2], iota49(HG), bd_f[:, c0:c0 + HG].unsqueeze(2).broadcast_to([EP, HG, NB]), ALU.is_equal).then_inc(s_hdve, 1)
                    e.wait_ge(s_hpe, groups)
                if name == "tensor":
                    for g in range(groups):
                        e.wait_ge(s_hdve, g + 2)
                        for k in range(HG):
                            c = g * HG + k
                            s, i = c // SC, c % SC
                            last = e.matmul(bank(0)[0:NB, s * NB:(s + 1) * NB], one_bs[:, g % 2, k, :], one_bd[:, g % 2, k, :],
                                            start=i == 0, stop=i == SC - 1)
                        last.then_inc(s_hpe, 1)
                tot, over, chunks, before = cell[:, 0], cell[:, 1], cell[:, 2], cell[:, 3]
                steps = [
                    v(lambda e: e.tensor_copy(hist[:, :, :], bank(0)[0:NB, 0:NS * NB].rearrange("p (s b) -> p s b", s=NS))),
                    v(lambda e: e.tensor_reduce(tot, hist[:, :, :].rearrange("p s b -> p b s"), AX.X, ALU.add)),
                    v(lambda e: e.tensor_scalar(over, tot, float(CAP), 0.0, ALU.subtract, ALU.max)),
                    v(lambda e: e.tensor_scalar(cell_i[:, 0], over, float(P - 1), None, ALU.add)),
                    v(lambda e: e.tensor_scalar(cell_i[:, 1], cell_i[:, 0], 7, None, ALU.logical_shift_right)),
                    v(lambda e: e.tensor_copy(chunks, cell_i[:, 1])),
                    v(lambda e: e.tensor_tensor_scan(before, chunks, chunks, 0.0, ALU.add, ALU.bypass)),
                    t(lambda e: e.matmul(bank(1)[0:NB, 0:1], upper[:, :], before[:, NB - 1:NB], start=True, stop=True)),
                    t(lambda e: e.matmul(bank(2)[0:NB, 0:1], ones49[:, :], before[:, NB - 1:NB], start=True, stop=True)),
                    v(lambda e: e.tensor_copy(n_extra[0:1, 0:1], bank(2)[0:1, 0:1])),
                    v(lambda e: e.tensor_tensor(before, before, chunks, ALU.subtract)),
                    v(lambda e: e.tensor_scalar(before, before, bank(1)[0:NB, 0:1], float(P), ALU.add, ALU.mult)),
                    v(lambda e: e.tensor_scalar(before, before, float(GRID - CAP), None, ALU.add)),
                    v(lambda e: e.memset(base[:, 0, 0, :], 0.0)),
                ]
                for s in range(NS):
                    steps.append(v(lambda e, s=s: e.tensor_copy(base[:, s, 1, :], before)))
                    if s:
                        steps.append(v(lambda e, s=s: e.tensor_tensor(base[:, s, 0, :], base[:, s - 1, 0, :], hist[:, s - 1, :], ALU.add)))
                for b in range(NB):
                    steps.append(sy(lambda e, b=b: e.dma_start(rec_rows[b], zeros[:, :])))
                serial(steps)

            def extra_count():
                e.wait_ge(order, count[0])
                e.sem_inc(absorb, 1)
                return e.value_load(n_extra[0:1, 0:1], min_val=0, max_val=NOV)

            def fill_extra():
                barrier()
                n = extra_count()
                with e.If(n > 0):
                    with e.Fori(0, n) as j:
                        in_turn([sy(lambda e: e.dma_start(rec_extra[ds(j, 1), :, :].rearrange("o p w -> (o p) w"), zeros[:, 0:RW]))])
                    in_turn_end()
                barrier()

            def place_edges():
                ITER = SC
                ident_e = ident[0:EP, 0:EP]
                attr = edge_attr_40.rearrange("(p s i) r -> p s (i r)", s=NS, i=SC)
                fields_s = fields[:, :, :].rearrange("p (s i) f -> p s i f", s=NS)
                by_stream = lambda arr: arr[:, :].rearrange("p (s i) -> p s i", s=NS)
                keyT, bsT, found_ps, hist_ps = bank(0, 2), bank(2, 2), bank(4, 2), bank(6)

                def scattered(i):
                    e.wait_ge(s_scat[i % 10], 16 * NS * (i // 10 + 1))

                at4 = lambda ps, s, w, tot=4: (s // 4) * 512 + (s % 4) * w
                if name == "sync":
                    for b in range(ITER // JB):
                        if b:
                            e.wait_ge(s_asm, 2 * b)
                        e.dma_start(attr_in[:, :, :, :].rearrange("p s i r -> p s (i r)"),
                                    attr[:, :, b * JB * RBF:(b + 1) * JB * RBF]).then_inc(s_edges, 16)
                if name == "scalar":
                    for b in range(ITER // JB):
                        e.wait_ge(s_edges, 16 * (b + 1))
                        for h in range(2):
                            n = 2 * b + h
                            if n >= 2:
                                for i in range(5 * (n - 2), 5 * (n - 1)):
                                    scattered(i)
                            for k in range(5):
                                j = 5 * h + k
                                e.copy(rec_out[:, n % 2, :, k, 0:RBF], attr_in[:, :, j, :])
                                last = e.copy(rec_out[:, n % 2, :, k, RBF:RW], fields_s[:, :, b * JB + j, :])
                            last.then_inc(s_asm, 1)
                if name == "tensor":
                    for i in range(ITER):
                        if i:
                            e.wait_ge(s_rank, i)
                        for s in range(NS):
                            o = at4(None, s, EP)
                            col = s * SC + i
                            e.transpose(keyT[0:EP, o:o + EP], key_f[:, col:col + 1].broadcast_to([EP, EP]), ident_e)
                            last = e.transpose(bsT[0:NB, o:o + EP], bs_f[:, col:col + 1].broadcast_to([EP, NB]), ident_e)
                        last.then_inc(s_pe, 1)
                        e.wait_ge(s_dve, 2 * i + 1)
                        for s in range(NS):
                            e.matmul(hist_ps[0:NB, s * NB:(s + 1) * NB], one_bs[:, i % 2, s, :], one_bd[:, i % 2, s, :], start=True, stop=True)
                        for s in range(NS):
                            o = at4(None, s, 2 * NB)
                            last = e.matmul(found_ps[0:EP, o:o + 2 * NB], one_bsT[:, s, :], base[:, s, :, :].rearrange("p a b -> p (a b)"), start=True, stop=True)
                        last.then_inc(s_pe, 1)
                if name == "vector":
                    iota49 = iota_f[0:EP, 0:NB].unsqueeze(1).broadcast_to([EP, NS, NB])
                    for i in range(ITER):
                        bsv = by_stream(bs_f)[:, :, i:i + 1].broadcast_to([EP, NS, NB])
                        bdv = by_stream(bd_f)[:, :, i:i + 1].broadcast_to([EP, NS, NB])
                        e.tensor_tensor(one_bs[:, i % 2], iota49, bsv, ALU.is_equal)
                        e.tensor_tensor(one_bd[:, i % 2], iota49, bdv, ALU.is_equal)
                        e.tensor_tensor(one_bd32[:, :, :], iota49, bdv, ALU.is_equal)
                        e.wait_ge(s_pe, 2 * i + 1)
                        for h in range(2):
                            last = e.tensor_scalar(one_bsT[:, 4 * h:4 * h + 4, :].rearrange("p s e -> p (s e)"), bsT[0:NB, h * 512:h * 512 + 4 * EP],
                                                   part_f[0:NB, 0:1], None, ALU.is_equal)
                        last.then_inc(s_dve, 1)
                        for s in range(NS):
                            o = at4(None, s, EP)
                            last = e.scalar_tensor_tensor(junk[:, s, :], keyT[0:EP, o:o + EP], key_f[:, s * SC + i:s * SC + i + 1], lower[:, :],
                                                          ALU.is_equal, ALU.mult, accum_out=rank[:, s:s + 1])
                        last.then_inc(s_rank, 1)
                        e.wait_ge(s_pe, 2 * i + 2)
                        for h in range(2):
                            e.tensor_tensor(look[:, 4 * h:4 * h + 4, :, :], found_ps[0:EP, h * 512:h * 512 + 8 * NB].rearrange("p (s a b) -> p s a b", s=4, a=2),
                                            one_bd32[:, 4 * h:4 * h + 4, :].unsqueeze(2).broadcast_to([EP, 4, 2, NB]), ALU.mult)
                        e.tensor_tensor(base[:, :, 0, :], base[:, :, 0, :], hist_ps[0:NB, 0:NS * NB].rearrange("p (s b) -> p s b", s=NS), ALU.add).then_inc(s_dve, 1)
                        e.wait_ge(s_dve, 2 * i + 2)
                        c = [0]
                        def link(ins):
                            c[0] += 1
                            ins.then_inc(s_load, 1)
                            e.wait_ge(s_load, 6 * i + c[0])
                        link(e.tensor_reduce(found[:, :, :], look[:, :, :, :], AX.X, ALU.add))
                        link(e.tensor_tensor(slot_m[:, :], rank[:, :], found[:, :, 0], ALU.add))
                        link(e.scalar_tensor_tensor(slot_a[:, :], slot_m[:, :], float(NB), by_stream(home)[:, :, i], ALU.mult, ALU.add))
                        link(e.tensor_tensor(slot_b[:, :], slot_m[:, :], found[:, :, 1], ALU.add))
                        link(e.tensor_tensor(slot_b[:, :], slot_b[:, :], slot_a[:, :], ALU.subtract))
                        link(e.scalar_tensor_tensor(slot_b[:, :], slot_m[:, :], float(CAP), slot_b[:, :], ALU.is_ge, ALU.mult))
                        if i >= 4:
                            scattered(i - 4)
                        e.tensor_tensor(slot_i[:, i % 4, :], slot_a[:, :], slot_b[:, :], ALU.add).then_inc(s_idx, 1)
                if name == "gpsimd":
                    for i in range(ITER):
                        e.wait_ge(s_idx, i + 1)
                        e.wait_ge(s_asm, i // 5 + 1)
                        for s in range(NS):
                            e.indirect_dma_start(REC[:, :], bass.IndirectOffsetOnAxis(ap=slot_i[:, i % 4, s:s + 1], axis=0),
                                                 rec_out[:, (i // 5) % 2, s, i % 5, :], None).then_inc(s_scat[i % 10], 16)
                    for i in range(ITER - 10, ITER):
                        scattered(i)
                barrier()
                serial([v(lambda e: e.tensor_scalar(iota_f[:, :], iota_f[:, :], 1.0, None, ALU.add))])

            def wide(ap, w=H):
                return ap.unsqueeze(2).broadcast_to([P, NB, w])

            def every(ap, w=H):
                return ap.unsqueeze(1).broadcast_to([P, NB, w])

            def normalise(to, of, tmp, g=None, b=None):
                mean, var = STAT[:, 0, :], STAT[:, 1, :]
                steps = [
                    v(lambda e: e.tensor_reduce(mean, of, AX.X, ALU.add)),
                    v(lambda e: e.tensor_scalar(mean, mean, 1.0 / H, None, ALU.mult)),
                    v(lambda e: e.tensor_tensor(to, of, wide(mean), ALU.subtract)),
                    v(lambda e: e.tensor_tensor(tmp, to, to, ALU.mult)),
                    v(lambda e: e.tensor_reduce(var, tmp, AX.X, ALU.add)),
                    v(lambda e: e.tensor_scalar(var, var, 1.0 / H, 1e-5, ALU.mult, ALU.add)),
                    a(lambda e: e.activation(mean, var, ACT.Sqrt)),
                    v(lambda e: e.reciprocal(var, mean)),
                    v(lambda e: e.tensor_tensor(to, to, wide(var), ALU.mult)),
                ]
                if g is not None:
                    steps += [v(lambda e: e.tensor_tensor(to, to, every(g), ALU.mult)),
                              v(lambda e: e.tensor_tensor(to, to, every(b), ALU.add))]
                return steps

            def split(parts, of, rest):
                return [
                    a(lambda e: e.copy(parts[0], of)),
                    v(lambda e: e.tensor_tensor(rest, of, parts[0], ALU.subtract)),
                    a(lambda e: e.copy(parts[1], rest)),
                    v(lambda e: e.tensor_tensor(parts[2], rest, parts[1], ALU.subtract)),
                ]

            def transposed(to, of):
                steps = []
                for b0 in range(0, NB, 16):
                    n = min(16, NB - b0)
                    steps += [
                        t(many([lambda e, b0=b0, k=k: e.transpose(bank(0, 4)[0:H, k * P:(k + 1) * P], of[:, b0 + k, 0:H], ident[:, :])
                                for k in range(n)])),
                        a(lambda e, b0=b0, n=n: e.copy(to[:, b0 * P:(b0 + n) * P], bank(0, 4)[0:H, 0:n * P])),
                    ]
                return steps

            def per_block(to, width, products):
                fit = 512 // width
                steps = []
                for b0 in range(0, NB, 8 * fit):
                    n = min(8 * fit, NB - b0)
                    spot = lambda k: bank(k // fit)[:, (k % fit) * width:(k % fit + 1) * width]
                    steps.append(t(many([
                        lambda e, b=b0 + k, k=k, m=m: e.matmul(spot(k), products[m][0](b), products[m][1], start=m == 0, stop=m == len(products) - 1)
                        for k in range(n) for m in range(len(products))])))
                    steps.append(a(many([
                        lambda e, b=b0 + j * fit, j=j, c=min(fit, n - j * fit):
                            e.copy(to[:, b:b + c, 0:width], bank(j)[:, 0:c * width].rearrange("p (b w) -> p b w", w=width))
                        for j in range(-(-n // fit))])))
                return steps

            def embed():
                cols = lambda b: z_hot[:, b * P:(b + 1) * P]
                serial([
                    v(lambda e: e.memset(z_row[:, :], 0)),
                    sy(lambda e: e.dma_start(z_row[:, 0:N], node_type_119.partition_broadcast(NELEM))),
                    sy(lambda e: e.dma_start(EMB[:, 0:G], emb)),
                    sy(lambda e: e.dma_start(adapt_sb[:, :], adapt)),
                    v(lambda e: e.tensor_scalar(z_hot[:, :], z_row[:, :], part_f[0:NELEM, 0:1], None, ALU.is_equal)),
                    t(lambda e: e.transpose(bank(0)[0:G, 0:NELEM], EMB[:, 0:G], ident[0:NELEM, 0:NELEM])),
                    a(lambda e: e.copy(embT[:, :], bank(0)[0:G, 0:NELEM])),
                    t(lambda e: e.matmul(bank(0)[0:NELEM, 0:G], embT[:, :], adapt_sb[:, :], start=True, stop=True)),
                    a(lambda e: e.copy(EMB[:, G:2 * G], bank(0)[0:NELEM, 0:G])),
                    *per_block(ze_tab, 2 * G, [(cols, EMB[:, :])]),
                ])

            def first_tables():
                serial([
                    *normalise(HN[:, :, :], X[:, :, :], W1[:, :, 0:H]),
                    v(lambda e: e.tensor_scalar(HN[:, :, :], HN[:, :, :], 0.0, None, ALU.max)),
                    v(lambda e: e.tensor_scalar(LOGM[:, :], MULT[:, :], 1.0, None, ALU.max)),
                    a(lambda e: e.activation(LOGM[:, :], LOGM[:, :], ACT.Ln)),
                    v(lambda e: e.tensor_tensor(W1[:, :, 0:H], HN[:, :, :], wide(MULT[:, :]), ALU.mult)),
                    v(lambda e: e.tensor_copy(W1[:, :, H:KW], MULT[:, :].unsqueeze(2))),
                    v(lambda e: e.tensor_copy(W1[:, :, KW:GW], ze_tab[:, :, G:2 * G])),
                    *split([TD[:, k, :, 0:GW] for k in range(3)], W1[:, :, 0:GW], W2[:, :, 0:GW]),
                    *split([TS[:, k, :, 0:G] for k in range(3)], ze_tab[:, :, 0:G], W2[:, :, 0:G]),
                    v(lambda e: e.memset(ACC[:, :, :], 0.0)),
                ])

            def after_gate():
                tot = STAT[:, 2, :]
                serial([
                    v(lambda e: e.tensor_scalar(tot, ACC[:, :, H], 1e-8, None, ALU.max)),
                    v(lambda e: e.reciprocal(STAT[:, 3, :], tot)),
                    v(lambda e: e.tensor_tensor(W1[:, :, 0:H], ACC[:, :, 0:H], wide(STAT[:, 3, :]), ALU.mult)),
                    v(lambda e: e.tensor_tensor(W1[:, :, 0:H], W1[:, :, 0:H], HN[:, :, :], ALU.add)),
                    *normalise(HN[:, :, :], W1[:, :, 0:H], W2[:, :, 0:H], GN[:, 0, :], GN[:, 1, :]),
                ])

            def layer_tables(l):
                serial([
                    *transposed(HT[:, :], HN[:, :, :]),
                    *per_block(W1[:, :, :], 2 * H, [(lambda b: HT[:, b * P:(b + 1) * P], WQK[:, l, :])]),
                    *normalise(W2[:, :, 0:H], W1[:, :, 0:H], W2[:, :, H:2 * H], LP[:, 0, l, :], LP[:, 1, l, :]),
                    v(lambda e: e.memset(W2[:, :, H:KW], 1.0)),
                ])
                serial([
                    a(lambda e: e.copy(TS[:, 0, :, :], W2[:, :, 0:KW])),
                    v(lambda e: e.tensor_tensor(W2[:, :, 0:KW], W2[:, :, 0:KW], TS[:, 0, :, :], ALU.subtract)),
                    a(lambda e: e.copy(TS[:, 1, :, :], W2[:, :, 0:KW])),
                    v(lambda e: e.tensor_tensor(TS[:, 2, :, :], W2[:, :, 0:KW], TS[:, 1, :, :], ALU.subtract)),
                    *normalise(W2[:, :, 0:H], W1[:, :, H:2 * H], W2[:, :, H:2 * H], LP[:, 2, l, :], LP[:, 3, l, :]),
                    v(lambda e: e.tensor_copy(W2[:, :, H:KW], LOGM[:, :].unsqueeze(2))),
                    v(lambda e: e.tensor_copy(W2[:, :, KW:DW], HN[:, :, :])),
                    *split([TD[:, k, :, :] for k in range(3)], W2[:, :, :], W1[:, :, :]),
                    v(lambda e: e.memset(ACC[:, :, :], 0.0)),
                    v(lambda e: e.memset(SMAX[:, :], -BIG)),
                ])

            def layer_update(l):
                den = STAT[:, 2, :]
                steps = [
                    v(lambda e: e.tensor_scalar(den, ACC[:, :, H], 1e-10, None, ALU.add)),
                    v(lambda e: e.reciprocal(STAT[:, 3, :], den)),
                    v(lambda e: e.tensor_tensor(W1[:, :, 0:H], ACC[:, :, 0:H], wide(STAT[:, 3, :]), ALU.mult)),
                    *transposed(HT[:, :], W1[:, :, 0:H]),
                ]
                for c in range(0, NPAD, 4 * 512):
                    n = min(4 * 512, NPAD - c)
                    steps += [
                        t(many([lambda e, c=c, k=k, w=min(512, n - k): e.matmul(bank(0, 4)[0:H, k:k + w], WM[:, l, :], HT[:, c + k:c + k + w], start=True, stop=True)
                                for k in range(0, n, 512)])),
                        a(lambda e, c=c, n=n: e.copy(AT[:, c:c + n], bank(0, 4)[0:H, 0:n])),
                    ]
                steps += [
                    *transposed(HT[:, :], HN[:, :, :]),
                    *per_block(W1[:, :, :], H, [(lambda b: HT[:, b * P:(b + 1) * P], WU[:, l, 0, :]),
                                                (lambda b: AT[:, b * P:(b + 1) * P], WU[:, l, 1, :])]),
                    v(lambda e: e.scalar_tensor_tensor(W2[:, :, 0:H], W1[:, :, 0:H], 0.01, W1[:, :, 0:H], ALU.mult, ALU.max)),
                    v(lambda e: e.tensor_tensor(W1[:, :, 0:H], W2[:, :, 0:H], HN[:, :, :], ALU.add)),
                    *normalise(HN[:, :, :], W1[:, :, 0:H], W2[:, :, 0:H], LP[:, 4, l, :], LP[:, 5, l, :]),
                ]
                serial(steps)

            def one(ap):
                return ap

            def bd_of(bd, k, n=1):
                return slice(bd + k, bd + k + n) if isinstance(bd, int) else ds(bd, n)

            def build_one_hots(n, ohg):
                spots = bank(0, 2)
                where = lambda f: rec[:, 0:n, f:f + 1].broadcast_to([P, n, P])
                iotas = iota_f[:, :].unsqueeze(1).broadcast_to([P, n, P])
                flip = lambda of: t(many([lambda e, c=c: e.matmul(spots[:, c * P:(c + 1) * P], of[:, c, :], ident8[:, :], start=True, stop=True) for c in range(n)]))
                take = lambda k: a(lambda e: e.activation(ohg[:, k, 0:n, :], spots[:, 0:n * P].rearrange("p (c e) -> p c e", c=n), ACT.Copy, saturate=False))
                return [
                    v(lambda e: e.tensor_tensor(ohg[:, 2, 0:n, :], iotas, where(F_SRC), ALU.is_equal, saturate=False)),
                    v(lambda e: e.tensor_tensor(oh_d[:, 0:n, :], iotas, where(F_DST), ALU.is_equal, saturate=False)),
                    flip(ohg[:, 2, :, :]), take(0), flip(oh_d[:, :, :]), take(1),
                ]

            def gather(n, spot, hot, rows, width):
                return t(many([lambda e, c=c, k=k: e.matmul(spot(c), hot[:, c, :], rows(c, k)[:, 0:width], start=k == 0, stop=k == 2)
                               for c in range(n) for k in range(3)]))

            def stage_src(bs, w=KW):
                return v(lambda e: e.tensor_copy(ts_row[:, :, 0:w], TS[:, :, ds(bs, 1), 0:w].rearrange("p k o w -> p k (o w)")))

            def stage_dst(bd, w=DW):
                return v(lambda e: e.tensor_copy(td_row[:, :, 0:w], TD[:, :, ds(bd, 1), 0:w].rearrange("p k o w -> p k (o w)")))

            def dst_rows(bd):
                return (lambda c, k: TD[:, k, bd + c, :]) if isinstance(bd, int) else (lambda c, k: td_row[:, k, :])

            src_rows = lambda c, k: ts_row[:, k, :]

            def scatter(n, hots, vals, spot):
                return t(many([lambda e, c=c: e.matmul(spot, hots[:, c, :], vals[:, c, :], start=c == 0, stop=c == n - 1) for c in range(n)]))

            d_spot = lambda c: bank(2, 2)[:, c * P:c * P + DW]
            d_all = lambda n: bank(2, 2)[:, 0:GC * P].rearrange("p (c w) -> p c w", w=P)[:, 0:n, :]
            q_spot = lambda c: bank(4)[:, c * KW:(c + 1) * KW]
            q_all = lambda n, w=KW: bank(4)[:, 0:n * KW].rearrange("p (c w) -> p c w", w=KW)[:, :, 0:w]

            def gate_values(n, ohg, bs, bd):
                both = range(0, n * P, 512)
                return [
                    t(many([lambda e, c=c: e.transpose(bank(0, 2)[0:RBF, c * P:(c + 1) * P], rec[:, c, 0:RBF], ident[:, :]) for c in range(n)])),
                    v(lambda e: e.tensor_copy(attrT[:, 0:n * P], bank(0, 2)[0:RBF, 0:n * P])),
                    t(many([lambda e, k=k: e.matmul(bank(0, 2)[0:H, k:min(k + 512, n * P)], F1[:, :], attrT[:, k:min(k + 512, n * P)], start=True, stop=True)
                            for k in both])),
                    a(lambda e: e.activation(act1[:, 0:n * P], bank(0, 2)[0:H, 0:n * P], ACT.Silu, bias=F1B[:, 0:1])),
                    t(many([f for c in range(n) for f in (
                        lambda e, c=c: e.matmul(bank(5)[:, c * H:(c + 1) * H], act1[:, c * P:(c + 1) * P], F2[:, :], start=True, stop=False),
                        lambda e, c=c: e.matmul(bank(5)[:, c * H:(c + 1) * H], ones_row[:, :], F2B[:, :], start=False, stop=True))])),
                    gather(n, lambda c: d_spot(c)[:, 0:GW], ohg[:, 1], dst_rows(bd), GW),
                    gather(n, lambda c: q_spot(c)[:, 0:G], ohg[:, 0], src_rows, G),
                    a(lambda e: e.copy(src_e[:, 0:n, :], q_all(n, G))),
                    v(lambda e: e.tensor_tensor(src_e[:, 0:n, :], src_e[:, 0:n, :], d_all(n)[:, :, KW:GW], ALU.mult)),
                    v(lambda e: e.tensor_reduce(cw[:, 2, 0:n], src_e[:, 0:n, :], AX.X, ALU.add)),
                    v(lambda e: e.tensor_tensor(gate[:, 0:n, :], bank(5)[:, 0:n * H].rearrange("p (c h) -> p c h", h=H),
                                                cw[:, 2, 0:n].unsqueeze(2).broadcast_to([P, n, H]), ALU.add)),
                    v(lambda e: e.tensor_tensor(gate[:, 0:n, :], gate[:, 0:n, :], d_all(n)[:, :, 0:H], ALU.mult)),
                    v(lambda e: e.scalar_tensor_tensor(cw[:, 0, 0:n], rec[:, 0:n, F_W], -1.0, rec[:, 0:n, F_W], ALU.mult, ALU.max)),
                    v(lambda e: e.tensor_scalar(cw[:, 0, 0:n], cw[:, 0, 0:n], CUT, None, ALU.min)),
                    a(lambda e: e.activation(cw[:, 1, 0:n], cw[:, 0, 0:n], ACT.Sin, bias=half_pi[:, 0:1], scale=-2 * HALF_PI / CUT)),
                    v(lambda e: e.tensor_scalar(cw[:, 1, 0:n], cw[:, 1, 0:n], 0.5, 0.5, ALU.mult, ALU.add)),
                    v(lambda e: e.scalar_tensor_tensor(cw[:, 0, 0:n], rec[:, 0:n, F_W], CUT, cw[:, 1, 0:n], ALU.is_lt, ALU.mult)),
                    v(lambda e: e.tensor_tensor(val[:, 0:n, 0:H], gate[:, 0:n, :], cw[:, 0, 0:n].unsqueeze(2).broadcast_to([P, n, H]), ALU.mult)),
                    v(lambda e: e.tensor_copy(val[:, 0:n, H:KW], d_all(n)[:, :, H:KW])),
                    a(lambda e: e.copy(os32[:, 0:n, :], ohg[:, 2, 0:n, :])),
                    scatter(n, os32, val, bank(6)[:, 0:KW]),
                    v(lambda e: e.tensor_tensor(ACC[:, ds(bs, 1), :], ACC[:, ds(bs, 1), :], bank(6)[:, 0:KW].unsqueeze(1), ALU.add)),
                ]

            def degrees(n, bd):
                return [
                    t(many([lambda e, c=c: e.matmul(bank(7)[:, c:c + 1], oh_d[:, c, :], ones8[:, :], start=True, stop=True) for c in range(n)])),
                    v(lambda e: e.tensor_tensor(DEG[:, bd_of(bd, 0, n)], DEG[:, bd_of(bd, 0, n)], bank(7)[:, 0:n], ALU.add)),
                ]

            def adjacency(ohg, bs, g):
                return [
                    t(many([lambda e, c=c: e.matmul(bank(0, 2)[:, c * P:(c + 1) * P], ohg[:, 2, c, :], oh_d[:, c, :], start=True, stop=True) for c in range(GC)])),
                    a(lambda e: e.copy(adj_out[:, :, :], bank(0, 2)[:, 0:GC * P].rearrange("p (c e) -> p c e", c=GC))),
                    sy(lambda e: e.dma_start(ADJ[ds(bs, 1), :, g * GC * P:(g + 1) * GC * P].rearrange("o p w -> (o p) w"),
                                             adj_out[:, :, :].rearrange("p c e -> p (c e)"))),
                    sy(lambda e: e.dma_start(OHD[ds(bs, 1), g, :, :].rearrange("o p w -> (o p) w"), ohg.rearrange("p k c e -> p (k c e)").bitcast(F32))),
                ]

            def load_rec(bs, g):
                return sy(lambda e: e.dma_start(rec[:, :, :].rearrange("p c w -> p (c w)"),
                                                rec_rows[ds(bs, 1), :, g * GC * RW:(g + 1) * GC * RW].rearrange("o p w -> (o p) w")))

            def extra_chunks(body):
                barrier()
                n = extra_count()
                with e.If(n > 0):
                    with e.Fori(0, n) as j:
                        in_turn([sy(lambda e: e.dma_start(rec[:, 0, :], rec_extra[ds(j, 1), :, :].rearrange("o p w -> (o p) w")))])
                        in_turn_end()
                        bs = e.value_load(rec[0:1, 0, F_BS:F_BS + 1].bitcast(I32), min_val=0, max_val=NB - 1)
                        bd = e.value_load(rec[0:1, 0, F_BD:F_BD + 1].bitcast(I32), min_val=0, max_val=NB - 1)
                        in_turn([(who, lambda e: e.drain(), 1) for who in ENGINES])
                        in_turn(body(bs, bd))
                    in_turn_end()
                barrier()

            def gate_pass():
                barrier()
                with e.Fori(0, NB) as bs:
                    in_turn([stage_src(bs, G)])
                    for g in range(NG):
                        ohg = oh[:, g]
                        in_turn([load_rec(bs, g), *build_one_hots(GC, ohg), *adjacency(ohg, bs, g), *degrees(GC, g * GC), *gate_values(GC, ohg, bs, g * GC)])
                in_turn_end()
                extra_chunks(lambda bs, bd: [stage_src(bs, G), stage_dst(bd, GW), *build_one_hots(1, oh[:, 0]), *degrees(1, bd), *gate_values(1, oh[:, 0], bs, bd)])

            def scores(n, ohg, bs, bd, to):
                return [
                    gather(n, d_spot, ohg[:, 1], dst_rows(bd), DW),
                    gather(n, q_spot, ohg[:, 0], src_rows, KW),
                    v(lambda e: e.scalar_tensor_tensor(xk[:, 0:n, 0:RBF], rec[:, 0:n, 0:RBF], 0.1, d_all(n)[:, :, 0:RBF], ALU.mult, ALU.add)),
                    v(lambda e: e.tensor_copy(xk[:, 0:n, RBF:KW], d_all(n)[:, :, RBF:KW])),
                    v(lambda e: e.tensor_tensor(xk[:, 0:n, :], xk[:, 0:n, :], q_all(n), ALU.mult)),
                    v(lambda e: e.tensor_reduce(to, xk[:, 0:n, :], AX.X, ALU.add)),
                ]

            def running_max(n, hots, score):
                return [a(lambda e: e.activation(os32[:, 0:n, :], hots[:, 0:n, :], ACT.Copy, bias=-BIG, scale=BIG))] + [
                    v(lambda e, c=c: e.scalar_tensor_tensor(runmax[:, :], os32[:, c, :], score(c), runmax[:, :], ALU.add, ALU.max)) for c in range(n)]

            def row_max(bs):
                return [
                    t(lambda e: e.transpose(bank(6)[:, 0:P], runmax[:, :], ident[:, :])),
                    v(lambda e: e.tensor_reduce(rowmax[:, 0:1], bank(6)[:, 0:P], AX.X, ALU.max)),
                    v(lambda e: e.tensor_tensor(SMAX[:, ds(bs, 1)], SMAX[:, ds(bs, 1)], rowmax[:, 0:1], ALU.max)),
                ]

            def weights(n, hot, bs, score, es):
                r = rowmax
                return [
                    v(lambda e: e.tensor_copy(r[:, 0:1], SMAX[:, ds(bs, 1)])),
                    v(lambda e: e.tensor_copy(smax3[:, 0:1], r[:, 0:1])),
                    v(lambda e: e.tensor_tensor(r[:, 1:2], r[:, 0:1], smax3[:, 0:1], ALU.subtract)),
                    v(lambda e: e.tensor_copy(smax3[:, 1:2], r[:, 1:2])),
                    v(lambda e: e.tensor_tensor(smax3[:, 2:3], r[:, 1:2], smax3[:, 1:2], ALU.subtract)),
                    t(many([lambda e, c=c: e.matmul(bank(6)[:, 3 * c:3 * c + 3], hot(c), smax3[:, :], start=True, stop=True) for c in range(n)])),
                    v(lambda e: e.tensor_reduce(es[:, 0, 0:n], bank(6)[:, 0:3 * n].rearrange("p (c k) -> p c k", k=3), AX.X, ALU.add)),
                    v(lambda e: e.tensor_tensor(es[:, 0, 0:n], score, es[:, 0, 0:n], ALU.subtract)),
                    v(lambda e: e.tensor_scalar(es[:, 0, 0:n], es[:, 0, 0:n], 20.0, None, ALU.min)),
                    a(lambda e: e.activation(es[:, 1, 0:n], es[:, 0, 0:n], ACT.Exp)),
                ]

            def extra_max(bs, bd):
                return [stage_src(bs), stage_dst(bd), *build_one_hots(1, oh[:, 0]), *scores(1, oh[:, 0], bs, bd, S1[:, 0:1]),
                        v(lambda e: e.memset(runmax[:, :], -BIG)),
                        *running_max(1, oh[:, 0, 2], lambda c: S1[:, 0:1]), *row_max(bs)]

            def extra_sum(bs, bd):
                return [stage_src(bs), stage_dst(bd), *build_one_hots(1, oh[:, 0]), *scores(1, oh[:, 0], bs, bd, S1[:, 0:1]),
                        *weights(1, lambda c: oh[:, 0, 0, 0, :], bs, S1[:, 0:1], ES[:, :, :]),
                        v(lambda e: e.tensor_scalar(V1[:, 0, 0:H], d_spot(0)[:, KW:DW], ES[:, 1, 0:1], None, ALU.mult)),
                        v(lambda e: e.tensor_copy(V1[:, 0, H:KW], ES[:, 1, 0:1])),
                        a(lambda e: e.copy(os32[:, 0, :], oh[:, 0, 2, 0, :])),
                        scatter(1, os32, V1, bank(7)[:, 0:KW]),
                        v(lambda e: e.tensor_tensor(ACC[:, ds(bs, 1), :], ACC[:, ds(bs, 1), :], bank(7)[:, 0:KW].unsqueeze(1), ALU.add))]

            def attention_row(b, p, now=True, then=True):
                sl = lambda r: slice(r, r + 1) if isinstance(r, int) else ds(r, 1)
                q = 1 - p
                buf = lambda g: (p + g) % 2
                D = lambda g, c: bank(2 * buf(g), 2)[:, c * P:c * P + DW]
                Dall = lambda g: bank(2 * buf(g), 2)[:, 0:GC * P].rearrange("p (c w) -> p c w", w=P)
                Q = lambda g, c: bank(4 + buf(g))[:, c * KW:(c + 1) * KW]
                Qall = lambda g: bank(4 + buf(g))[:, 0:GC * KW].rearrange("p (c w) -> p c w", w=KW)
                cols = lambda g: slice(g * GC, (g + 1) * GC)

                if name == "sync" and now:
                    for g in range(NG):
                        of_row(summed, g + 1, back=2)
                        e.dma_start(cells[:, p, g].rearrange("p k c e -> p (k c e)").bitcast(F32),
                                    OHD[sl(b), g, :, :].rearrange("o p w -> (o p) w")).then_inc(s_cells[p][g], 16)
                        e.dma_start(recs[:, p, g].rearrange("p c w -> p (c w)"),
                                    rec_rows[sl(b), :, g * GC * RW:(g + 1) * GC * RW].rearrange("o p w -> (o p) w")).then_inc(s_cells[p][g], 16)

                if name == "tensor":
                    def gathers(g):
                        if g == 0:
                            of_row(staged, 1)
                        if g >= 2:
                            of_row(multiplied, g - 1)
                            of_row(carried, g - 1)
                        else:
                            of_row(multiplied, g - 1 + NG, back=1)
                            of_row(carried, g - 1 + NG, back=1)
                        e.wait_ge(s_cells[p][g], e.snap(loads[p], min_val=0, max_val=1 << 16) * 32 + 32)
                        e.sem_inc(absorb, 1)
                        for c in range(GC):
                            for k in range(3):
                                e.matmul(D(g, c), cells[:, p, g, 1, c, :], TD[:, k, g * GC + c, :], start=k == 0, stop=k == 2)
                        for c in range(GC):
                            for k in range(3):
                                last = e.matmul(Q(g, c), cells[:, p, g, 0, c, :], ts2[:, p, k, :], start=k == 0, stop=k == 2)
                        last.then_inc(gathered.sem, 1)

                    def flip():
                        of_row(combined, 1, back=1)
                        e.transpose(bank(6)[:, 0:P], slot_top[:, :], ident[:, :]).then_inc(flipped.sem, 1)

                    def gather_max():
                        of_row(parted, 4, back=1)
                        for c in range(NB):
                            last = e.matmul(bank(6)[:, P + 3 * c:P + 3 * c + 3], cells[:, q, c // GC, 0, c % GC, :], top3[:, :], start=True, stop=True)
                        last.then_inc(max_gathered.sem, 1)

                    def sums(g):
                        if g == 0:
                            of_row(added, 1, back=2)
                        of_row(weighted, g + 1, back=1)
                        for c in range(GC):
                            last = e.matmul(bank(7)[:, 0:3 * KW], cells[:, q, g, 2, c, :], values3[:, g * GC + c, :, :].rearrange("p k w -> p (k w)"),
                                            start=g + c == 0, stop=g * GC + c == NB - 1)
                        last.then_inc(summed.sem, 1)

                    plan = [(gathers, 0), (flip,), (gathers, 1), (gather_max,), (gathers, 2), (gathers, 3), (gathers, 4), (sums, 0),
                            (sums, 1), (gathers, 5), (sums, 2), (sums, 3), (gathers, 6), (sums, 4), (sums, 5), (sums, 6)]
                    for f, *x in plan:
                        if now if f is gathers else then:
                            f(*x)

                if name == "vector":
                    links = [0]

                    def link(ins):
                        links[0] += 1
                        ins.then_inc(dve_link.sem, 1)
                        of_row(dve_link, links[0], plain=False)

                    def score_cells(g):
                        of_row(gathered, g + 1)
                        x1, x2 = xks[:, 0], xks[:, 1]
                        e.scalar_tensor_tensor(x1[:, :, 0:RBF], recs[:, p, g, :, 0:RBF], 0.1, Dall(g)[:, :, 0:RBF], ALU.mult, ALU.add)
                        link(e.tensor_copy(x1[:, :, RBF:KW], Dall(g)[:, :, RBF:KW]))
                        ins = e.tensor_tensor(x2, x1, Qall(g), ALU.mult)
                        ins.then_inc(multiplied.sem, 1)
                        of_row(multiplied, g + 1, plain=False)
                        link(e.tensor_reduce(score[:, p, cols(g)], x2, AX.X, ALU.add))

                    def max_cells(g):
                        of_row(masked, g + 1)
                        for c in range(GC):
                            s1 = score[:, p, g * GC + c:g * GC + c + 1]
                            if g == 0:
                                last = e.tensor_scalar(slot_max[:, c, :], mask[:, buf(g), c, :], s1, None, ALU.add)
                            else:
                                last = e.scalar_tensor_tensor(slot_max[:, c, :], mask[:, buf(g), c, :], s1, slot_max[:, c, :], ALU.add, ALU.max)
                        last.then_inc(maxed.sem, 1)

                    def take_max():
                        of_row(flipped, 1, back=1)
                        e.tensor_reduce(top[:, 0:1], bank(6)[:, 0:P], AX.X, ALU.max).then_inc(row_maxed.sem, 1)
                        of_row(row_maxed, 1, back=1, plain=False)
                        e.tensor_tensor(top[:, 1:2], top[:, 0:1], SMAX[:, sl(b - 1)], ALU.max).then_inc(row_maxed.sem, 1)

                    def fold_max():
                        of_row(max_gathered, 1, back=1)
                        e.tensor_reduce(edge_top[:, 0, :], bank(6)[:, P:P + 3 * NB].rearrange("p (c k) -> p c k", k=3), AX.X, ALU.add).then_inc(folded.sem, 1)

                    def add_row():
                        of_row(summed, NG, back=1)
                        e.tensor_reduce(row_sum[:, :], bank(7)[:, 0:3 * KW].rearrange("p (k w) -> p w k", k=3), AX.X, ALU.add).then_inc(added.sem, 1)
                        of_row(added, 1, back=1)
                        e.tensor_tensor(ACC[:, sl(b - 1), :], ACC[:, sl(b - 1), :], row_sum[:, :].unsqueeze(1), ALU.add)

                    for g in range(NG):
                        if now:
                            score_cells(g)
                            max_cells(g)
                        if g == 0 and then:
                            take_max()
                        if g == 1 and then:
                            fold_max()
                    if then:
                        add_row()
                    if now:
                        of_row(maxed, NG, plain=False)
                        e.tensor_reduce(slot_top[:, :], slot_max[:, :, :].rearrange("p c n -> p n c"), AX.X, ALU.max).then_inc(combined.sem, 1)

                if name == "scalar":
                    def carry(g):
                        if g == 0:
                            of_row(summed, NG, back=2)
                        of_row(multiplied, g + 1)
                        e.copy(values[:, p, cols(g), 0:H], Dall(g)[:, :, KW:DW]).then_inc(carried.sem, 1)

                    def mask_cells(g):
                        of_row(gathered, g + 1)
                        if g >= 2:
                            of_row(maxed, g - 1)
                        else:
                            of_row(maxed, g - 1 + NG, back=1)
                        e.activation(mask[:, buf(g), :, :], cells[:, p, g, 2, :, :], ACT.Copy, bias=-BIG, scale=BIG).then_inc(masked.sem, 1)

                    def raise_weights():
                        of_row(bounded, 2, back=1)
                        e.activation(values[:, q, :, H:KW], edge_top[:, 2, :].unsqueeze(2), ACT.Exp).then_inc(raised.sem, 1)

                    def high(g):
                        of_row(scaled, g + 1, back=1)
                        of_row(summed, g + 1, back=2)
                        e.copy(values3[:, cols(g), 0, :], values[:, q, cols(g), :]).then_inc(high_part.sem, 1)

                    def middle(g):
                        of_row(less_high, g + 1, back=1)
                        e.copy(values3[:, cols(g), 1, :], values[:, q, cols(g), :]).then_inc(middle_part.sem, 1)

                    both = lambda g: [(mask_cells, g + 1), (carry, g)]
                    plan = [(mask_cells, 0), *both(0), *both(1), (raise_weights,), (high, 0), *both(2), (high, 1), (middle, 0),
                            *both(3), (high, 2), (middle, 1), *both(4), (high, 3), (high, 4), (middle, 2), (middle, 3),
                            *both(5), (high, 5), (high, 6), (middle, 4), (middle, 5), (carry, 6), (middle, 6)]
                    for f, *x in plan:
                        if now if f in (carry, mask_cells) else then:
                            f(*x)

                if name == "gpsimd":
                    def chained(what, c, ins):
                        ins.then_inc(what.sem, 1)
                        of_row(what, c, back=1, plain=True)

                    if now:
                        of_row(gathered, NG, back=2)
                        e.tensor_copy(ts2[:, p, :, :], TS[:, :, sl(b), :].rearrange("p k o w -> p k (o w)")).then_inc(staged.sem, 1)
                    if then:
                        of_row(row_maxed, 2, back=1)
                        e.tensor_copy(SMAX[:, sl(b - 1)], top[:, 1:2])
                        chained(parted, 1, e.tensor_copy(top3[:, 0:1], top[:, 1:2]))
                        chained(parted, 2, e.tensor_tensor(top[:, 2:3], top[:, 1:2], top3[:, 0:1], ALU.subtract))
                        chained(parted, 3, e.tensor_copy(top3[:, 1:2], top[:, 2:3]))
                        e.tensor_tensor(top3[:, 2:3], top[:, 2:3], top3[:, 1:2], ALU.subtract).then_inc(parted.sem, 1)
                        of_row(folded, 1, back=1)
                        chained(bounded, 1, e.tensor_tensor(edge_top[:, 1, :], score[:, q, :], edge_top[:, 0, :], ALU.subtract))
                        e.tensor_scalar(edge_top[:, 2, :], edge_top[:, 1, :], 20.0, None, ALU.min).then_inc(bounded.sem, 1)
                        of_row(raised, 1, back=1)
                        def scale(g):
                            of = values[:, q, cols(g), :]
                            e.tensor_tensor(of[:, :, 0:H], of[:, :, 0:H], of[:, :, H:KW].broadcast_to([P, GC, H]), ALU.mult).then_inc(scaled.sem, 1)

                        def take_high(g):
                            of_row(high_part, g + 1, back=1)
                            e.tensor_tensor(values[:, q, cols(g), :], values[:, q, cols(g), :], values3[:, cols(g), 0, :], ALU.subtract).then_inc(less_high.sem, 1)

                        def take_middle(g):
                            of_row(middle_part, g + 1, back=1)
                            e.tensor_tensor(values3[:, cols(g), 2, :], values[:, q, cols(g), :], values3[:, cols(g), 1, :], ALU.subtract).then_inc(weighted.sem, 1)

                        for g in range(NG + 2):
                            if g < NG:
                                scale(g)
                            if 0 <= g - 1 < NG:
                                take_high(g - 1)
                            if g >= 2:
                                take_middle(g - 2)

                if now:
                    e.reg_add(row, row, 1)
                    e.reg_add(loads[p], loads[p], 1)

            def attention_pass():
                extra_chunks(extra_max)
                attention_row(0, 0, then=False)
                with e.Fori(0, (NB - 1) // 2) as i:
                    attention_row(i * 2 + 1, 1)
                    attention_row(i * 2 + 2, 0)
                attention_row(NB, 1, now=False)
                extra_chunks(extra_sum)

            def spread_setup():
                serial([
                    v(lambda e: e.tensor_tensor(X[:, :, :], X[:, :, :], HN[:, :, :], ALU.add)),
                    *normalise(HN[:, :, :], X[:, :, :], mm[:, :, :]),
                    v(lambda e: e.tensor_scalar(HN[:, :, :], HN[:, :, :], 0.0, None, ALU.max)),
                    a(lambda e: e.activation(STAT[:, 0, :], DEG[:, :], ACT.Sqrt)),
                    v(lambda e: e.reciprocal(dinv[:, :], STAT[:, 0, :])),
                    v(lambda e: e.tensor_tensor(g_f[:, :, :], HN[:, :, :], wide(dinv[:, :]), ALU.mult)),
                ])

            tiles = [(b, min(4, NB - b)) for b in range(0, NB, 4)]

            def spread_extra(bs, bd):
                hot = lambda to, f: v(lambda e: e.tensor_tensor(to[:, :], iota_f[:, :], rec_l[:, f:f + 1].broadcast_to([P, P]), ALU.is_equal))
                return [
                    hot(ohs_l, F_SRC), hot(ohd_l, F_DST),
                    t(lambda e: e.transpose(bank(4)[:, 0:P], ohs_l[:, :], ident[:, :])),
                    a(lambda e: e.copy(ohsT_l[:, :], bank(4)[:, 0:P])),
                    v(lambda e: e.tensor_copy(val_l[:, :], g_f[:, ds(bs, 1), :].rearrange("p o h -> p (o h)"))),
                    t(lambda e: e.matmul(bank(5)[:, 0:H], ohsT_l[:, :], val_l[:, :], start=True, stop=True)),
                    a(lambda e: e.copy(val_l[:, :], bank(5)[:, 0:H])),
                    t(lambda e: e.matmul(bank(6)[:, 0:H], ohd_l[:, :], val_l[:, :], start=True, stop=True)),
                    v(lambda e: e.tensor_tensor(mm[:, ds(bd, 1), :], mm[:, ds(bd, 1), :], bank(6)[:, 0:H].unsqueeze(1), ALU.add)),
                ]

            def spread_extra_chunks():
                barrier()
                n = extra_count()
                with e.If(n > 0):
                    with e.Fori(0, n) as j:
                        in_turn([sy(lambda e: e.dma_start(rec_l[:, :], rec_extra[ds(j, 1), :, :].rearrange("o p w -> (o p) w")))])
                        in_turn_end()
                        bs = e.value_load(rec_l[0:1, F_BS:F_BS + 1].bitcast(I32), min_val=0, max_val=NB - 1)
                        bd = e.value_load(rec_l[0:1, F_BD:F_BD + 1].bitcast(I32), min_val=0, max_val=NB - 1)
                        in_turn([(who, lambda e: e.drain(), 1) for who in ENGINES])
                        in_turn(spread_extra(bs, bd))
                    in_turn_end()
                barrier()

            def spread_step(k):
                serial(split([g3[:, :, j, :] for j in range(3)], g_f[:, :, :], g_r[:, :, :]))
                barrier()
                for i, (b0, nb) in enumerate(tiles):
                    n = k * len(tiles) + i
                    if name == "sync":
                        if n >= 2:
                            e.wait_ge(s_apes, n - 1)
                        e.dma_start(AJ[:, n % 2, :, 0:nb * P], adj_groups[:, :, b0 * P:(b0 + nb) * P]).then_inc(s_aload[n % 2], 16)
                    if name == "tensor":
                        e.wait_ge(s_aload[n % 2], 16 * (n // 2 + 1))
                        if n >= 2:
                            e.wait_ge(s_afold, n - 1)
                        for c in range(nb):
                            spot = bank(2 * (n % 2), 2)[:, c * 256:c * 256 + 3 * H]
                            for bs in range(NB):
                                last = e.matmul(spot, AJ[:, n % 2, bs, c * P:(c + 1) * P], g3[:, bs, :, :].rearrange("p k h -> p (k h)"),
                                                start=bs == 0, stop=bs == NB - 1)
                        last.then_inc(s_apes, 1)
                    if name == "vector":
                        e.wait_ge(s_apes, n + 1)
                        spots = bank(2 * (n % 2), 2).rearrange("p (c w) -> p c w", w=256)[:, 0:nb, 0:3 * H]
                        e.tensor_reduce(mm[:, b0:b0 + nb, :], spots.rearrange("p c (k h) -> p c h k", k=3), AX.X, ALU.add).then_inc(s_afold, 1)
                spread_extra_chunks()
                serial([
                    v(lambda e: e.tensor_tensor(mm[:, :, :], mm[:, :, :], g_f[:, :, :], ALU.add)),
                    v(lambda e: e.tensor_tensor(mm[:, :, :], mm[:, :, :], wide(dinv[:, :]), ALU.mult)),
                    v(lambda e: e.tensor_scalar(mm[:, :, :], mm[:, :, :], 1.0 - ALPHA, None, ALU.mult)),
                    v(lambda e: e.scalar_tensor_tensor(mm[:, :, :], HN[:, :, :], ALPHA, mm[:, :, :], ALU.mult, ALU.add)),
                    v(lambda e: e.tensor_tensor(g_f[:, :, :], mm[:, :, :], wide(dinv[:, :]), ALU.mult)),
                ])

            def store():
                serial([
                    v(lambda e: e.tensor_tensor(X[:, :, :], X[:, :, :], mm[:, :, :], ALU.add)),
                    sy(lambda e: e.dma_start(out[0:(NB - 1) * P, :].rearrange("(b p) h -> p b h", p=P), X[:, 0:NB - 1, :])),
                    sy(lambda e: e.dma_start(out[(NB - 1) * P:N, :], X[0:TAIL, NB - 1, :])),
                ])

            load_all()
            count_cells()
            fill_extra()
            place_edges()
            if debug == "rec":
                serial([sy(lambda e: e.dma_start(out, REC[0:out.shape[0], :]))])
                e.wait_ge(order, count[0])
                return
            embed()
            first_tables()
            gate_pass()
            after_gate()
            if debug != "gate":
                for l in range(L):
                    layer_tables(l)
                    attention_pass()
                    layer_update(l)
                    if debug == "layer0":
                        break
            if debug in ("gate", "layer0"):
                serial([v(lambda e: e.tensor_copy(X[:, :, :], HN[:, :, :])), v(lambda e: e.memset(W1[:, :, :], 0.0))])
                serial([
                    sy(lambda e: e.dma_start(out[0:(NB - 1) * P, :].rearrange("(b p) h -> p b h", p=P), X[:, 0:NB - 1, :])),
                    sy(lambda e: e.dma_start(out[(NB - 1) * P:N, :], X[0:TAIL, NB - 1, :])),
                ])
                e.wait_ge(order, count[0])
                return
            spread_setup()
            for k in range(KSTEP):
                spread_step(k)
            store()
            e.wait_ge(order, count[0])

        block.sync(lambda e: program("sync", e))
        block.tensor(lambda e: program("tensor", e))
        block.vector(lambda e: program("vector", e))
        block.scalar(lambda e: program("scalar", e))
        block.gpsimd(lambda e: program("gpsimd", e))


def kernel(x, src, dst, edge_attr_40, edge_weight, node_type_119, node_vec, L0_gnn_Wq, L0_gnn_gq, L0_gnn_bq, L0_gnn_Wk,
           L0_gnn_gk, L0_gnn_bk, L0_gnn_Wm, L0_gnn_Wu, L0_gnn_go, L0_gnn_bo, L0_gnn_F1W, L0_gnn_F1b, L0_gnn_F2W,
           L0_gnn_F2b, L0_gnn_gn, L0_gnn_bn, L0_gnn_emb, L0_gnn_adapt):
    import numpy as np
    from concourse import bacc
    from concourse.bass_utils import run_bass_kernel_spmd

    arrays = {
        "x": x, "src": src, "dst": dst, "edge_attr_40": edge_attr_40, "edge_weight": edge_weight,
        "node_type_119": node_type_119, "node_vec": node_vec, "Wq": L0_gnn_Wq, "gq": L0_gnn_gq, "bq": L0_gnn_bq,
        "Wk": L0_gnn_Wk, "gk": L0_gnn_gk, "bk": L0_gnn_bk, "Wm": L0_gnn_Wm, "Wu": L0_gnn_Wu, "go": L0_gnn_go,
        "bo": L0_gnn_bo, "F1W": L0_gnn_F1W, "F1b": L0_gnn_F1b, "F2W": L0_gnn_F2W, "F2b": L0_gnn_F2b, "gn": L0_gnn_gn,
        "bn": L0_gnn_bn, "emb": L0_gnn_emb, "adapt": L0_gnn_adapt,
    }
    arrays = {name: np.ascontiguousarray(a) for name, a in arrays.items()}
    nc = bacc.Bacc("TRN2", target_bir_lowering=False, num_devices=1)
    args = {name: nc.dram_tensor(f"in_{name}", a.shape, mybir.dt.from_np(a.dtype), kind="ExternalInput").ap()
            for name, a in arrays.items()}
    out = nc.dram_tensor("out", (N, H), F32, kind="ExternalOutput").ap()
    build(nc, out=out, **args)
    result = run_bass_kernel_spmd(nc, [{f"in_{name}": a for name, a in arrays.items()}], core_ids=[0])
    return result.results[0]["out"]
```

```python
from contextlib import ExitStack

import concourse.bass as bass
from concourse import mybir

F32, BF16, FP8, I32 = mybir.dt.float32, mybir.dt.bfloat16, mybir.dt.float8e4, mybir.dt.int32
ALU, ACT, AX = mybir.AluOpType, mybir.ActivationFunctionType, mybir.AxisListType
ds = bass.ds

N, E, H, RBF, L, G, NELEM = 6250, 200000, 48, 40, 4, 32, 119
CUT, KSTEP, ALPHA = 6.0, 5, 0.8
P = 128
NB = -(-N // P)
TAIL = N - (NB - 1) * P
NPAD = NB * P
CAP = P
EP = 125
ET = E // EP
NS = 8
SC = ET // NS
JB = 10
CELLS = NB * NB
GRID = CELLS * P
NOV = E // P
F_SRC, F_DST, F_W, F_BS, F_BD, RW = 40, 41, 42, 43, 44, 45
GC = 7
NG = NB // GC
KW = H + 1
DW = 2 * H + 1
GW = H + 1 + G
BIG = 1e30
HALF_PI = 1.5707963267948966
ENGINES = ("sync", "tensor", "vector", "scalar", "gpsimd")


def build(nc, x, src, dst, edge_attr_40, edge_weight, node_type_119, node_vec, Wq, gq, bq, Wk, gk, bk, Wm, Wu, go,
          bo, F1W, F1b, F2W, F2b, gn, bn, emb, adapt, out, debug=None):
    REC = nc.dram_tensor("edge_records", (GRID + NOV * P, RW), F32)
    OHD = nc.dram_tensor("one_hots", (NB, NG, P, 3 * GC * P // 4), F32)
    ADJ = nc.dram_tensor("adjacency", (NB, P, NB * P), BF16)
    rec_rows = REC[0:GRID, :].rearrange("(b p c) w -> b p (c w)", p=P, c=NB)
    rec_extra = REC[GRID:GRID + NOV * P, :].rearrange("(j p) w -> j p w", p=P)
    adj_groups = ADJ[:, :, :].rearrange("b s e -> s b e")

    ctx = ExitStack()
    with ctx:
        def sem(name):
            return ctx.enter_context(nc.semaphore(name))

        order, turn, absorb = sem("order"), sem("turn"), sem("absorb")
        s_load, s_edges, s_pe, s_dve, s_rank, s_idx = (sem(n) for n in
            ("prep_load", "edge_loads", "prep_pe", "prep_dve", "rank_done", "slots_done"))
        s_asm = sem("records_assembled")
        s_scat = [sem(f"records_scattered_{k}") for k in range(10)]
        s_hpe, s_hdve = sem("hist_pe"), sem("hist_dve")
        s_aload = [sem(f"adj_loaded_{k}") for k in range(2)]
        s_apes, s_afold = sem("adj_multiplied"), sem("adj_folded")

        class Rows:

            def __init__(self, name, each, owner):
                self.sem, self.each, self.owner = sem(name), each, owner

        gathered = Rows("cells_gathered", NG, "tensor")
        flipped = Rows("maxima_flipped", 1, "tensor")
        max_gathered = Rows("maxima_gathered", 1, "tensor")
        summed = Rows("cells_summed", NG, "tensor")
        dve_link = Rows("dve_link", 2 * NG, "vector")
        multiplied = Rows("scores_multiplied", NG, "vector")
        maxed = Rows("cells_maxed", NG, "vector")
        combined = Rows("maxima_combined", 1, "vector")
        row_maxed = Rows("row_maximum", 2, "vector")
        folded = Rows("maxima_folded", 1, "vector")
        added = Rows("row_added", 2, "vector")
        carried = Rows("features_carried", NG, "scalar")
        masked = Rows("masks_ready", NG, "scalar")
        raised = Rows("weights_raised", 1, "scalar")
        staged = Rows("source_rows_staged", 1, "gpsimd")
        parted = Rows("maxima_parted", 4, "gpsimd")
        bounded = Rows("scores_bounded", 2, "gpsimd")
        scaled = Rows("values_scaled", NG, "gpsimd")
        less_high = Rows("values_less_high", NG, "gpsimd")
        high_part = Rows("high_parts", NG, "scalar")
        middle_part = Rows("middle_parts", NG, "scalar")
        weighted = Rows("values_weighted", NG, "gpsimd")
        all_rows = [gathered, flipped, max_gathered, summed, dve_link, multiplied, maxed, combined, row_maxed, folded,
                    added, carried, masked, raised, staged, parted, bounded, scaled, less_high, high_part, middle_part, weighted]
        hot_src = Rows("gate_hot_src", NG, "vector")
        attr_taken = Rows("gate_attributes_taken", NG, "vector")
        mlp_taken = Rows("gate_mlp_taken", NG, "vector")
        nodes_taken = Rows("gate_nodes_taken", NG, "vector")
        valued = Rows("gate_valued", NG, "vector")
        pair_made = Rows("gate_pairs", NG, "vector")
        pair_added = Rows("gate_pairs_added", NG, "vector")
        cut_link = Rows("gate_cutoff", 3, "vector")
        row_added = Rows("gate_row_added", 1, "vector")
        angled = Rows("gate_angles", 1, "vector")
        waved = Rows("gate_cosines", 1, "scalar")
        hot_dst = Rows("gate_hot_dst", NG, "vector")
        table_staged = Rows("gate_table_staged", 1, "gpsimd")
        first_rest = Rows("gate_first_rest", NG, "gpsimd")
        third_part = Rows("gate_third_part", NG, "gpsimd")
        attr_flipped = Rows("gate_attributes_flipped", NG, "tensor")
        src_flipped = Rows("gate_src_flipped", NG, "tensor")
        dst_flipped = Rows("gate_dst_flipped", NG, "tensor")
        hidden = Rows("gate_hidden", NG, "tensor")
        adj_made = Rows("gate_adjacency_made", NG, "tensor")
        looked_up = Rows("gate_looked_up", NG, "tensor")
        scattered = Rows("gate_scattered", NG, "tensor")
        src_taken = Rows("gate_src_taken", NG, "scalar")
        dst_taken = Rows("gate_dst_taken", NG, "scalar")
        src_copied = Rows("gate_src_copied", NG, "scalar")
        activated = Rows("gate_activated", NG, "scalar")
        adj_taken = Rows("gate_adjacency_taken", NG, "scalar")
        first_part = Rows("gate_first_part", NG, "scalar")
        second_part = Rows("gate_second_part", NG, "scalar")
        recs_loaded = Rows("gate_records_loaded", 16, "sync")
        hots_stored = [Rows(f"gate_hots_stored_{g}", 32, "sync") for g in range(NG)]
        all_rows += [hot_src, attr_taken, mlp_taken, nodes_taken, valued, pair_made, pair_added, cut_link, row_added, angled, waved, hot_dst,
                     table_staged, first_rest, third_part, attr_flipped, src_flipped, dst_flipped, hidden, adj_made,
                     looked_up, scattered, src_taken, dst_taken, src_copied, activated, adj_taken, first_part, second_part,
                     recs_loaded, *hots_stored]
        s_cells = [[sem(f"cells_loaded_{p}_{g}") for g in range(NG)] for p in range(2)]

        def scope():
            return ExitStack()

        def sb(stack, name, shape, dt=F32):
            return stack.enter_context(nc.sbuf_tensor(name, shape, dt))

        X = sb(ctx, "X", [P, NB, H])
        HN = sb(ctx, "HN", [P, NB, H])
        ACC = sb(ctx, "ACC", [P, NB, KW])
        SMAX = sb(ctx, "SMAX", [P, NB])
        DEG = sb(ctx, "DEG", [P, NB])
        MULT = sb(ctx, "MULT", [P, NB])
        LOGM = sb(ctx, "LOGM", [P, NB])
        STAT = sb(ctx, "STAT", [P, 4, NB])
        iota_f = sb(ctx, "iota_f", [P, P])
        iota_i = sb(ctx, "iota_i", [P, P], I32)
        part_f = sb(ctx, "part_f", [P, 1])
        part_i = sb(ctx, "part_i", [P, 1], I32)
        ident = sb(ctx, "ident", [P, P])
        ident8 = sb(ctx, "ident8", [P, P], FP8)
        ones8 = sb(ctx, "ones8", [P, 1], FP8)
        ones_row = sb(ctx, "ones_row", [1, P])
        half_pi = sb(ctx, "half_pi", [P, 1])
        zero1 = sb(ctx, "zero1", [P, 1])
        LP = sb(ctx, "LP", [P, 6, L, H])
        GN = sb(ctx, "GN", [P, 2, H])
        WQK = sb(ctx, "WQK", [H, L, 2 * H])
        WM = sb(ctx, "WM", [H, L, H])
        WU = sb(ctx, "WU", [H, L, 2, H])
        F1 = sb(ctx, "F1", [RBF, H])
        F1B = sb(ctx, "F1B", [H, 1])
        F2 = sb(ctx, "F2", [KW, H])
        F2B = sb(ctx, "F2B", [1, H])
        n_extra = sb(ctx, "n_extra", [1, 1], I32)

        psum = ctx.enter_context(nc.psum_tensor("psum", [P, 8 * 512], F32))

        def bank(b, n=1):
            return psum[:, b * 512:(b + n) * 512]

        with scope() as st:
            src_i, dst_i = sb(st, "src_i", [EP, ET], I32), sb(st, "dst_i", [EP, ET], I32)
            tmp_i = sb(st, "tmp_i", [EP, ET], I32)
            fields = sb(st, "fields", [EP, ET, RW - RBF])
            bs_f, bd_f, key_f = (sb(st, n, [EP, ET]) for n in ("bs_f", "bd_f", "key_f"))
            home = sb(st, "home", [EP, ET])
            hist = sb(st, "hist", [NB, NS, NB])
            base = sb(st, "base", [NB, NS, 2, NB])
            cell = sb(st, "cell", [NB, 6, NB])
            cell_i = sb(st, "cell_i", [NB, 2, NB], I32)
            one_bs, one_bd = sb(st, "one_bs", [EP, 2, NS, NB], BF16), sb(st, "one_bd", [EP, 2, NS, NB], BF16)
            one_bd32 = sb(st, "one_bd32", [EP, NS, NB])
            one_bsT = sb(st, "one_bsT", [NB, NS, EP])
            lower = sb(st, "lower", [EP, EP])
            upper = sb(st, "upper", [NB, NB])
            ones49 = sb(st, "ones49", [NB, NB])
            junk = sb(st, "junk", [EP, NS, EP])
            look = sb(st, "look", [EP, NS, 2, NB])
            found = sb(st, "found", [EP, NS, 2])
            rank = sb(st, "rank", [EP, NS])
            slot_a, slot_b, slot_m = (sb(st, n, [EP, NS]) for n in ("slot_a", "slot_b", "slot_m"))
            slot_i = sb(st, "slot_i", [EP, 4, NS], I32)
            attr_in = sb(st, "attr_in", [EP, NS, JB, RBF])
            rec_out = sb(st, "rec_out", [EP, 2, NS, 5, RW])
            zeros = sb(st, "zeros", [P, NB * RW])
        ze_tab = sb(ctx, "ze_tab", [P, NB, 2 * G])
        with scope() as st:
            z_row = sb(st, "z_row", [NELEM, NPAD], I32)
            z_hot = sb(st, "z_hot", [NELEM, NPAD])
            EMB = sb(st, "EMB", [NELEM, 2 * G])
            embT = sb(st, "embT", [G, NELEM])
            adapt_sb = sb(st, "adapt_sb", [G, G])
        with scope() as st:
            TD = sb(st, "TD", [P, 3, NB, DW], BF16)
            TS = sb(st, "TS", [P, 3, NB, KW], BF16)
            with scope() as s2:
                HT = sb(s2, "HT", [H, NPAD])
                AT = sb(s2, "AT", [H, NPAD])
                W1 = sb(s2, "W1", [P, NB, DW])
                W2 = sb(s2, "W2", [P, NB, DW])
            with scope() as s2:
                rec = sb(s2, "rec", [P, GC, RW])
                td_row = sb(s2, "td_row", [P, 3, DW], BF16)
                ts_row = sb(s2, "ts_row", [P, 3, KW], BF16)
                oh = sb(s2, "oh", [P, NG, 3, GC, P], FP8)
                oh_d = sb(s2, "oh_d", [P, GC, P], FP8)
                os32 = sb(s2, "os32", [P, GC, P])
                adj_out = sb(s2, "adj_out", [P, GC, P], BF16)
                attrT = sb(s2, "attrT", [RBF, GC * P])
                act1 = sb(s2, "act1", [H, GC * P])
                src_e = sb(s2, "src_e", [P, GC, G])
                gate = sb(s2, "gate", [P, GC, H])
                cw = sb(s2, "cw", [P, 3, GC])
                val = sb(s2, "val", [P, GC, KW])
                xk = sb(s2, "xk", [P, GC, KW])
                runmax = sb(s2, "runmax", [P, P])
                rowmax = sb(s2, "rowmax", [P, 4])
                smax3 = sb(s2, "smax3", [P, 3], BF16)
                S1 = sb(s2, "S1", [P, 1])
                ES = sb(s2, "ES", [P, 2, 1])
                V1 = sb(s2, "V1", [P, 1, KW])
            with scope() as s2:
                recs_g = sb(s2, "recs_g", [P, 2, NB, RW])
                hots = sb(s2, "hots", [P, NG, 3, GC, P], FP8)
                hots_dst = sb(s2, "hots_dst", [P, NG, GC, P], FP8)
                adjs = sb(s2, "adjs", [P, NG, GC, P], BF16)
                attr_t = sb(s2, "attr_t", [RBF, 2, GC * P])
                act_t = sb(s2, "act_t", [KW, 2, GC * P])
                table_g = sb(s2, "table_g", [P, 2, 3, G], BF16)
                src_g = sb(s2, "src_g", [P, GC, G])
                pairs = sb(s2, "pairs", [P, GC, G])
                pair_sum = sb(s2, "pair_sum", [P, GC])
                gates = sb(s2, "gates", [P, 2, GC, H])
                angle = sb(s2, "angle", [P, NB])
                wave = sb(s2, "wave", [P, NB])
                cutoff = sb(s2, "cutoff", [P, 2, NB])
                vals_g = sb(s2, "vals_g", [P, NG, GC, KW])
                vals3_g = sb(s2, "vals3_g", [P, NG, GC, 3, KW], BF16)
                sum_g = sb(s2, "sum_g", [P, KW])
            with scope() as s2:
                cells = sb(s2, "cells", [P, 2, NG, 3, GC, P], FP8)
                recs = sb(s2, "recs", [P, 2, NG, GC, RW])
                values = sb(s2, "values", [P, 2, NB, KW])
                mask = sb(s2, "mask", [P, 2, GC, P])
                values3 = sb(s2, "values3", [P, NB, 3, KW], BF16)
                xks = sb(s2, "xks", [P, 2, GC, KW])
                score = sb(s2, "score", [P, 2, NB])
                slot_max = sb(s2, "slot_max", [P, GC, P])
                slot_top = sb(s2, "slot_top", [P, P])
                row_sum = sb(s2, "row_sum", [P, KW])
                top = sb(s2, "top", [P, 4])
                top3 = sb(s2, "top3", [P, 3], BF16)
                edge_top = sb(s2, "edge_top", [P, 3, NB])
                ts2 = sb(s2, "ts2", [P, 2, 3, KW], BF16)
        with scope() as st:
            AJ = sb(st, "AJ", [P, 2, NB, 4 * P], BF16)
            dinv = sb(st, "dinv", [P, NB])
            g_f = sb(st, "g_f", [P, NB, H])
            g_r = sb(st, "g_r", [P, NB, H])
            g3 = sb(st, "g3", [P, NB, 3, H], BF16)
            mm = sb(st, "mm", [P, NB, H])
            rec_l = sb(st, "rec_l", [P, RW])
            ohs_l, ohd_l, ohsT_l = (sb(st, n, [P, P]) for n in ("ohs_l", "ohd_l", "ohsT_l"))
            val_l = sb(st, "val_l", [P, H])

        block = ctx.enter_context(nc.Block())

        def program(name, e):
            count = [0]

            def serial(steps, wait_last=False):
                for who, fn, inc in steps:
                    if who == name:
                        e.wait_ge(order, count[0])
                        fn(e).then_inc(order, inc)
                    count[0] += inc

            def barrier():
                for who in ENGINES:
                    if who == name:
                        e.wait_ge(order, count[0])
                        e.drain().then_inc(order, 1)
                    count[0] += 1
                e.wait_ge(order, count[0])

            turns = e.alloc_register("turns_" + name)
            e.reg_mov(turns, 1)
            if name == "sync":
                e.sem_inc(turn, 1)

            row = e.alloc_register("row_" + name)
            e.reg_mov(row, 2)
            loads = [e.alloc_register(f"loads_{k}_{name}") for k in range(2)]
            for k in range(2):
                e.reg_mov(loads[k], 0)
            for r in all_rows:
                if r.owner == name:
                    e.sem_inc(r.sem, 2 * r.each)

            past_end = [0]

            def of_row(what, c, back=0, plain=True):
                back -= past_end[0]
                e.wait_ge(what.sem, e.snap(row, min_val=2, max_val=1 << 20) * what.each + (c - back * what.each))
                if plain:
                    e.sem_inc(absorb, 1)

            def in_turn(steps):
                off = 0
                for who, fn, inc in steps:
                    if who == name:
                        e.wait_ge(turn, e.snap(turns, min_val=1, max_val=1 << 29) + off)
                        e.sem_inc(absorb, 1)
                        fn(e).then_inc(turn, inc)
                    off += inc
                e.reg_add(turns, turns, off)

            def in_turn_end():
                e.wait_ge(turn, e.snap(turns, min_val=1, max_val=1 << 29))
                e.sem_inc(absorb, 1)

            def sy(fn): return ("sync", fn, 16)
            def po(fn): return ("gpsimd", fn, 1)
            def v(fn): return ("vector", fn, 1)
            def a(fn): return ("scalar", fn, 1)
            def t(fn): return ("tensor", fn, 1)

            def many(fns):
                def run(e):
                    for f in fns:
                        last = f(e)
                    return last
                return run

            def bc(ap, shape):
                return ap.broadcast_to(shape)

            def load_all():
                flat = lambda w: w.rearrange("l h -> (l h)").partition_broadcast(P)
                vec = lambda w: w.partition_broadcast(P)
                col = lambda w: w.rearrange("(h o) -> h o", o=1)
                x_main = x[0:(NB - 1) * P, :].rearrange("(b p) h -> p b h", p=P)
                steps = [
                    v(lambda e: e.memset(X[:, :, :], 0.0)),
                    v(lambda e: e.memset(MULT[:, :], 1.0)),
                    sy(lambda e: e.dma_start(X[:, 0:NB - 1, :], x_main)),
                    sy(lambda e: e.dma_start(X[0:TAIL, NB - 1, :], x[(NB - 1) * P:N, :])),
                    sy(lambda e: e.dma_start(MULT[0:TAIL, NB - 1:NB], node_vec[(NB - 1) * P:N].rearrange("(p o) -> p o", o=1))),
                ]
                def mult_main(e):
                    with nc.allow_non_contiguous_dma(reason="one column of node values per block"):
                        return e.dma_start(MULT[:, 0:NB - 1], node_vec[0:(NB - 1) * P].rearrange("(b p) -> p b", p=P))
                steps.append(sy(mult_main))
                for n, w in enumerate((gq, bq, gk, bk, go, bo)):
                    steps.append(sy(lambda e, n=n, w=w: e.dma_start(LP[:, n, :, :].rearrange("p l h -> p (l h)"), flat(w))))
                steps += [
                    sy(lambda e: e.dma_start(GN[:, 0, :], vec(gn))), sy(lambda e: e.dma_start(GN[:, 1, :], vec(bn))),
                    sy(lambda e: e.dma_start(WQK[:, :, 0:H], Wq.rearrange("l i o -> i l o"))),
                    sy(lambda e: e.dma_start(WQK[:, :, H:2 * H], Wk.rearrange("l i o -> i l o"))),
                    sy(lambda e: e.dma_start(WM[:, :, :], Wm.rearrange("l i o -> i l o"))),
                    sy(lambda e: e.dma_start(WU[:, :, 0, :], Wu[:, 0:H, :].rearrange("l i o -> i l o"))),
                    sy(lambda e: e.dma_start(WU[:, :, 1, :], Wu[:, H:2 * H, :].rearrange("l i o -> i l o"))),
                    sy(lambda e: e.dma_start(F1[:, :], F1W)), sy(lambda e: e.dma_start(F2[0:H, :], F2W)),
                    sy(lambda e: e.dma_start(F2[H:KW, :], F2b.rearrange("(o h) -> o h", o=1))),
                    sy(lambda e: e.dma_start(F1B[:, :], col(F1b))),
                    sy(lambda e: e.dma_start(F2B[:, :], F2b.rearrange("(o h) -> o h", o=1))),
                    po(lambda e: e.iota(iota_i[:, :], pattern=[[1, P]], base=1, channel_multiplier=0)),
                    po(lambda e: e.iota(part_i[:, :], pattern=[[0, 1]], base=0, channel_multiplier=1)),
                    v(lambda e: e.tensor_copy(iota_f[:, :], iota_i[:, :])),
                    v(lambda e: e.tensor_copy(part_f[:, :], part_i[:, :])),
                    v(lambda e: e.tensor_scalar(ident[:, :], iota_f[:, :], 1.0, part_f[:, 0:1], ALU.subtract, ALU.is_equal)),
                    v(lambda e: e.tensor_copy(ident8[:, :], ident[:, :], saturate=False)),
                    v(lambda e: e.tensor_copy(ones8[:, :], iota_f[:, 0:1], saturate=False)),
                    v(lambda e: e.memset(ones_row[:, :], 1.0)),
                    v(lambda e: e.memset(half_pi[:, :], HALF_PI)),
                    v(lambda e: e.memset(zero1[:, :], 0.0)),
                    v(lambda e: e.memset(DEG[:, :], 1.0)),
                ]
                serial(steps)

            def count_cells():
                serial([
                    v(lambda e: e.memset(zeros[:, :], 0.0)),
                    sy(lambda e: e.dma_start(src_i[:, :], src.rearrange("(p t) -> p t", t=ET))),
                    sy(lambda e: e.dma_start(dst_i[:, :], dst.rearrange("(p t) -> p t", t=ET))),
                    sy(lambda e: e.dma_start(home[:, :], edge_weight.rearrange("(p t) -> p t", t=ET))),
                    v(lambda e: e.tensor_copy(fields[:, :, 2], home[:, :])),
                ])
                for raw, local, block_f, fb in ((src_i, 0, bs_f, 3), (dst_i, 1, bd_f, 4)):
                    serial([
                        v(lambda e, raw=raw: e.tensor_scalar(tmp_i[:, :], raw[:, :], P - 1, None, ALU.bitwise_and)),
                        v(lambda e, local=local: e.tensor_scalar(fields[:, :, local], tmp_i[:, :], 1.0, None, ALU.add)),
                        v(lambda e, raw=raw: e.tensor_scalar(tmp_i[:, :], raw[:, :], 7, None, ALU.logical_shift_right)),
                        v(lambda e, block_f=block_f: e.tensor_copy(block_f[:, :], tmp_i[:, :])),
                        v(lambda e, fb=fb: e.tensor_copy(fields[:, :, fb].bitcast(I32), tmp_i[:, :])),
                    ])
                serial([
                    v(lambda e: e.scalar_tensor_tensor(key_f[:, :], bs_f[:, :], float(NB), bd_f[:, :], ALU.mult, ALU.add)),
                    v(lambda e: e.scalar_tensor_tensor(home[:, :], bs_f[:, :], float(NB * P), bd_f[:, :], ALU.mult, ALU.add)),
                    v(lambda e: e.tensor_scalar(lower[:, :], iota_f[0:EP, 0:EP], 1.0, part_f[0:EP, 0:1], ALU.subtract, ALU.is_lt)),
                    v(lambda e: e.tensor_scalar(upper[:, :], iota_f[0:NB, 0:NB], 1.0, part_f[0:NB, 0:1], ALU.subtract, ALU.is_gt)),
                    v(lambda e: e.memset(ones49[:, :], 1.0)),
                ])
                HG = NS
                groups = ET // HG
                iota49 = lambda n: iota_f[0:EP, 0:NB].unsqueeze(1).broadcast_to([EP, n, NB])
                if name == "vector":
                    e.tensor_scalar(iota_f[:, :], iota_f[:, :], 1.0, None, ALU.subtract).then_inc(s_hdve, 1)
                    e.wait_ge(s_hdve, 1)
                    for g in range(groups):
                        if g >= 2:
                            e.wait_ge(s_hpe, g - 1)
                        c0 = g * HG
                        e.tensor_tensor(one_bs[:, g % 2], iota49(HG), bs_f[:, c0:c0 + HG].unsqueeze(2).broadcast_to([EP, HG, NB]), ALU.is_equal)
                        e.tensor_tensor(one_bd[:, g % 2], iota49(HG), bd_f[:, c0:c0 + HG].unsqueeze(2).broadcast_to([EP, HG, NB]), ALU.is_equal).then_inc(s_hdve, 1)
                    e.wait_ge(s_hpe, groups)
                if name == "tensor":
                    for g in range(groups):
                        e.wait_ge(s_hdve, g + 2)
                        for k in range(HG):
                            c = g * HG + k
                            s, i = c // SC, c % SC
                            last = e.matmul(bank(0)[0:NB, s * NB:(s + 1) * NB], one_bs[:, g % 2, k, :], one_bd[:, g % 2, k, :],
                                            start=i == 0, stop=i == SC - 1)
                        last.then_inc(s_hpe, 1)
                tot, over, chunks, before = cell[:, 0], cell[:, 1], cell[:, 2], cell[:, 3]
                steps = [
                    v(lambda e: e.tensor_copy(hist[:, :, :], bank(0)[0:NB, 0:NS * NB].rearrange("p (s b) -> p s b", s=NS))),
                    v(lambda e: e.tensor_reduce(tot, hist[:, :, :].rearrange("p s b -> p b s"), AX.X, ALU.add)),
                    v(lambda e: e.tensor_scalar(over, tot, float(CAP), 0.0, ALU.subtract, ALU.max)),
                    v(lambda e: e.tensor_scalar(cell_i[:, 0], over, float(P - 1), None, ALU.add)),
                    v(lambda e: e.tensor_scalar(cell_i[:, 1], cell_i[:, 0], 7, None, ALU.logical_shift_right)),
                    v(lambda e: e.tensor_copy(chunks, cell_i[:, 1])),
                    v(lambda e: e.tensor_tensor_scan(before, chunks, chunks, 0.0, ALU.add, ALU.bypass)),
                    t(lambda e: e.matmul(bank(1)[0:NB, 0:1], upper[:, :], before[:, NB - 1:NB], start=True, stop=True)),
                    t(lambda e: e.matmul(bank(2)[0:NB, 0:1], ones49[:, :], before[:, NB - 1:NB], start=True, stop=True)),
                    v(lambda e: e.tensor_copy(n_extra[0:1, 0:1], bank(2)[0:1, 0:1])),
                    v(lambda e: e.tensor_tensor(before, before, chunks, ALU.subtract)),
                    v(lambda e: e.tensor_scalar(before, before, bank(1)[0:NB, 0:1], float(P), ALU.add, ALU.mult)),
                    v(lambda e: e.tensor_scalar(before, before, float(GRID - CAP), None, ALU.add)),
                    v(lambda e: e.memset(base[:, 0, 0, :], 0.0)),
                ]
                for s in range(NS):
                    steps.append(v(lambda e, s=s: e.tensor_copy(base[:, s, 1, :], before)))
                    if s:
                        steps.append(v(lambda e, s=s: e.tensor_tensor(base[:, s, 0, :], base[:, s - 1, 0, :], hist[:, s - 1, :], ALU.add)))
                for b in range(NB):
                    steps.append(sy(lambda e, b=b: e.dma_start(rec_rows[b], zeros[:, :])))
                serial(steps)

            def extra_count():
                e.wait_ge(order, count[0])
                e.sem_inc(absorb, 1)
                return e.value_load(n_extra[0:1, 0:1], min_val=0, max_val=NOV)

            def fill_extra():
                barrier()
                n = extra_count()
                with e.If(n > 0):
                    with e.Fori(0, n) as j:
                        in_turn([sy(lambda e: e.dma_start(rec_extra[ds(j, 1), :, :].rearrange("o p w -> (o p) w"), zeros[:, 0:RW]))])
                    in_turn_end()
                barrier()

            def place_edges():
                ITER = SC
                ident_e = ident[0:EP, 0:EP]
                attr = edge_attr_40.rearrange("(p s i) r -> p s (i r)", s=NS, i=SC)
                fields_s = fields[:, :, :].rearrange("p (s i) f -> p s i f", s=NS)
                by_stream = lambda arr: arr[:, :].rearrange("p (s i) -> p s i", s=NS)
                keyT, bsT, found_ps, hist_ps = bank(0, 2), bank(2, 2), bank(4, 2), bank(6)

                def scattered(i):
                    e.wait_ge(s_scat[i % 10], 16 * NS * (i // 10 + 1))

                at4 = lambda ps, s, w, tot=4: (s // 4) * 512 + (s % 4) * w
                if name == "sync":
                    for b in range(ITER // JB):
                        if b:
                            e.wait_ge(s_asm, 2 * b)
                        e.dma_start(attr_in[:, :, :, :].rearrange("p s i r -> p s (i r)"),
                                    attr[:, :, b * JB * RBF:(b + 1) * JB * RBF]).then_inc(s_edges, 16)
                if name == "scalar":
                    for b in range(ITER // JB):
                        e.wait_ge(s_edges, 16 * (b + 1))
                        for h in range(2):
                            n = 2 * b + h
                            if n >= 2:
                                for i in range(5 * (n - 2), 5 * (n - 1)):
                                    scattered(i)
                            for k in range(5):
                                j = 5 * h + k
                                e.copy(rec_out[:, n % 2, :, k, 0:RBF], attr_in[:, :, j, :])
                                last = e.copy(rec_out[:, n % 2, :, k, RBF:RW], fields_s[:, :, b * JB + j, :])
                            last.then_inc(s_asm, 1)
                if name == "tensor":
                    for i in range(ITER):
                        if i:
                            e.wait_ge(s_rank, i)
                        for s in range(NS):
                            o = at4(None, s, EP)
                            col = s * SC + i
                            e.transpose(keyT[0:EP, o:o + EP], key_f[:, col:col + 1].broadcast_to([EP, EP]), ident_e)
                            last = e.transpose(bsT[0:NB, o:o + EP], bs_f[:, col:col + 1].broadcast_to([EP, NB]), ident_e)
                        last.then_inc(s_pe, 1)
                        e.wait_ge(s_dve, 2 * i + 1)
                        for s in range(NS):
                            e.matmul(hist_ps[0:NB, s * NB:(s + 1) * NB], one_bs[:, i % 2, s, :], one_bd[:, i % 2, s, :], start=True, stop=True)
                        for s in range(NS):
                            o = at4(None, s, 2 * NB)
                            last = e.matmul(found_ps[0:EP, o:o + 2 * NB], one_bsT[:, s, :], base[:, s, :, :].rearrange("p a b -> p (a b)"), start=True, stop=True)
                        last.then_inc(s_pe, 1)
                if name == "vector":
                    iota49 = iota_f[0:EP, 0:NB].unsqueeze(1).broadcast_to([EP, NS, NB])
                    for i in range(ITER):
                        bsv = by_stream(bs_f)[:, :, i:i + 1].broadcast_to([EP, NS, NB])
                        bdv = by_stream(bd_f)[:, :, i:i + 1].broadcast_to([EP, NS, NB])
                        e.tensor_tensor(one_bs[:, i % 2], iota49, bsv, ALU.is_equal)
                        e.tensor_tensor(one_bd[:, i % 2], iota49, bdv, ALU.is_equal)
                        e.tensor_tensor(one_bd32[:, :, :], iota49, bdv, ALU.is_equal)
                        e.wait_ge(s_pe, 2 * i + 1)
                        for h in range(2):
                            last = e.tensor_scalar(one_bsT[:, 4 * h:4 * h + 4, :].rearrange("p s e -> p (s e)"), bsT[0:NB, h * 512:h * 512 + 4 * EP],
                                                   part_f[0:NB, 0:1], None, ALU.is_equal)
                        last.then_inc(s_dve, 1)
                        for s in range(NS):
                            o = at4(None, s, EP)
                            last = e.scalar_tensor_tensor(junk[:, s, :], keyT[0:EP, o:o + EP], key_f[:, s * SC + i:s * SC + i + 1], lower[:, :],
                                                          ALU.is_equal, ALU.mult, accum_out=rank[:, s:s + 1])
                        last.then_inc(s_rank, 1)
                        e.wait_ge(s_pe, 2 * i + 2)
                        for h in range(2):
                            e.tensor_tensor(look[:, 4 * h:4 * h + 4, :, :], found_ps[0:EP, h * 512:h * 512 + 8 * NB].rearrange("p (s a b) -> p s a b", s=4, a=2),
                                            one_bd32[:, 4 * h:4 * h + 4, :].unsqueeze(2).broadcast_to([EP, 4, 2, NB]), ALU.mult)
                        e.tensor_tensor(base[:, :, 0, :], base[:, :, 0, :], hist_ps[0:NB, 0:NS * NB].rearrange("p (s b) -> p s b", s=NS), ALU.add).then_inc(s_dve, 1)
                        e.wait_ge(s_dve, 2 * i + 2)
                        c = [0]
                        def link(ins):
                            c[0] += 1
                            ins.then_inc(s_load, 1)
                            e.wait_ge(s_load, 6 * i + c[0])
                        link(e.tensor_reduce(found[:, :, :], look[:, :, :, :], AX.X, ALU.add))
                        link(e.tensor_tensor(slot_m[:, :], rank[:, :], found[:, :, 0], ALU.add))
                        link(e.scalar_tensor_tensor(slot_a[:, :], slot_m[:, :], float(NB), by_stream(home)[:, :, i], ALU.mult, ALU.add))
                        link(e.tensor_tensor(slot_b[:, :], slot_m[:, :], found[:, :, 1], ALU.add))
                        link(e.tensor_tensor(slot_b[:, :], slot_b[:, :], slot_a[:, :], ALU.subtract))
                        link(e.scalar_tensor_tensor(slot_b[:, :], slot_m[:, :], float(CAP), slot_b[:, :], ALU.is_ge, ALU.mult))
                        if i >= 4:
                            scattered(i - 4)
                        e.tensor_tensor(slot_i[:, i % 4, :], slot_a[:, :], slot_b[:, :], ALU.add).then_inc(s_idx, 1)
                if name == "gpsimd":
                    for i in range(ITER):
                        e.wait_ge(s_idx, i + 1)
                        e.wait_ge(s_asm, i // 5 + 1)
                        for s in range(NS):
                            e.indirect_dma_start(REC[:, :], bass.IndirectOffsetOnAxis(ap=slot_i[:, i % 4, s:s + 1], axis=0),
                                                 rec_out[:, (i // 5) % 2, s, i % 5, :], None).then_inc(s_scat[i % 10], 16)
                    for i in range(ITER - 10, ITER):
                        scattered(i)
                barrier()
                serial([v(lambda e: e.tensor_scalar(iota_f[:, :], iota_f[:, :], 1.0, None, ALU.add))])

            def wide(ap, w=H):
                return ap.unsqueeze(2).broadcast_to([P, NB, w])

            def every(ap, w=H):
                return ap.unsqueeze(1).broadcast_to([P, NB, w])

            def normalise(to, of, tmp, g=None, b=None):
                mean, var = STAT[:, 0, :], STAT[:, 1, :]
                steps = [
                    v(lambda e: e.tensor_reduce(mean, of, AX.X, ALU.add)),
                    v(lambda e: e.tensor_scalar(mean, mean, 1.0 / H, None, ALU.mult)),
                    v(lambda e: e.tensor_tensor(to, of, wide(mean), ALU.subtract)),
                    v(lambda e: e.tensor_tensor(tmp, to, to, ALU.mult)),
                    v(lambda e: e.tensor_reduce(var, tmp, AX.X, ALU.add)),
                    v(lambda e: e.tensor_scalar(var, var, 1.0 / H, 1e-5, ALU.mult, ALU.add)),
                    a(lambda e: e.activation(mean, var, ACT.Sqrt)),
                    v(lambda e: e.reciprocal(var, mean)),
                    v(lambda e: e.tensor_tensor(to, to, wide(var), ALU.mult)),
                ]
                if g is not None:
                    steps += [v(lambda e: e.tensor_tensor(to, to, every(g), ALU.mult)),
                              v(lambda e: e.tensor_tensor(to, to, every(b), ALU.add))]
                return steps

            def split(parts, of, rest):
                return [
                    a(lambda e: e.copy(parts[0], of)),
                    v(lambda e: e.tensor_tensor(rest, of, parts[0], ALU.subtract)),
                    a(lambda e: e.copy(parts[1], rest)),
                    v(lambda e: e.tensor_tensor(parts[2], rest, parts[1], ALU.subtract)),
                ]

            def transposed(to, of):
                steps = []
                for b0 in range(0, NB, 16):
                    n = min(16, NB - b0)
                    steps += [
                        t(many([lambda e, b0=b0, k=k: e.transpose(bank(0, 4)[0:H, k * P:(k + 1) * P], of[:, b0 + k, 0:H], ident[:, :])
                                for k in range(n)])),
                        a(lambda e, b0=b0, n=n: e.copy(to[:, b0 * P:(b0 + n) * P], bank(0, 4)[0:H, 0:n * P])),
                    ]
                return steps

            def per_block(to, width, products):
                fit = 512 // width
                steps = []
                for b0 in range(0, NB, 8 * fit):
                    n = min(8 * fit, NB - b0)
                    spot = lambda k: bank(k // fit)[:, (k % fit) * width:(k % fit + 1) * width]
                    steps.append(t(many([
                        lambda e, b=b0 + k, k=k, m=m: e.matmul(spot(k), products[m][0](b), products[m][1], start=m == 0, stop=m == len(products) - 1)
                        for k in range(n) for m in range(len(products))])))
                    steps.append(a(many([
                        lambda e, b=b0 + j * fit, j=j, c=min(fit, n - j * fit):
                            e.copy(to[:, b:b + c, 0:width], bank(j)[:, 0:c * width].rearrange("p (b w) -> p b w", w=width))
                        for j in range(-(-n // fit))])))
                return steps

            def embed():
                cols = lambda b: z_hot[:, b * P:(b + 1) * P]
                serial([
                    v(lambda e: e.memset(z_row[:, :], 0)),
                    sy(lambda e: e.dma_start(z_row[:, 0:N], node_type_119.partition_broadcast(NELEM))),
                    sy(lambda e: e.dma_start(EMB[:, 0:G], emb)),
                    sy(lambda e: e.dma_start(adapt_sb[:, :], adapt)),
                    v(lambda e: e.tensor_scalar(z_hot[:, :], z_row[:, :], part_f[0:NELEM, 0:1], None, ALU.is_equal)),
                    t(lambda e: e.transpose(bank(0)[0:G, 0:NELEM], EMB[:, 0:G], ident[0:NELEM, 0:NELEM])),
                    a(lambda e: e.copy(embT[:, :], bank(0)[0:G, 0:NELEM])),
                    t(lambda e: e.matmul(bank(0)[0:NELEM, 0:G], embT[:, :], adapt_sb[:, :], start=True, stop=True)),
                    a(lambda e: e.copy(EMB[:, G:2 * G], bank(0)[0:NELEM, 0:G])),
                    *per_block(ze_tab, 2 * G, [(cols, EMB[:, :])]),
                ])

            def first_tables():
                serial([
                    *normalise(HN[:, :, :], X[:, :, :], W1[:, :, 0:H]),
                    v(lambda e: e.tensor_scalar(HN[:, :, :], HN[:, :, :], 0.0, None, ALU.max)),
                    v(lambda e: e.tensor_scalar(LOGM[:, :], MULT[:, :], 1.0, None, ALU.max)),
                    a(lambda e: e.activation(LOGM[:, :], LOGM[:, :], ACT.Ln)),
                    v(lambda e: e.tensor_tensor(W1[:, :, 0:H], HN[:, :, :], wide(MULT[:, :]), ALU.mult)),
                    v(lambda e: e.tensor_copy(W1[:, :, H:KW], MULT[:, :].unsqueeze(2))),
                    v(lambda e: e.tensor_copy(W1[:, :, KW:GW], ze_tab[:, :, G:2 * G])),
                    *split([TD[:, k, :, 0:GW] for k in range(3)], W1[:, :, 0:GW], W2[:, :, 0:GW]),
                    *split([TS[:, k, :, 0:G] for k in range(3)], ze_tab[:, :, 0:G], W2[:, :, 0:G]),
                    v(lambda e: e.memset(ACC[:, :, :], 0.0)),
                ])

            def after_gate():
                tot = STAT[:, 2, :]
                serial([
                    v(lambda e: e.tensor_scalar(tot, ACC[:, :, H], 1e-8, None, ALU.max)),
                    v(lambda e: e.reciprocal(STAT[:, 3, :], tot)),
                    v(lambda e: e.tensor_tensor(W1[:, :, 0:H], ACC[:, :, 0:H], wide(STAT[:, 3, :]), ALU.mult)),
                    v(lambda e: e.tensor_tensor(W1[:, :, 0:H], W1[:, :, 0:H], HN[:, :, :], ALU.add)),
                    *normalise(HN[:, :, :], W1[:, :, 0:H], W2[:, :, 0:H], GN[:, 0, :], GN[:, 1, :]),
                ])

            def layer_tables(l):
                serial([
                    *transposed(HT[:, :], HN[:, :, :]),
                    *per_block(W1[:, :, :], 2 * H, [(lambda b: HT[:, b * P:(b + 1) * P], WQK[:, l, :])]),
                    *normalise(W2[:, :, 0:H], W1[:, :, 0:H], W2[:, :, H:2 * H], LP[:, 0, l, :], LP[:, 1, l, :]),
                    v(lambda e: e.memset(W2[:, :, H:KW], 1.0)),
                ])
                serial([
                    a(lambda e: e.copy(TS[:, 0, :, :], W2[:, :, 0:KW])),
                    v(lambda e: e.tensor_tensor(W2[:, :, 0:KW], W2[:, :, 0:KW], TS[:, 0, :, :], ALU.subtract)),
                    a(lambda e: e.copy(TS[:, 1, :, :], W2[:, :, 0:KW])),
                    v(lambda e: e.tensor_tensor(TS[:, 2, :, :], W2[:, :, 0:KW], TS[:, 1, :, :], ALU.subtract)),
                    *normalise(W2[:, :, 0:H], W1[:, :, H:2 * H], W2[:, :, H:2 * H], LP[:, 2, l, :], LP[:, 3, l, :]),
                    v(lambda e: e.tensor_copy(W2[:, :, H:KW], LOGM[:, :].unsqueeze(2))),
                    v(lambda e: e.tensor_copy(W2[:, :, KW:DW], HN[:, :, :])),
                    *split([TD[:, k, :, :] for k in range(3)], W2[:, :, :], W1[:, :, :]),
                    v(lambda e: e.memset(ACC[:, :, :], 0.0)),
                    v(lambda e: e.memset(SMAX[:, :], -BIG)),
                ])

            def layer_update(l):
                den = STAT[:, 2, :]
                steps = [
                    v(lambda e: e.tensor_scalar(den, ACC[:, :, H], 1e-10, None, ALU.add)),
                    v(lambda e: e.reciprocal(STAT[:, 3, :], den)),
                    v(lambda e: e.tensor_tensor(W1[:, :, 0:H], ACC[:, :, 0:H], wide(STAT[:, 3, :]), ALU.mult)),
                    *transposed(HT[:, :], W1[:, :, 0:H]),
                ]
                for c in range(0, NPAD, 4 * 512):
                    n = min(4 * 512, NPAD - c)
                    steps += [
                        t(many([lambda e, c=c, k=k, w=min(512, n - k): e.matmul(bank(0, 4)[0:H, k:k + w], WM[:, l, :], HT[:, c + k:c + k + w], start=True, stop=True)
                                for k in range(0, n, 512)])),
                        a(lambda e, c=c, n=n: e.copy(AT[:, c:c + n], bank(0, 4)[0:H, 0:n])),
                    ]
                steps += [
                    *transposed(HT[:, :], HN[:, :, :]),
                    *per_block(W1[:, :, :], H, [(lambda b: HT[:, b * P:(b + 1) * P], WU[:, l, 0, :]),
                                                (lambda b: AT[:, b * P:(b + 1) * P], WU[:, l, 1, :])]),
                    v(lambda e: e.scalar_tensor_tensor(W2[:, :, 0:H], W1[:, :, 0:H], 0.01, W1[:, :, 0:H], ALU.mult, ALU.max)),
                    v(lambda e: e.tensor_tensor(W1[:, :, 0:H], W2[:, :, 0:H], HN[:, :, :], ALU.add)),
                    *normalise(HN[:, :, :], W1[:, :, 0:H], W2[:, :, 0:H], LP[:, 4, l, :], LP[:, 5, l, :]),
                ]
                serial(steps)

            def bd_of(bd, k, n=1):
                return slice(bd + k, bd + k + n) if isinstance(bd, int) else ds(bd, n)

            def build_one_hots(n, ohg):
                spots = bank(0, 2)
                where = lambda f: rec[:, 0:n, f:f + 1].broadcast_to([P, n, P])
                iotas = iota_f[:, :].unsqueeze(1).broadcast_to([P, n, P])
                flip = lambda of: t(many([lambda e, c=c: e.matmul(spots[:, c * P:(c + 1) * P], of[:, c, :], ident8[:, :], start=True, stop=True) for c in range(n)]))
                take = lambda k: a(lambda e: e.activation(ohg[:, k, 0:n, :], spots[:, 0:n * P].rearrange("p (c e) -> p c e", c=n), ACT.Copy, saturate=False))
                return [
                    v(lambda e: e.tensor_tensor(ohg[:, 2, 0:n, :], iotas, where(F_SRC), ALU.is_equal, saturate=False)),
                    v(lambda e: e.tensor_tensor(oh_d[:, 0:n, :], iotas, where(F_DST), ALU.is_equal, saturate=False)),
                    flip(ohg[:, 2, :, :]), take(0), flip(oh_d[:, :, :]), take(1),
                ]

            def gather(n, spot, hot, rows, width):
                return t(many([lambda e, c=c, k=k: e.matmul(spot(c), hot[:, c, :], rows(c, k)[:, 0:width], start=k == 0, stop=k == 2)
                               for c in range(n) for k in range(3)]))

            def stage_src(bs, w=KW):
                return v(lambda e: e.tensor_copy(ts_row[:, :, 0:w], TS[:, :, ds(bs, 1), 0:w].rearrange("p k o w -> p k (o w)")))

            def stage_dst(bd, w=DW):
                return v(lambda e: e.tensor_copy(td_row[:, :, 0:w], TD[:, :, ds(bd, 1), 0:w].rearrange("p k o w -> p k (o w)")))

            def dst_rows(bd):
                return (lambda c, k: TD[:, k, bd + c, :]) if isinstance(bd, int) else (lambda c, k: td_row[:, k, :])

            src_rows = lambda c, k: ts_row[:, k, :]

            def scatter(n, hots, vals, spot):
                return t(many([lambda e, c=c: e.matmul(spot, hots[:, c, :], vals[:, c, :], start=c == 0, stop=c == n - 1) for c in range(n)]))

            d_spot = lambda c: bank(2, 2)[:, c * P:c * P + DW]
            d_all = lambda n: bank(2, 2)[:, 0:GC * P].rearrange("p (c w) -> p c w", w=P)[:, 0:n, :]
            q_spot = lambda c: bank(4)[:, c * KW:(c + 1) * KW]
            q_all = lambda n, w=KW: bank(4)[:, 0:n * KW].rearrange("p (c w) -> p c w", w=KW)[:, :, 0:w]

            def gate_values(n, ohg, bs, bd):
                both = range(0, n * P, 512)
                return [
                    t(many([lambda e, c=c: e.transpose(bank(0, 2)[0:RBF, c * P:(c + 1) * P], rec[:, c, 0:RBF], ident[:, :]) for c in range(n)])),
                    v(lambda e: e.tensor_copy(attrT[:, 0:n * P], bank(0, 2)[0:RBF, 0:n * P])),
                    t(many([lambda e, k=k: e.matmul(bank(0, 2)[0:H, k:min(k + 512, n * P)], F1[:, :], attrT[:, k:min(k + 512, n * P)], start=True, stop=True)
                            for k in both])),
                    a(lambda e: e.activation(act1[:, 0:n * P], bank(0, 2)[0:H, 0:n * P], ACT.Silu, bias=F1B[:, 0:1])),
                    t(many([f for c in range(n) for f in (
                        lambda e, c=c: e.matmul(bank(5)[:, c * H:(c + 1) * H], act1[:, c * P:(c + 1) * P], F2[0:H, :], start=True, stop=False),
                        lambda e, c=c: e.matmul(bank(5)[:, c * H:(c + 1) * H], ones_row[:, :], F2B[:, :], start=False, stop=True))])),
                    gather(n, lambda c: d_spot(c)[:, 0:GW], ohg[:, 1], dst_rows(bd), GW),
                    gather(n, lambda c: q_spot(c)[:, 0:G], ohg[:, 0], src_rows, G),
                    a(lambda e: e.copy(src_e[:, 0:n, :], q_all(n, G))),
                    v(lambda e: e.tensor_tensor(src_e[:, 0:n, :], src_e[:, 0:n, :], d_all(n)[:, :, KW:GW], ALU.mult)),
                    v(lambda e: e.tensor_reduce(cw[:, 2, 0:n], src_e[:, 0:n, :], AX.X, ALU.add)),
                    v(lambda e: e.tensor_tensor(gate[:, 0:n, :], bank(5)[:, 0:n * H].rearrange("p (c h) -> p c h", h=H),
                                                cw[:, 2, 0:n].unsqueeze(2).broadcast_to([P, n, H]), ALU.add)),
                    v(lambda e: e.tensor_tensor(gate[:, 0:n, :], gate[:, 0:n, :], d_all(n)[:, :, 0:H], ALU.mult)),
                    v(lambda e: e.scalar_tensor_tensor(cw[:, 0, 0:n], rec[:, 0:n, F_W], -1.0, rec[:, 0:n, F_W], ALU.mult, ALU.max)),
                    v(lambda e: e.tensor_scalar(cw[:, 0, 0:n], cw[:, 0, 0:n], CUT, None, ALU.min)),
                    a(lambda e: e.activation(cw[:, 1, 0:n], cw[:, 0, 0:n], ACT.Sin, bias=half_pi[:, 0:1], scale=-2 * HALF_PI / CUT)),
                    v(lambda e: e.tensor_scalar(cw[:, 1, 0:n], cw[:, 1, 0:n], 0.5, 0.5, ALU.mult, ALU.add)),
                    v(lambda e: e.scalar_tensor_tensor(cw[:, 0, 0:n], rec[:, 0:n, F_W], CUT, cw[:, 1, 0:n], ALU.is_lt, ALU.mult)),
                    v(lambda e: e.tensor_tensor(val[:, 0:n, 0:H], gate[:, 0:n, :], cw[:, 0, 0:n].unsqueeze(2).broadcast_to([P, n, H]), ALU.mult)),
                    v(lambda e: e.tensor_copy(val[:, 0:n, H:KW], d_all(n)[:, :, H:KW])),
                    a(lambda e: e.copy(os32[:, 0:n, :], ohg[:, 2, 0:n, :])),
                    scatter(n, os32, val, bank(6)[:, 0:KW]),
                    v(lambda e: e.tensor_tensor(ACC[:, ds(bs, 1), :], ACC[:, ds(bs, 1), :], bank(6)[:, 0:KW].unsqueeze(1), ALU.add)),
                ]

            def degrees(n, bd):
                return [
                    t(many([lambda e, c=c: e.matmul(bank(7)[:, c:c + 1], oh_d[:, c, :], ones8[:, :], start=True, stop=True) for c in range(n)])),
                    v(lambda e: e.tensor_tensor(DEG[:, bd_of(bd, 0, n)], DEG[:, bd_of(bd, 0, n)], bank(7)[:, 0:n], ALU.add)),
                ]

            def adjacency(ohg, bs, g):
                return [
                    t(many([lambda e, c=c: e.matmul(bank(0, 2)[:, c * P:(c + 1) * P], ohg[:, 2, c, :], oh_d[:, c, :], start=True, stop=True) for c in range(GC)])),
                    a(lambda e: e.copy(adj_out[:, :, :], bank(0, 2)[:, 0:GC * P].rearrange("p (c e) -> p c e", c=GC))),
                    sy(lambda e: e.dma_start(ADJ[ds(bs, 1), :, g * GC * P:(g + 1) * GC * P].rearrange("o p w -> (o p) w"),
                                             adj_out[:, :, :].rearrange("p c e -> p (c e)"))),
                    sy(lambda e: e.dma_start(OHD[ds(bs, 1), g, :, :].rearrange("o p w -> (o p) w"), ohg.rearrange("p k c e -> p (k c e)").bitcast(F32))),
                ]

            def load_rec(bs, g):
                return sy(lambda e: e.dma_start(rec[:, :, :].rearrange("p c w -> p (c w)"),
                                                rec_rows[ds(bs, 1), :, g * GC * RW:(g + 1) * GC * RW].rearrange("o p w -> (o p) w")))

            def extra_chunks(body):
                barrier()
                n = extra_count()
                with e.If(n > 0):
                    with e.Fori(0, n) as j:
                        in_turn([sy(lambda e: e.dma_start(rec[:, 0, :], rec_extra[ds(j, 1), :, :].rearrange("o p w -> (o p) w")))])
                        in_turn_end()
                        bs = e.value_load(rec[0:1, 0, F_BS:F_BS + 1].bitcast(I32), min_val=0, max_val=NB - 1)
                        bd = e.value_load(rec[0:1, 0, F_BD:F_BD + 1].bitcast(I32), min_val=0, max_val=NB - 1)
                        in_turn([(who, lambda e: e.drain(), 1) for who in ENGINES])
                        in_turn(body(bs, bd))
                    in_turn_end()
                barrier()

            def gate_row(b, p, now=True, then=True):
                sl = lambda r: slice(r, r + 1) if isinstance(r, int) else ds(r, 1)
                of = lambda k: k % NG
                buf = lambda k: (p + k) % 2
                par = lambda k: p if k >= 0 else 1 - p
                cols = lambda k: slice(of(k) * GC, (of(k) + 1) * GC)
                wide_a, wide_b, wide_c = bank(0, 2), bank(2, 2), bank(4, 2)
                looked = wide_c[:, 0:GC * P].rearrange("p (c w) -> p c w", w=P)
                mlp = bank(6)[:, 0:GC * H].rearrange("p (c h) -> p c h", h=H)
                counts = bank(6)[:, GC * H:GC * H + NB]
                total = bank(7)[:, 0:3 * KW]
                w_of = lambda r: recs_g[:, r, :, F_W]
                halves = [(c, min(c + 512, GC * P)) for c in range(0, GC * P, 512)]

                def until(what, k, plain=True):
                    of_row(what, of(k) + 1, back=-(k // NG), plain=plain)

                def until_row(what, k, c=1, plain=True):
                    of_row(what, c, back=-(k // NG), plain=plain)

                def stages(plan):
                    for g in range(NG):
                        for lag, fn in plan:
                            if now if g - lag >= 0 else then:
                                fn(g - lag)

                if name == "sync":
                    if now:
                        of_row(recs_loaded, 16, back=1)
                        of_row(hidden, NG, back=2)
                        e.dma_start(recs_g[:, p, :, :].rearrange("p c w -> p (c w)"),
                                    rec_rows[sl(b), :, :].rearrange("o p w -> (o p) w")).then_inc(recs_loaded.sem, 16)
                    if then:
                        for g in range(NG):
                            of_row(dst_taken, g + 1, back=1)
                            e.dma_start(OHD[sl(b - 1), g, :, :].rearrange("o p w -> (o p) w"),
                                        hots[:, g].rearrange("p k c e -> p (k c e)").bitcast(F32)).then_inc(hots_stored[g].sem, 16)
                            of_row(adj_taken, g + 1, back=1)
                            e.dma_start(ADJ[sl(b - 1), :, g * GC * P:(g + 1) * GC * P].rearrange("o p w -> (o p) w"),
                                        adjs[:, g].rearrange("p c e -> p (c e)")).then_inc(hots_stored[g].sem, 16)

                if name == "tensor":
                    def flip_attr(k):
                        until_row(recs_loaded, k, 16)
                        until(activated, k - 1)
                        for c in range(GC):
                            last = e.transpose(wide_a[0:RBF, c * P:(c + 1) * P], recs_g[:, par(k), of(k) * GC + c, 0:RBF], ident[:, :])
                        last.then_inc(attr_flipped.sem, 1)

                    def flip_src(k):
                        until(hot_src, k)
                        until(adj_taken, k - 1)
                        for c in range(GC):
                            last = e.matmul(wide_b[:, c * P:(c + 1) * P], hots[:, of(k), 2, c, :], ident8[:, :], start=True, stop=True)
                        last.then_inc(src_flipped.sem, 1)

                    def flip_dst(k):
                        until(hot_dst, k)
                        until(nodes_taken, k - 2)
                        for c in range(GC):
                            last = e.matmul(wide_c[:, c * P:(c + 1) * P], hots_dst[:, of(k), c, :], ident8[:, :], start=True, stop=True)
                        last.then_inc(dst_flipped.sem, 1)

                    def hide(k):
                        until(attr_taken, k)
                        for c, d in halves:
                            last = e.matmul(wide_a[0:H, c:d], F1[:, :], attr_t[:, buf(k), c:d], start=True, stop=True)
                        last.then_inc(hidden.sem, 1)

                    def make_adj(k):
                        until(src_taken, k)
                        for c in range(GC):
                            last = e.matmul(wide_b[:, c * P:(c + 1) * P], hots[:, of(k), 2, c, :], hots_dst[:, of(k), c, :], start=True, stop=True)
                        last.then_inc(adj_made.sem, 1)

                    def finish_mlp(k):
                        until(activated, k)
                        until(mlp_taken, k - 1)
                        for c in range(GC):
                            e.matmul(counts[:, of(k) * GC + c:of(k) * GC + c + 1], hots_dst[:, of(k), c, :], ones8[:, :], start=True, stop=True)
                        for c in range(GC):
                            e.matmul(mlp[:, c, :], act_t[:, buf(k), c * P:(c + 1) * P], F2[:, :], start=True, stop=True)

                    def look_up(k):
                        until_row(table_staged, k)
                        if now or k + 1 < 0:
                            until(dst_taken, k + 1)
                        else:
                            until(nodes_taken, k - 1)
                        for c in range(GC):
                            for j in range(3):
                                e.matmul(looked[:, c, 0:GW], hots[:, of(k), 1, c, :], TD[:, j, of(k) * GC + c, 0:GW], start=j == 0, stop=j == 2)
                            for j in range(3):
                                last = e.matmul(looked[:, c, GW:GW + G], hots[:, of(k), 0, c, :], table_g[:, par(k), j, :], start=j == 0, stop=j == 2)
                        last.then_inc(looked_up.sem, 1)

                    def scatter_group(k):
                        if of(k) == 0:
                            until_row(row_added, k - NG)
                        until(third_part, k)
                        for c in range(GC):
                            last = e.matmul(total, hots[:, of(k), 2, c, :], vals3_g[:, of(k), c, :, :].rearrange("p k w -> p (k w)"),
                                            start=of(k) + c == 0, stop=of(k) * GC + c == NB - 1)
                        last.then_inc(scattered.sem, 1)

                    stages([(1, flip_src), (1, flip_attr), (2, finish_mlp), (1, flip_dst), (1, make_adj), (1, hide), (2, look_up), (4, scatter_group)])

                if name == "vector":
                    def link(c, ins):
                        ins.then_inc(cut_link.sem, 1)
                        of_row(cut_link, c, plain=False)

                    def make_hot(k):
                        until_row(recs_loaded, k, 16)
                        until(scattered, k - NG)
                        of_row(hots_stored[of(k)], 32, back=1 - k // NG)
                        e.tensor_tensor(hots[:, of(k), 2, :, :], iota_f[:, :].unsqueeze(1).broadcast_to([P, GC, P]),
                                        recs_g[:, par(k), cols(k), F_SRC:F_SRC + 1].broadcast_to([P, GC, P]), ALU.is_equal, saturate=False).then_inc(hot_src.sem, 1)
                        e.tensor_tensor(hots_dst[:, of(k), :, :], iota_f[:, :].unsqueeze(1).broadcast_to([P, GC, P]),
                                        recs_g[:, par(k), cols(k), F_DST:F_DST + 1].broadcast_to([P, GC, P]), ALU.is_equal, saturate=False).then_inc(hot_dst.sem, 1)

                    def take_attr(k):
                        until(attr_flipped, k)
                        until(hidden, k - 2)
                        e.tensor_copy(attr_t[:, buf(k), :], wide_a[0:RBF, 0:GC * P]).then_inc(attr_taken.sem, 1)

                    def angles(k):
                        if of(k) == 0:
                            until_row(recs_loaded, k, 16)
                            until_row(waved, k - NG)
                            link(1, e.scalar_tensor_tensor(angle[:, :], w_of(p), -1.0, w_of(p), ALU.mult, ALU.max))
                            e.tensor_scalar(angle[:, :], angle[:, :], CUT, None, ALU.min).then_inc(angled.sem, 1)

                    def cut(k):
                        if of(k) == 0:
                            until_row(waved, k)
                            link(2, e.tensor_scalar(wave[:, :], wave[:, :], 0.5, 0.5, ALU.mult, ALU.add))
                            link(3, e.scalar_tensor_tensor(cutoff[:, p, :], w_of(p), CUT, wave[:, :], ALU.is_lt, ALU.mult))

                    def make_values(k):
                        until(src_copied, k)
                        e.tensor_tensor(pairs[:, :, :], looked[:, :, KW:GW], src_g[:, :, :], ALU.mult).then_inc(pair_made.sem, 1)
                        until(pair_made, k, plain=False)
                        e.tensor_reduce(pair_sum[:, :], pairs[:, :, :], AX.X, ALU.add).then_inc(pair_added.sem, 1)
                        until(pair_added, k, plain=False)
                        if of(k) == NG - 1:
                            e.tensor_tensor(DEG[:, :], DEG[:, :], counts, ALU.add)
                        e.tensor_tensor(gates[:, 0, :, :], mlp, pair_sum[:, :].unsqueeze(2).broadcast_to([P, GC, H]), ALU.add).then_inc(mlp_taken.sem, 1)
                        until(mlp_taken, k, plain=False)
                        until(third_part, k - NG)
                        e.tensor_copy(vals_g[:, of(k), :, H:KW], looked[:, :, H:KW])
                        e.tensor_tensor(gates[:, 1, :, :], gates[:, 0, :, :], looked[:, :, 0:H], ALU.mult).then_inc(nodes_taken.sem, 1)
                        until(nodes_taken, k, plain=False)
                        e.tensor_tensor(vals_g[:, of(k), :, 0:H], gates[:, 1, :, :], cutoff[:, par(k), cols(k)].unsqueeze(2).broadcast_to([P, GC, H]), ALU.mult).then_inc(valued.sem, 1)

                    def add_row(k):
                        if of(k) == NG - 1:
                            until(scattered, k)
                            e.tensor_reduce(sum_g[:, :], total.rearrange("p (k w) -> p w k", k=3), AX.X, ALU.add).then_inc(row_added.sem, 1)
                            of_row(row_added, 1, back=1)
                            e.tensor_tensor(ACC[:, sl(b - 1), :], ACC[:, sl(b - 1), :], sum_g[:, :].unsqueeze(1), ALU.add)

                    stages([(5, add_row), (0, angles), (3, make_values), (1, take_attr), (0, make_hot), (1, cut)])

                if name == "scalar":
                    def wave_of(k):
                        if of(k) == 0:
                            until_row(angled, k)
                            e.activation(wave[:, :], angle[:, :], ACT.Sin, bias=half_pi[:, 0:1], scale=-2 * HALF_PI / CUT).then_inc(waved.sem, 1)

                    def take_hot(j, flipped, taken, at):
                        def take(k):
                            until(flipped, k)
                            of_row(hots_stored[of(k)], 32, back=1 - k // NG)
                            e.activation(hots[:, of(k), j, :, :], at[:, 0:GC * P].rearrange("p (c e) -> p c e", c=GC), ACT.Copy, saturate=False).then_inc(taken.sem, 1)
                        return take

                    def activate(k):
                        until(hidden, k)
                        until(looked_up, k - 2)
                        e.activation(act_t[0:H, buf(k), :], wide_a[0:H, 0:GC * P], ACT.Silu, bias=F1B[:, 0:1]).then_inc(activated.sem, 1)

                    def copy_src(k):
                        until(looked_up, k)
                        until(pair_made, k - 1)
                        e.copy(src_g[:, :, :], looked[:, :, GW:GW + G]).then_inc(src_copied.sem, 1)

                    def take_adj(k):
                        until(adj_made, k)
                        e.copy(adjs[:, of(k), :, :], wide_b[:, 0:GC * P].rearrange("p (c e) -> p c e", c=GC)).then_inc(adj_taken.sem, 1)

                    def first(k):
                        until(valued, k)
                        until(scattered, k - NG)
                        e.copy(vals3_g[:, of(k), :, 0, :], vals_g[:, of(k), :, :]).then_inc(first_part.sem, 1)

                    def second(k):
                        until(first_rest, k)
                        e.copy(vals3_g[:, of(k), :, 1, :], vals_g[:, of(k), :, :]).then_inc(second_part.sem, 1)

                    stages([(3, copy_src), (1, take_hot(0, src_flipped, src_taken, wide_b)),
                            (1, take_hot(1, dst_flipped, dst_taken, wide_c)), (3, first), (1, take_adj), (1, activate), (3, second), (0, wave_of)])

                if name == "gpsimd":
                    def stage_table(k):
                        if of(k) == 0:
                            of_row(looked_up, NG, back=2)
                            e.tensor_copy(table_g[:, p, :, :], TS[:, :, sl(b), 0:G].rearrange("p k o w -> p k (o w)")).then_inc(table_staged.sem, 1)

                    def rest(k):
                        until(first_part, k)
                        e.tensor_tensor(vals_g[:, of(k), :, :], vals_g[:, of(k), :, :], vals3_g[:, of(k), :, 0, :], ALU.subtract).then_inc(first_rest.sem, 1)

                    def third(k):
                        until(second_part, k)
                        e.tensor_tensor(vals3_g[:, of(k), :, 2, :], vals_g[:, of(k), :, :], vals3_g[:, of(k), :, 1, :], ALU.subtract).then_inc(third_part.sem, 1)

                    stages([(0, stage_table), (3, rest), (3, third)])

                if now:
                    e.reg_add(row, row, 1)

            def gate_pass():
                serial([v(lambda e: e.memset(act_t[:, :, :], 1.0))])
                barrier()
                gate_row(0, 0, then=False)
                with e.Fori(0, (NB - 1) // 2) as i:
                    gate_row(i * 2 + 1, 1)
                    gate_row(i * 2 + 2, 0)
                gate_row(NB, 1, now=False)
                if name == "sync":
                    for g in range(NG):
                        of_row(hots_stored[g], 32, back=1)
                e.reg_mov(row, 2)
                extra_chunks(lambda bs, bd: [stage_src(bs, G), stage_dst(bd, GW), *build_one_hots(1, oh[:, 0]), *degrees(1, bd), *gate_values(1, oh[:, 0], bs, bd)])

            def scores(n, ohg, bs, bd, to):
                return [
                    gather(n, d_spot, ohg[:, 1], dst_rows(bd), DW),
                    gather(n, q_spot, ohg[:, 0], src_rows, KW),
                    v(lambda e: e.scalar_tensor_tensor(xk[:, 0:n, 0:RBF], rec[:, 0:n, 0:RBF], 0.1, d_all(n)[:, :, 0:RBF], ALU.mult, ALU.add)),
                    v(lambda e: e.tensor_copy(xk[:, 0:n, RBF:KW], d_all(n)[:, :, RBF:KW])),
                    v(lambda e: e.tensor_tensor(xk[:, 0:n, :], xk[:, 0:n, :], q_all(n), ALU.mult)),
                    v(lambda e: e.tensor_reduce(to, xk[:, 0:n, :], AX.X, ALU.add)),
                ]

            def running_max(n, hots, score):
                return [a(lambda e: e.activation(os32[:, 0:n, :], hots[:, 0:n, :], ACT.Copy, bias=-BIG, scale=BIG))] + [
                    v(lambda e, c=c: e.scalar_tensor_tensor(runmax[:, :], os32[:, c, :], score(c), runmax[:, :], ALU.add, ALU.max)) for c in range(n)]

            def row_max(bs):
                return [
                    t(lambda e: e.transpose(bank(6)[:, 0:P], runmax[:, :], ident[:, :])),
                    v(lambda e: e.tensor_reduce(rowmax[:, 0:1], bank(6)[:, 0:P], AX.X, ALU.max)),
                    v(lambda e: e.tensor_tensor(SMAX[:, ds(bs, 1)], SMAX[:, ds(bs, 1)], rowmax[:, 0:1], ALU.max)),
                ]

            def weights(n, hot, bs, score, es):
                r = rowmax
                return [
                    v(lambda e: e.tensor_copy(r[:, 0:1], SMAX[:, ds(bs, 1)])),
                    v(lambda e: e.tensor_copy(smax3[:, 0:1], r[:, 0:1])),
                    v(lambda e: e.tensor_tensor(r[:, 1:2], r[:, 0:1], smax3[:, 0:1], ALU.subtract)),
                    v(lambda e: e.tensor_copy(smax3[:, 1:2], r[:, 1:2])),
                    v(lambda e: e.tensor_tensor(smax3[:, 2:3], r[:, 1:2], smax3[:, 1:2], ALU.subtract)),
                    t(many([lambda e, c=c: e.matmul(bank(6)[:, 3 * c:3 * c + 3], hot(c), smax3[:, :], start=True, stop=True) for c in range(n)])),
                    v(lambda e: e.tensor_reduce(es[:, 0, 0:n], bank(6)[:, 0:3 * n].rearrange("p (c k) -> p c k", k=3), AX.X, ALU.add)),
                    v(lambda e: e.tensor_tensor(es[:, 0, 0:n], score, es[:, 0, 0:n], ALU.subtract)),
                    v(lambda e: e.tensor_scalar(es[:, 0, 0:n], es[:, 0, 0:n], 20.0, None, ALU.min)),
                    a(lambda e: e.activation(es[:, 1, 0:n], es[:, 0, 0:n], ACT.Exp)),
                ]

            def extra_max(bs, bd):
                return [stage_src(bs), stage_dst(bd), *build_one_hots(1, oh[:, 0]), *scores(1, oh[:, 0], bs, bd, S1[:, 0:1]),
                        v(lambda e: e.memset(runmax[:, :], -BIG)),
                        *running_max(1, oh[:, 0, 2], lambda c: S1[:, 0:1]), *row_max(bs)]

            def extra_sum(bs, bd):
                return [stage_src(bs), stage_dst(bd), *build_one_hots(1, oh[:, 0]), *scores(1, oh[:, 0], bs, bd, S1[:, 0:1]),
                        *weights(1, lambda c: oh[:, 0, 0, 0, :], bs, S1[:, 0:1], ES[:, :, :]),
                        v(lambda e: e.tensor_scalar(V1[:, 0, 0:H], d_spot(0)[:, KW:DW], ES[:, 1, 0:1], None, ALU.mult)),
                        v(lambda e: e.tensor_copy(V1[:, 0, H:KW], ES[:, 1, 0:1])),
                        a(lambda e: e.copy(os32[:, 0, :], oh[:, 0, 2, 0, :])),
                        scatter(1, os32, V1, bank(7)[:, 0:KW]),
                        v(lambda e: e.tensor_tensor(ACC[:, ds(bs, 1), :], ACC[:, ds(bs, 1), :], bank(7)[:, 0:KW].unsqueeze(1), ALU.add))]

            def attention_row(b, p, now=True, then=True, late=True, ahead=True):
                sl = lambda r: slice(r, r + 1) if isinstance(r, int) else ds(r, 1)
                q = 1 - p
                buf = lambda g: (p + g) % 2
                D = lambda g, c: bank(2 * buf(g), 2)[:, c * P:c * P + DW]
                Dall = lambda g: bank(2 * buf(g), 2)[:, 0:GC * P].rearrange("p (c w) -> p c w", w=P)
                Q = lambda g, c: bank(4 + buf(g))[:, c * KW:(c + 1) * KW]
                Qall = lambda g: bank(4 + buf(g))[:, 0:GC * KW].rearrange("p (c w) -> p c w", w=KW)
                cols = lambda g: slice(g * GC, (g + 1) * GC)

                def run_plan(plan, of_now):
                    for f, *x in plan:
                        if now if f in of_now else late if x[1:] == [2] else then:
                            f(*x)

                if name == "sync" and now:
                    for g in range(NG):
                        of_row(summed, g + 1, back=2)
                        e.dma_start(cells[:, p, g].rearrange("p k c e -> p (k c e)").bitcast(F32),
                                    OHD[sl(b), g, :, :].rearrange("o p w -> (o p) w")).then_inc(s_cells[p][g], 16)
                        e.dma_start(recs[:, p, g].rearrange("p c w -> p (c w)"),
                                    rec_rows[sl(b), :, g * GC * RW:(g + 1) * GC * RW].rearrange("o p w -> (o p) w")).then_inc(s_cells[p][g], 16)

                if name == "tensor":
                    def gathers(g):
                        if g == 0:
                            of_row(staged, 1)
                        if g >= 2:
                            of_row(multiplied, g - 1)
                            of_row(carried, g - 1)
                        else:
                            of_row(multiplied, g - 1 + NG, back=1)
                            of_row(carried, g - 1 + NG, back=1)
                        e.wait_ge(s_cells[p][g], e.snap(loads[p], min_val=0, max_val=1 << 16) * 32 + 32)
                        e.sem_inc(absorb, 1)
                        for c in range(GC):
                            for k in range(3):
                                e.matmul(D(g, c), cells[:, p, g, 1, c, :], TD[:, k, g * GC + c, :], start=k == 0, stop=k == 2)
                        for c in range(GC):
                            for k in range(3):
                                last = e.matmul(Q(g, c), cells[:, p, g, 0, c, :], ts2[:, p, k, :], start=k == 0, stop=k == 2)
                        last.then_inc(gathered.sem, 1)

                    def flip():
                        of_row(combined, 1, back=1)
                        e.transpose(bank(6)[:, 0:P], slot_top[:, :], ident[:, :]).then_inc(flipped.sem, 1)

                    def gather_max():
                        of_row(parted, 4, back=1)
                        for c in range(NB):
                            last = e.matmul(bank(6)[:, P + 3 * c:P + 3 * c + 3], cells[:, q, c // GC, 0, c % GC, :], top3[:, :], start=True, stop=True)
                        last.then_inc(max_gathered.sem, 1)

                    def sums(g, back=1):
                        if g == 0:
                            of_row(added, 1, back=2)
                        of_row(weighted, g + 1, back=back)
                        for c in range(GC):
                            last = e.matmul(bank(7)[:, 0:3 * KW], cells[:, q if back == 1 else p, g, 2, c, :], values3[:, g * GC + c, :, :].rearrange("p k w -> p (k w)"),
                                            start=g + c == 0, stop=g * GC + c == NB - 1)
                        last.then_inc(summed.sem, 1)

                    run_plan([(gathers, 0), (gathers, 1), (flip,), (gather_max,), (sums, 3, 2), (sums, 4, 2), (gathers, 2), (sums, 5, 2), (sums, 6, 2),
                              (gathers, 3), (gathers, 4), (sums, 0), (gathers, 5), (sums, 1), (gathers, 6), (sums, 2)], (gathers,))

                if name == "vector":
                    links = [0]

                    def link(ins):
                        links[0] += 1
                        ins.then_inc(dve_link.sem, 1)
                        of_row(dve_link, links[0], plain=False)

                    def score_cells(g):
                        of_row(gathered, g + 1)
                        x1, x2 = xks[:, 0], xks[:, 1]
                        e.scalar_tensor_tensor(x1[:, :, 0:RBF], recs[:, p, g, :, 0:RBF], 0.1, Dall(g)[:, :, 0:RBF], ALU.mult, ALU.add)
                        link(e.tensor_copy(x1[:, :, RBF:KW], Dall(g)[:, :, RBF:KW]))
                        ins = e.tensor_tensor(x2, x1, Qall(g), ALU.mult)
                        ins.then_inc(multiplied.sem, 1)
                        of_row(multiplied, g + 1, plain=False)
                        link(e.tensor_reduce(score[:, p, cols(g)], x2, AX.X, ALU.add))

                    def max_cells(g):
                        of_row(masked, g + 1)
                        for c in range(GC):
                            s1 = score[:, p, g * GC + c:g * GC + c + 1]
                            if g == 0:
                                last = e.tensor_scalar(slot_max[:, c, :], mask[:, buf(g), c, :], s1, None, ALU.add)
                            else:
                                last = e.scalar_tensor_tensor(slot_max[:, c, :], mask[:, buf(g), c, :], s1, slot_max[:, c, :], ALU.add, ALU.max)
                        last.then_inc(maxed.sem, 1)

                    def take_max():
                        of_row(flipped, 1, back=1)
                        e.tensor_reduce(top[:, 0:1], bank(6)[:, 0:P], AX.X, ALU.max).then_inc(row_maxed.sem, 1)
                        of_row(row_maxed, 1, back=1, plain=False)
                        e.tensor_tensor(top[:, 1:2], top[:, 0:1], SMAX[:, sl(b - 1)], ALU.max).then_inc(row_maxed.sem, 1)

                    def fold_max():
                        e.sem_inc(absorb, 1)
                        of_row(max_gathered, 1, back=1)
                        e.tensor_reduce(edge_top[:, 0, :], bank(6)[:, P:P + 3 * NB].rearrange("p (c k) -> p c k", k=3), AX.X, ALU.add).then_inc(folded.sem, 1)

                    def add_row():
                        of_row(summed, NG, back=2)
                        e.tensor_reduce(row_sum[:, :], bank(7)[:, 0:3 * KW].rearrange("p (k w) -> p w k", k=3), AX.X, ALU.add).then_inc(added.sem, 1)
                        of_row(added, 1, back=2)
                        e.tensor_tensor(ACC[:, sl(b - 2), :], ACC[:, sl(b - 2), :], row_sum[:, :].unsqueeze(1), ALU.add).then_inc(added.sem, 1)
                        of_row(added, 2, back=2)

                    if then:
                        take_max()
                    for g in range(NG):
                        if now:
                            score_cells(g)
                        if g == 1 and then:
                            fold_max()
                        if now:
                            max_cells(g)
                        if g == 2 and late:
                            add_row()
                    if now:
                        of_row(maxed, NG, plain=False)
                        e.tensor_reduce(slot_top[:, :], slot_max[:, :, :].rearrange("p c n -> p n c"), AX.X, ALU.max).then_inc(combined.sem, 1)

                if name == "scalar":
                    def carry(g):
                        of_row(weighted, g + 1, back=2)
                        of_row(multiplied, g + 1)
                        e.copy(values[:, p, cols(g), 0:H], Dall(g)[:, :, KW:DW]).then_inc(carried.sem, 1)

                    def mask_cells(g):
                        of_row(gathered, g + 1)
                        if g >= 2:
                            of_row(maxed, g - 1)
                        else:
                            of_row(maxed, g - 1 + NG, back=1)
                        e.activation(mask[:, buf(g), :, :], cells[:, p, g, 2, :, :], ACT.Copy, bias=-BIG, scale=BIG).then_inc(masked.sem, 1)

                    def raise_weights():
                        of_row(bounded, 2, back=1)
                        e.activation(values[:, q, :, H:KW], edge_top[:, 2, :].unsqueeze(2), ACT.Exp).then_inc(raised.sem, 1)

                    def high(g):
                        of_row(scaled, g + 1, back=1)
                        of_row(summed, g + 1, back=2)
                        e.copy(values3[:, cols(g), 0, :], values[:, q, cols(g), :]).then_inc(high_part.sem, 1)

                    def middle(g, back=1):
                        of_row(less_high, g + 1, back=back)
                        e.copy(values3[:, cols(g), 1, :], values[:, q if back == 1 else p, cols(g), :]).then_inc(middle_part.sem, 1)

                    run_plan([(mask_cells, 0), (carry, 0), (mask_cells, 1), (carry, 1), (middle, 6, 2), (raise_weights,), (high, 0), (mask_cells, 2),
                              (high, 1), (middle, 0), (carry, 2), (mask_cells, 3), (high, 2), (middle, 1), (carry, 3),
                              (mask_cells, 4), (high, 3), (middle, 2), (carry, 4), (mask_cells, 5), (high, 4), (middle, 3), (carry, 5),
                              (mask_cells, 6), (high, 5), (middle, 4), (carry, 6), (high, 6), (middle, 5)], (carry, mask_cells))

                if name == "gpsimd":
                    def chained(what, c, ins):
                        ins.then_inc(what.sem, 1)
                        of_row(what, c, back=1, plain=True)

                    def stage_next():
                        of_row(gathered, NG, back=1)
                        e.tensor_copy(ts2[:, q, :, :], TS[:, :, sl(b + 1), :].rearrange("p k o w -> p k (o w)")).then_inc(staged.sem, 1)

                    if then:
                        of_row(row_maxed, 2, back=1)
                        e.tensor_copy(SMAX[:, sl(b - 1)], top[:, 1:2])
                        chained(parted, 1, e.tensor_copy(top3[:, 0:1], top[:, 1:2]))
                        chained(parted, 2, e.tensor_tensor(top[:, 2:3], top[:, 1:2], top3[:, 0:1], ALU.subtract))
                        chained(parted, 3, e.tensor_copy(top3[:, 1:2], top[:, 2:3]))
                        e.tensor_tensor(top3[:, 2:3], top[:, 2:3], top3[:, 1:2], ALU.subtract).then_inc(parted.sem, 1)

                    def scale(g):
                        if g == 0:
                            of_row(raised, 1, back=1)
                        of = values[:, q, cols(g), :]
                        e.tensor_tensor(of[:, :, 0:H], of[:, :, 0:H], of[:, :, H:KW].broadcast_to([P, GC, H]), ALU.mult).then_inc(scaled.sem, 1)

                    def take_high(g, back=1):
                        of_row(high_part, g + 1, back=back)
                        of = values[:, q if back == 1 else p, cols(g), :]
                        e.tensor_tensor(of, of, values3[:, cols(g), 0, :], ALU.subtract).then_inc(less_high.sem, 1)

                    def take_middle(g, back=1):
                        of_row(middle_part, g + 1, back=back)
                        of = values[:, q if back == 1 else p, cols(g), :]
                        e.tensor_tensor(values3[:, cols(g), 2, :], of, values3[:, cols(g), 1, :], ALU.subtract).then_inc(weighted.sem, 1)

                    def bound():
                        of_row(folded, 1, back=1)
                        chained(bounded, 1, e.tensor_tensor(edge_top[:, 1, :], score[:, q, :], edge_top[:, 0, :], ALU.subtract))
                        e.tensor_scalar(edge_top[:, 2, :], edge_top[:, 1, :], 20.0, None, ALU.min).then_inc(bounded.sem, 1)

                    plan = [(take_high, 6, 2), (take_middle, 5, 2), (take_middle, 6, 2), (bound,)]
                    for g in range(NG):
                        plan += [(scale, g), *([(take_high, g - 1)] if g >= 1 else []), *([(take_middle, g - 2)] if g >= 2 else [])]
                        if g == 2 and ahead:
                            plan.append((stage_next,))
                    run_plan(plan, (stage_next,))

                if now:
                    e.reg_add(row, row, 1)
                    e.reg_add(loads[p], loads[p], 1)

            def attention_pass():
                extra_chunks(extra_max)
                if name == "gpsimd":
                    e.tensor_copy(ts2[:, 0, :, :], TS[:, :, 0, :]).then_inc(staged.sem, 1)
                attention_row(0, 0, then=False, late=False)
                attention_row(1, 1, late=False)
                attention_row(2, 0)
                with e.Fori(0, (NB - 5) // 2) as i:
                    attention_row(i * 2 + 3, 1)
                    attention_row(i * 2 + 4, 0)
                attention_row(NB - 2, 1)
                attention_row(NB - 1, 0, ahead=False)
                attention_row(NB, 1, now=False, ahead=False)
                past_end[0] = 1
                attention_row(NB + 1, 0, now=False, then=False)
                past_end[0] = 0
                extra_chunks(extra_sum)

            def spread_setup():
                serial([
                    v(lambda e: e.tensor_tensor(X[:, :, :], X[:, :, :], HN[:, :, :], ALU.add)),
                    *normalise(HN[:, :, :], X[:, :, :], mm[:, :, :]),
                    v(lambda e: e.tensor_scalar(HN[:, :, :], HN[:, :, :], 0.0, None, ALU.max)),
                    a(lambda e: e.activation(STAT[:, 0, :], DEG[:, :], ACT.Sqrt)),
                    v(lambda e: e.reciprocal(dinv[:, :], STAT[:, 0, :])),
                    v(lambda e: e.tensor_tensor(g_f[:, :, :], HN[:, :, :], wide(dinv[:, :]), ALU.mult)),
                ])

            tiles = [(b, min(4, NB - b)) for b in range(0, NB, 4)]

            def spread_extra(bs, bd):
                hot = lambda to, f: v(lambda e: e.tensor_tensor(to[:, :], iota_f[:, :], rec_l[:, f:f + 1].broadcast_to([P, P]), ALU.is_equal))
                return [
                    hot(ohs_l, F_SRC), hot(ohd_l, F_DST),
                    t(lambda e: e.transpose(bank(4)[:, 0:P], ohs_l[:, :], ident[:, :])),
                    a(lambda e: e.copy(ohsT_l[:, :], bank(4)[:, 0:P])),
                    v(lambda e: e.tensor_copy(val_l[:, :], g_f[:, ds(bs, 1), :].rearrange("p o h -> p (o h)"))),
                    t(lambda e: e.matmul(bank(5)[:, 0:H], ohsT_l[:, :], val_l[:, :], start=True, stop=True)),
                    a(lambda e: e.copy(val_l[:, :], bank(5)[:, 0:H])),
                    t(lambda e: e.matmul(bank(6)[:, 0:H], ohd_l[:, :], val_l[:, :], start=True, stop=True)),
                    v(lambda e: e.tensor_tensor(mm[:, ds(bd, 1), :], mm[:, ds(bd, 1), :], bank(6)[:, 0:H].unsqueeze(1), ALU.add)),
                ]

            def spread_extra_chunks():
                barrier()
                n = extra_count()
                with e.If(n > 0):
                    with e.Fori(0, n) as j:
                        in_turn([sy(lambda e: e.dma_start(rec_l[:, :], rec_extra[ds(j, 1), :, :].rearrange("o p w -> (o p) w")))])
                        in_turn_end()
                        bs = e.value_load(rec_l[0:1, F_BS:F_BS + 1].bitcast(I32), min_val=0, max_val=NB - 1)
                        bd = e.value_load(rec_l[0:1, F_BD:F_BD + 1].bitcast(I32), min_val=0, max_val=NB - 1)
                        in_turn([(who, lambda e: e.drain(), 1) for who in ENGINES])
                        in_turn(spread_extra(bs, bd))
                    in_turn_end()
                barrier()

            def spread_step(k):
                serial(split([g3[:, :, j, :] for j in range(3)], g_f[:, :, :], g_r[:, :, :]))
                barrier()
                for i, (b0, nb) in enumerate(tiles):
                    n = k * len(tiles) + i
                    if name == "sync":
                        if n >= 2:
                            e.wait_ge(s_apes, n - 1)
                        e.dma_start(AJ[:, n % 2, :, 0:nb * P], adj_groups[:, :, b0 * P:(b0 + nb) * P]).then_inc(s_aload[n % 2], 16)
                    if name == "tensor":
                        e.wait_ge(s_aload[n % 2], 16 * (n // 2 + 1))
                        if n >= 2:
                            e.wait_ge(s_afold, n - 1)
                        for c in range(nb):
                            spot = bank(2 * (n % 2), 2)[:, c * 256:c * 256 + 3 * H]
                            for bs in range(NB):
                                last = e.matmul(spot, AJ[:, n % 2, bs, c * P:(c + 1) * P], g3[:, bs, :, :].rearrange("p k h -> p (k h)"),
                                                start=bs == 0, stop=bs == NB - 1)
                        last.then_inc(s_apes, 1)
                    if name == "vector":
                        e.wait_ge(s_apes, n + 1)
                        spots = bank(2 * (n % 2), 2).rearrange("p (c w) -> p c w", w=256)[:, 0:nb, 0:3 * H]
                        e.tensor_reduce(mm[:, b0:b0 + nb, :], spots.rearrange("p c (k h) -> p c h k", k=3), AX.X, ALU.add).then_inc(s_afold, 1)
                spread_extra_chunks()
                serial([
                    v(lambda e: e.tensor_tensor(mm[:, :, :], mm[:, :, :], g_f[:, :, :], ALU.add)),
                    v(lambda e: e.tensor_tensor(mm[:, :, :], mm[:, :, :], wide(dinv[:, :]), ALU.mult)),
                    v(lambda e: e.tensor_scalar(mm[:, :, :], mm[:, :, :], 1.0 - ALPHA, None, ALU.mult)),
                    v(lambda e: e.scalar_tensor_tensor(mm[:, :, :], HN[:, :, :], ALPHA, mm[:, :, :], ALU.mult, ALU.add)),
                    v(lambda e: e.tensor_tensor(g_f[:, :, :], mm[:, :, :], wide(dinv[:, :]), ALU.mult)),
                ])

            def store():
                serial([
                    v(lambda e: e.tensor_tensor(X[:, :, :], X[:, :, :], mm[:, :, :], ALU.add)),
                    sy(lambda e: e.dma_start(out[0:(NB - 1) * P, :].rearrange("(b p) h -> p b h", p=P), X[:, 0:NB - 1, :])),
                    sy(lambda e: e.dma_start(out[(NB - 1) * P:N, :], X[0:TAIL, NB - 1, :])),
                ])

            load_all()
            count_cells()
            fill_extra()
            place_edges()
            if debug == "rec":
                serial([sy(lambda e: e.dma_start(out, REC[0:out.shape[0], :]))])
                e.wait_ge(order, count[0])
                return
            embed()
            first_tables()
            gate_pass()
            after_gate()
            if debug != "gate":
                for l in range(L):
                    layer_tables(l)
                    attention_pass()
                    layer_update(l)
                    if debug == "layer0":
                        break
            if debug in ("gate", "layer0"):
                serial([v(lambda e: e.tensor_copy(X[:, :, :], HN[:, :, :])), v(lambda e: e.memset(W1[:, :, :], 0.0))])
                serial([
                    sy(lambda e: e.dma_start(out[0:(NB - 1) * P, :].rearrange("(b p) h -> p b h", p=P), X[:, 0:NB - 1, :])),
                    sy(lambda e: e.dma_start(out[(NB - 1) * P:N, :], X[0:TAIL, NB - 1, :])),
                ])
                e.wait_ge(order, count[0])
                return
            spread_setup()
            for k in range(KSTEP):
                spread_step(k)
            store()
            e.wait_ge(order, count[0])

        block.sync(lambda e: program("sync", e))
        block.tensor(lambda e: program("tensor", e))
        block.vector(lambda e: program("vector", e))
        block.scalar(lambda e: program("scalar", e))
        block.gpsimd(lambda e: program("gpsimd", e))


def kernel(x, src, dst, edge_attr_40, edge_weight, node_type_119, node_vec, L0_gnn_Wq, L0_gnn_gq, L0_gnn_bq, L0_gnn_Wk,
           L0_gnn_gk, L0_gnn_bk, L0_gnn_Wm, L0_gnn_Wu, L0_gnn_go, L0_gnn_bo, L0_gnn_F1W, L0_gnn_F1b, L0_gnn_F2W,
           L0_gnn_F2b, L0_gnn_gn, L0_gnn_bn, L0_gnn_emb, L0_gnn_adapt):
    import numpy as np
    from concourse import bacc
    from concourse.bass_utils import run_bass_kernel_spmd

    arrays = {
        "x": x, "src": src, "dst": dst, "edge_attr_40": edge_attr_40, "edge_weight": edge_weight,
        "node_type_119": node_type_119, "node_vec": node_vec, "Wq": L0_gnn_Wq, "gq": L0_gnn_gq, "bq": L0_gnn_bq,
        "Wk": L0_gnn_Wk, "gk": L0_gnn_gk, "bk": L0_gnn_bk, "Wm": L0_gnn_Wm, "Wu": L0_gnn_Wu, "go": L0_gnn_go,
        "bo": L0_gnn_bo, "F1W": L0_gnn_F1W, "F1b": L0_gnn_F1b, "F2W": L0_gnn_F2W, "F2b": L0_gnn_F2b, "gn": L0_gnn_gn,
        "bn": L0_gnn_bn, "emb": L0_gnn_emb, "adapt": L0_gnn_adapt,
    }
    arrays = {name: np.ascontiguousarray(a) for name, a in arrays.items()}
    nc = bacc.Bacc("TRN2", target_bir_lowering=False, num_devices=1)
    args = {name: nc.dram_tensor(f"in_{name}", a.shape, mybir.dt.from_np(a.dtype), kind="ExternalInput").ap()
            for name, a in arrays.items()}
    out = nc.dram_tensor("out", (N, H), F32, kind="ExternalOutput").ap()
    build(nc, out=out, **args)
    result = run_bass_kernel_spmd(nc, [{f"in_{name}": a for name, a in arrays.items()}], core_ids=[0])
    return result.results[0]["out"]
```
